# Optimizing a Trainium2 kernel written in Bass

```python
import numpy as np
import jax
import jax.numpy as jnp

def _softmax(x, axis=-1):
    return jax.nn.softmax(x, axis=axis)

def _gelu(x):
    return jax.nn.gelu(x, approximate=True)

def _silu(x):
    return jax.nn.silu(x)

def _sigmoid(x):
    return jax.nn.sigmoid(x)

def _layernorm(x, axis=-1, eps=1e-05):
    m = jnp.mean(x, axis=axis, keepdims=True)
    v = jnp.var(x, axis=axis, keepdims=True)
    return (x - m) / jnp.sqrt(v + eps)

def _scatter_add(tgt, idx, src, axis=0):
    return tgt.at[idx].add(src)

def _segment_sum(src, seg, n):
    return jax.ops.segment_sum(src, seg, n)
kernel_name = 'mk_xattn_ffn_d2_seqx_r8_30220a'

def setup_inputs(seed: int=0):
    np.random.seed(seed)
    _w = jnp.asarray

    def _rec_inputs():
        import jax
        import jax.numpy as jnp
        _rk = jax.random.key(seed)
        x = -0.000125 + 0.9999 * jax.random.normal(jax.random.fold_in(_rk, 1), (16, 128, 256), jnp.float32)
        _lenS = 128 - jax.random.randint(jax.random.fold_in(_rk, 7), (16,), 0, max(1, 128 // 4) + 1, jnp.int32)
        _lenS2 = 128 - jax.random.randint(jax.random.fold_in(_rk, 8), (16,), 0, max(1, 128 // 4) + 1, jnp.int32)
        _ctx_2048P = jax.random.normal(jax.random.fold_in(_rk, 11), (16, 16, 256), jnp.float32)
        _ctx_2048c = jax.random.dirichlet(jax.random.fold_in(_rk, 511), 0.3 * jnp.ones((16,), jnp.float32), (16, 128))
        _ctx_2048t = jnp.einsum('bsk,bkd->bsd', _ctx_2048c, _ctx_2048P)
        _ctx_2048t = _ctx_2048t * jax.lax.rsqrt(jnp.mean(jnp.square(_ctx_2048t)) + 1e-12) * 0.953939
        ctx_2048 = -0.000514642 + 1.00011 * (_ctx_2048t + 0.3 * jax.random.normal(jax.random.fold_in(_rk, 611), (16, 128, 256), jnp.float32))
        itok_BxS_0_1023 = jax.random.randint(jax.random.fold_in(_rk, 13), (16, 128), 0, 128, jnp.int32)
        _validS = jnp.arange(128)[None, :] < _lenS[:, None]
        _validS2 = jnp.arange(128)[None, :] < _lenS2[:, None]
        _causal = jnp.tril(jnp.ones((128, 128), dtype=bool))
        mask_BxS2_bk0 = jnp.logical_not(jnp.broadcast_to(_validS2[:, :], (16, 128)))
        return (x, ctx_2048, itok_BxS_0_1023, mask_BxS2_bk0)
    x, ctx_2048, itok_BxS_0_1023, mask_BxS2_bk0 = _rec_inputs()

    def _L0_xattn_setup():
        import jax, jax.numpy as jnp
        import numpy as np
        key = jax.random.key(seed)
        k1, k2, k3 = jax.random.split(key, 3)
        B, S, D, M = (8, 256, 256, 128)
        hidden_states = jax.random.normal(k1, (B, S, D), dtype=jnp.float32)
        memory_tokens = jax.random.normal(k2, (B, M, D), dtype=jnp.float32)
        memory_mask = jax.random.randint(k3, (B, M), 0, 2).astype(jnp.bool_)
        return {'hidden_states': hidden_states, 'memory_tokens': memory_tokens, 'memory_mask': memory_mask}
    _L0_xattn_all = _L0_xattn_setup()
    _L0_xattn_in = {k: v for k, v in _L0_xattn_all.items() if k in ()}
    del _L0_xattn_all

    def _L0_ffn_setup():
        import jax, jax.numpy as jnp
        import numpy as np
        B, S, D = (2, 256, 256)
        H, HD = (16, 128)
        E, K, I = (16, 6, 176)
        SI = 352
        EPS = 1e-06

        def rmsnorm(x, w):
            v = jnp.mean(jnp.square(x), axis=-1, keepdims=True)
            return x * jax.lax.rsqrt(v + EPS) * w
        key = jax.random.key(seed)
        ks = jax.random.split(key, 14)
        s = 0.02
        return {'hidden_states': jax.random.normal(ks[0], (B, S, D), jnp.float32), 'ln1_w': jnp.ones((D,), jnp.float32), 'ln2_w': jnp.ones((D,), jnp.float32), 'wq': jax.random.normal(ks[1], (D, H * HD), jnp.float32) * s, 'wk': jax.random.normal(ks[2], (D, H * HD), jnp.float32) * s, 'wv': jax.random.normal(ks[3], (D, H * HD), jnp.float32) * s, 'wo': jax.random.normal(ks[4], (H * HD, D), jnp.float32) * s, 'gate_w': jax.random.normal(ks[5], (E, D), jnp.float32) * s, 'eg_w': jax.random.normal(ks[6], (E, I, D), jnp.float32) * s, 'eu_w': jax.random.normal(ks[7], (E, I, D), jnp.float32) * s, 'ed_w': jax.random.normal(ks[8], (E, D, I), jnp.float32) * s, 'sg_w': jax.random.normal(ks[9], (SI, D), jnp.float32) * s, 'su_w': jax.random.normal(ks[10], (SI, D), jnp.float32) * s, 'sd_w': jax.random.normal(ks[11], (D, SI), jnp.float32) * s}
    _L0_ffn_all = _L0_ffn_setup()
    _L0_ffn_in = {k: v for k, v in _L0_ffn_all.items() if k in ('ln1_w', 'ln2_w', 'wq', 'wk', 'wv', 'wo', 'gate_w', 'eg_w', 'eu_w', 'ed_w', 'sg_w', 'su_w', 'sd_w')}
    del _L0_ffn_all

    def _L1_xattn_setup():
        import jax, jax.numpy as jnp
        import numpy as np
        B, Lq, Lk = (2, 512, 128)
        Q_DIM, KV_DIM = (256, 256)
        H, HD = (16, 128)
        KVC, QC, R = (64, 96, 64)
        LOOKBACK = 8
        NEG = -1e+30

        def _rope(x, L):
            half = x.shape[-1] // 2
            inv_freq = 1.0 / 10000.0 ** (jnp.arange(half, dtype=jnp.float32) / half)
            ang = jnp.arange(L, dtype=jnp.float32)[:, None] * inv_freq
            cos, sin = (jnp.cos(ang), jnp.sin(ang))
            x1, x2 = (x[..., :half], x[..., half:])
            return jnp.concatenate([x1 * cos - x2 * sin, x1 * sin + x2 * cos], axis=-1)
        key = jax.random.key(seed)
        ks = jax.random.split(key, 11)

        def w(k, shape, fan_in):
            return jax.random.normal(k, shape, jnp.float32) / np.sqrt(fan_in).astype(np.float32)
        return {'q': jax.random.normal(ks[0], (B, Lq, Q_DIM), jnp.float32), 'kv': jax.random.normal(ks[1], (B, Lk, KV_DIM), jnp.float32), 'seg_id': jnp.sort(jax.random.randint(ks[2], (B, Lq), 0, Lk), axis=-1), 'W_kvc': w(ks[3], (KV_DIM, KVC), KV_DIM), 'W_dq': w(ks[4], (Q_DIM, QC), Q_DIM), 'W_uq': w(ks[5], (QC, H * HD), QC), 'W_qr': w(ks[6], (QC, H * R), QC), 'W_uk': w(ks[7], (KVC, H * HD), KVC), 'W_kr': w(ks[8], (KVC, R), KVC), 'W_uv': w(ks[9], (KVC, H * HD), KVC), 'W_o': w(ks[10], (H * HD, Q_DIM), H * HD)}
    _L1_xattn_all = _L1_xattn_setup()
    _L1_xattn_in = {k: v for k, v in _L1_xattn_all.items() if k in ('W_kvc', 'W_dq', 'W_uq', 'W_qr', 'W_uk', 'W_kr', 'W_uv', 'W_o')}
    del _L1_xattn_all

    def _L1_ffn_setup():
        import jax, jax.numpy as jnp
        import numpy as np
        _FP8_MAX = 448.0
        _BLOCK = 32
        _EPS = 1e-30

        def _mx_dequant(t):
            rows, feat = t.shape
            blocks = t.reshape(rows, feat // _BLOCK, _BLOCK)
            max_abs = jnp.max(jnp.abs(blocks), axis=-1)
            scales = jnp.maximum(max_abs / _FP8_MAX, _EPS)
            q = (blocks / scales[..., None]).astype(jnp.float8_e4m3fn).astype(jnp.float32)
            return (q * scales[..., None]).reshape(rows, feat)

        def _mx_linear(x2d, w):
            return _mx_dequant(x2d) @ _mx_dequant(w).T
        key = jax.random.key(seed)
        k1, k2, k3, k4 = jax.random.split(key, 4)
        B, S, H, I = (2, 128, 256, 1024)
        return {'x': jax.random.normal(k1, (B, S, H), dtype=jnp.float32), 'gate_w': jax.random.normal(k2, (I, H), dtype=jnp.float32) * 0.02, 'up_w': jax.random.normal(k3, (I, H), dtype=jnp.float32) * 0.02, 'down_w': jax.random.normal(k4, (H, I), dtype=jnp.float32) * 0.02}
    _L1_ffn_all = _L1_ffn_setup()
    _L1_ffn_in = {k: v for k, v in _L1_ffn_all.items() if k in ('gate_w', 'up_w', 'down_w')}
    del _L1_ffn_all
    return {'x': x, 'ctx_2048': ctx_2048, 'itok_BxS_0_1023': itok_BxS_0_1023, 'mask_BxS2_bk0': mask_BxS2_bk0, 'L0_ffn_ln1_w': _L0_ffn_in['ln1_w'], 'L0_ffn_ln2_w': _L0_ffn_in['ln2_w'], 'L0_ffn_wq': _L0_ffn_in['wq'], 'L0_ffn_wk': _L0_ffn_in['wk'], 'L0_ffn_wv': _L0_ffn_in['wv'], 'L0_ffn_wo': _L0_ffn_in['wo'], 'L0_ffn_gate_w': _L0_ffn_in['gate_w'], 'L0_ffn_eg_w': _L0_ffn_in['eg_w'], 'L0_ffn_eu_w': _L0_ffn_in['eu_w'], 'L0_ffn_ed_w': _L0_ffn_in['ed_w'], 'L0_ffn_sg_w': _L0_ffn_in['sg_w'], 'L0_ffn_su_w': _L0_ffn_in['su_w'], 'L0_ffn_sd_w': _L0_ffn_in['sd_w'], 'L1_xattn_W_kvc': _L1_xattn_in['W_kvc'], 'L1_xattn_W_dq': _L1_xattn_in['W_dq'], 'L1_xattn_W_uq': _L1_xattn_in['W_uq'], 'L1_xattn_W_qr': _L1_xattn_in['W_qr'], 'L1_xattn_W_uk': _L1_xattn_in['W_uk'], 'L1_xattn_W_kr': _L1_xattn_in['W_kr'], 'L1_xattn_W_uv': _L1_xattn_in['W_uv'], 'L1_xattn_W_o': _L1_xattn_in['W_o'], 'L1_ffn_gate_w': _L1_ffn_in['gate_w'], 'L1_ffn_up_w': _L1_ffn_in['up_w'], 'L1_ffn_down_w': _L1_ffn_in['down_w']}

def reference(x, ctx_2048, itok_BxS_0_1023, mask_BxS2_bk0, L0_ffn_ln1_w, L0_ffn_ln2_w, L0_ffn_wq, L0_ffn_wk, L0_ffn_wv, L0_ffn_wo, L0_ffn_gate_w, L0_ffn_eg_w, L0_ffn_eu_w, L0_ffn_ed_w, L0_ffn_sg_w, L0_ffn_su_w, L0_ffn_sd_w, L1_xattn_W_kvc, L1_xattn_W_dq, L1_xattn_W_uq, L1_xattn_W_qr, L1_xattn_W_uk, L1_xattn_W_kr, L1_xattn_W_uv, L1_xattn_W_o, L1_ffn_gate_w, L1_ffn_up_w, L1_ffn_down_w):
    import jax
    import jax.numpy as jnp

    def _L0_xattn_ref(hidden_states, memory_tokens, memory_mask):
        import jax, jax.numpy as jnp
        import numpy as np
        B, S, D = hidden_states.shape
        scale = 1.0 / jnp.sqrt(jnp.asarray(D, hidden_states.dtype))
        scores = jnp.einsum('bsd,bmd->bsm', hidden_states, memory_tokens) * scale
        neg_inf = jnp.asarray(-1e+30, scores.dtype)
        scores = jnp.where(memory_mask[:, None, :], scores, neg_inf)
        attn = jax.nn.softmax(scores, axis=-1)
        readout = jnp.einsum('bsm,bmd->bsd', attn, memory_tokens)
        valid_b = jnp.any(memory_mask, axis=-1)
        out = jnp.where(valid_b[:, None, None], readout, jnp.zeros_like(readout))
        return out

    def _L0_ffn_ref(hidden_states, ln1_w, ln2_w, wq, wk, wv, wo, gate_w, eg_w, eu_w, ed_w, sg_w, su_w, sd_w):
        import jax, jax.numpy as jnp
        import numpy as np
        B, S, D = (2, 256, 256)
        H, HD = (16, 128)
        E, K, I = (16, 6, 176)
        SI = 352
        EPS = 1e-06

        def rmsnorm(x, w):
            v = jnp.mean(jnp.square(x), axis=-1, keepdims=True)
            return x * jax.lax.rsqrt(v + EPS) * w
        b, s, d = hidden_states.shape
        x = hidden_states
        h = rmsnorm(x, ln1_w)
        q = (h @ wq).reshape(b, s, H, HD)
        k = (h @ wk).reshape(b, s, H, HD)
        v = (h @ wv).reshape(b, s, H, HD)
        scores = jnp.einsum('bqhd,bkhd->bhqk', q, k) / np.sqrt(HD).astype(np.float32)
        causal = jnp.tril(jnp.ones((s, s), bool))
        scores = jnp.where(causal, scores, jnp.float32(-1000000000.0))
        attn = jax.nn.softmax(scores, axis=-1)
        ao = jnp.einsum('bhqk,bkhd->bqhd', attn, v).reshape(b, s, H * HD) @ wo
        x = x + ao
        h = rmsnorm(x, ln2_w)
        t = h.reshape(-1, d)
        T = t.shape[0]
        logits = t @ gate_w.T
        probs = jax.nn.softmax(logits, axis=-1)
        topv, topi = jax.lax.top_k(probs, K)
        topv = topv / jnp.sum(topv, axis=-1, keepdims=True)
        cw = jnp.zeros((T, E), t.dtype).at[jnp.arange(T)[:, None], topi].add(topv)
        g = jnp.einsum('td,eid->eti', t, eg_w)
        u = jnp.einsum('td,eid->eti', t, eu_w)
        hh = jax.nn.silu(g) * u
        routed = jnp.einsum('eti,edi,te->td', hh, ed_w, cw)
        shared = jax.nn.silu(t @ sg_w.T) * (t @ su_w.T) @ sd_w.T
        out = x + (routed + shared).reshape(b, s, d)
        return out

    def _L1_xattn_ref(q, kv, seg_id, W_kvc, W_dq, W_uq, W_qr, W_uk, W_kr, W_uv, W_o):
        import jax, jax.numpy as jnp
        import numpy as np
        B, Lq, Lk = (2, 512, 128)
        Q_DIM, KV_DIM = (256, 256)
        H, HD = (16, 128)
        KVC, QC, R = (64, 96, 64)
        LOOKBACK = 8
        NEG = -1e+30

        def _rope(x, L):
            half = x.shape[-1] // 2
            inv_freq = 1.0 / 10000.0 ** (jnp.arange(half, dtype=jnp.float32) / half)
            ang = jnp.arange(L, dtype=jnp.float32)[:, None] * inv_freq
            cos, sin = (jnp.cos(ang), jnp.sin(ang))
            x1, x2 = (x[..., :half], x[..., half:])
            return jnp.concatenate([x1 * cos - x2 * sin, x1 * sin + x2 * cos], axis=-1)
        b, lq, _ = q.shape
        lk = kv.shape[1]
        kv_c = kv @ W_kvc
        q_c = q @ W_dq
        q_nope = (q_c @ W_uq).reshape(b, lq, H, HD).transpose(0, 2, 1, 3)
        q_rope = (q_c @ W_qr).reshape(b, lq, H, R).transpose(0, 2, 1, 3)
        k_nope = (kv_c @ W_uk).reshape(b, lk, H, HD)
        v = (kv_c @ W_uv).reshape(b, lk, H, HD)
        k_rope = kv_c @ W_kr
        q_rope = _rope(q_rope, lq)
        k_rope = _rope(k_rope, lk)
        scale = 1.0 / np.sqrt(HD + R).astype(np.float32)
        scores = (jnp.einsum('bhqd,bkhd->bhqk', q_nope, k_nope) + jnp.einsum('bhqr,bkr->bhqk', q_rope, k_rope)) * scale
        k_ids = jnp.arange(lk)[None, None, :]
        qs = seg_id[:, :, None]
        good = (k_ids <= qs) & (k_ids >= qs - LOOKBACK)
        scores = jnp.where(good[:, None, :, :], scores, NEG)
        attn = jax.nn.softmax(scores, axis=-1)
        out = jnp.einsum('bhqk,bkhd->bqhd', attn, v).reshape(b, lq, H * HD)
        return out @ W_o

    def _L1_ffn_ref(x, gate_w, up_w, down_w):
        import jax, jax.numpy as jnp
        import numpy as np
        _FP8_MAX = 448.0
        _BLOCK = 32
        _EPS = 1e-30

        def _mx_dequant(t):
            rows, feat = t.shape
            blocks = t.reshape(rows, feat // _BLOCK, _BLOCK)
            max_abs = jnp.max(jnp.abs(blocks), axis=-1)
            scales = jnp.maximum(max_abs / _FP8_MAX, _EPS)
            q = (blocks / scales[..., None]).astype(jnp.float8_e4m3fn).astype(jnp.float32)
            return (q * scales[..., None]).reshape(rows, feat)

        def _mx_linear(x2d, w):
            return _mx_dequant(x2d) @ _mx_dequant(w).T
        B, S, H = x.shape
        x2d = x.reshape(B * S, H)
        gate = _mx_linear(x2d, gate_w)
        up = _mx_linear(x2d, up_w)
        h = jax.nn.silu(gate) * up
        out = _mx_linear(h, down_w)
        return out.reshape(B, S, H)
    x = x + _L0_xattn_ref(_layernorm(x, axis=-1), ctx_2048, mask_BxS2_bk0)
    x = x + _L0_ffn_ref(_layernorm(x, axis=-1), L0_ffn_ln1_w, L0_ffn_ln2_w, L0_ffn_wq, L0_ffn_wk, L0_ffn_wv, L0_ffn_wo, L0_ffn_gate_w, L0_ffn_eg_w, L0_ffn_eu_w, L0_ffn_ed_w, L0_ffn_sg_w, L0_ffn_su_w, L0_ffn_sd_w)
    x = x + _L1_xattn_ref(_layernorm(x, axis=-1), ctx_2048, itok_BxS_0_1023, L1_xattn_W_kvc, L1_xattn_W_dq, L1_xattn_W_uq, L1_xattn_W_qr, L1_xattn_W_uk, L1_xattn_W_kr, L1_xattn_W_uv, L1_xattn_W_o)
    x = x + _L1_ffn_ref(_layernorm(x, axis=-1), L1_ffn_gate_w, L1_ffn_up_w, L1_ffn_down_w)
    return x

_drawn_inputs = setup_inputs


def setup_inputs(seed=0):
    import zlib

    import numpy as np

    out = dict(_drawn_inputs(seed))
    spreads = {'L0_ffn_ln1_w': (1.0, 0.6), 'L0_ffn_ln2_w': (1.0, 0.6)}
    factors = {'L0_ffn_wq': 8.0,
     'L0_ffn_wk': 8.0,
     'L0_ffn_gate_w': 8.0,
     'L0_ffn_eg_w': 8.0,
     'L0_ffn_eu_w': 8.0,
     'L0_ffn_ed_w': 8.0,
     'L0_ffn_sg_w': 5.849,
     'L0_ffn_su_w': 5.817,
     'L0_ffn_sd_w': 5.808,
     'L1_ffn_gate_w': 3.664,
     'L1_ffn_up_w': 3.412,
     'L1_ffn_down_w': 3.429,
     'L1_xattn_W_dq': 4.001,
     'L1_xattn_W_uq': 4.692,
     'L1_xattn_W_qr': 6.437,
     'L1_xattn_W_uk': 4.698,
     'L1_xattn_W_kr': 6.362}
    for name, (base, spread) in spreads.items():
        noise = np.random.default_rng([zlib.crc32(name.encode()), seed]).standard_normal(out[name].shape)
        drawn = base * np.exp(spread * noise) if base else spread * noise
        out[name] = jnp.asarray(drawn.astype(out[name].dtype))
    for name, factor in factors.items():
        out[name] = (out[name] * factor).astype(out[name].dtype)
    return out
```

```python
from contextlib import ExitStack

import concourse.bass as bass
from concourse import mybir

F32 = mybir.dt.float32
F32R = mybir.dt.float32r
I32 = mybir.dt.int32
U8 = mybir.dt.uint8
ALU = mybir.AluOpType
ACT = mybir.ActivationFunctionType
X_AXIS = mybir.AxisListType.X
ds = bass.ds

P = 128
BATCHES = 16
D = 256
KT = D // P
GROUP = 4
GROUPS = BATCHES // GROUP
GW = GROUP * P

HEADS = 16
HD = 128
PAIRS = HEADS // 2
LN_EPS = 1e-5
RMS_EPS = 1e-6


class Env:
    pass


def constants_and_state(nc, ctx, ins):
    e = Env()

    def sb(name, shape, dt=F32):
        return ctx.enter_context(nc.sbuf_tensor(name, shape, dt))

    e.X = sb("X", [P, BATCHES, D])
    e.ident = sb("ident", [P, P])
    e.ident_r = sb("ident_r", [P, P], F32R)
    e.one = sb("one", [P, 1])
    return e


def copy_pool(pool, e, out, src):
    return pool.tensor_tensor(out, src, e.one[:, 0:1].broadcast_to(list(src.shape)), ALU.mult)


def rsqrt_steps(ve, link, var, y, t, u):
    link(ve.tensor_scalar(y.bitcast(I32), var.bitcast(I32), -0.5, 1597463007.0, ALU.mult, ALU.add))
    for _ in range(3):
        link(ve.scalar_tensor_tensor(out=t, in0=y, scalar=-0.5, in1=y, op0=ALU.mult, op1=ALU.mult))
        link(ve.tensor_tensor(u, t, var, ALU.mult))
        link(ve.scalar_tensor_tensor(out=y, in0=u, scalar=1.5, in1=y, op0=ALU.add, op1=ALU.mult))


def over_groups(a):
    return a.unsqueeze(2).broadcast_to([P, GROUP, P])


def phase_a(nc, e, ins, w):
    with ExitStack() as ctx:
        def sb(name, shape, dt=F32):
            return ctx.enter_context(nc.sbuf_tensor(name, shape, dt))

        def sem(name):
            return ctx.enter_context(nc.semaphore(name))

        ctxn = sb("ctxn", [P, BATCHES, D])
        ctxT = sb("ctxT", [P, KT, BATCHES * P])
        mask8 = sb("mask8", [P, BATCHES * P], U8)
        mbias = sb("mbias", [P, BATCHES * P], F32R)
        valid = sb("valid", [P, BATCHES])
        st = sb("st", [P, GROUP, 6])
        mv = sb("mv", [P, GROUP, 2])
        va = sb("va", [P, GROUP])
        rs = sb("rs", [P, GROUP])
        rr = sb("rr", [P, GROUP])
        nt = sb("nt", [P, GROUP])
        nu = sb("nu", [P, GROUP])
        xn = sb("xn", [P, GROUP, D])
        lnT = sb("lnT", [P, KT, GW])
        nmax = sb("nmax", [P, GROUP])
        sums = sb("sums", [P, GROUP])
        rec = sb("rec", [P, GROUP])
        prob = sb("prob", [P, GROUP, P])
        probT = sb("probT", [P, GW])
        bank = [ctx.enter_context(nc.psum_tensor(f"a_bank{i}", [P, GW], F32)) for i in range(8)]
        xT_ps, sc_ps, pT_ps, av_ps, hT_ps = bank[0:2], bank[2], bank[3], bank[4:6], bank[6:8]

        names = ("a_x a_ctx a_ctxT a_mask a_lnw a_w a_zero a_ident a_identr a_bias a_dve a_ln a_xT a_lnT a_scores a_max "
                 "a_prob a_rec a_pT a_pTsb a_av a_h a_hT a_hhi a_hlo a_valid a_split").split()
        s = {n: sem(n) for n in names}

        with nc.Block() as block:
            @block.sync
            def _(sp):
                sp.dma_start(e.X[:], ins["x"].rearrange("b p d -> p b d")).then_inc(s["a_x"], 16)
                sp.dma_start(ctxT[:], ins["ctxT"].rearrange("(k p) t -> p k t", p=P)).then_inc(s["a_ctxT"], 16)
                sp.dma_start(ctxn[:], ins["ctx"].rearrange("b p d -> p b d")).then_inc(s["a_ctx"], 16)
                sp.dma_start(w.raw[:], ins["w_attn"][:, 0:2]).then_inc(s["a_w"], 16)

            @block.gpsimd
            def _(pool):
                pool.memset(e.one[:], 1.0)
                pool.memset(e.ident[:], 0.0).then_inc(s["a_zero"], 1)
                pool.wait_ge(s["a_zero"], 1)
                pool.affine_select(out=e.ident[:], in_=e.ident[:], compare_op=ALU.not_equal, fill=1.0, base=0,
                                   pattern=[[-1, P]], channel_multiplier=1).then_inc(s["a_ident"], 1)
                pool.memset(w.causal32[:], 0.0).then_inc(s["a_zero"], 1)
                pool.wait_ge(s["a_zero"], 2)
                pool.affine_select(out=w.causal32[:], in_=w.causal32[:], compare_op=ALU.is_ge, fill=-1.0e9, base=0,
                                   pattern=[[-1, P]], channel_multiplier=1).then_inc(s["a_zero"], 1)
                pool.wait_ge(s["a_zero"], 3)
                pool.tensor_scalar(w.causal[:], w.causal32[:], 1.0, None, ALU.mult).then_inc(s["a_identr"], 1)
                pool.wait_ge(s["a_ident"], 1)
                pool.tensor_scalar(e.ident_r[:], e.ident[:], 1.0, None, ALU.mult).then_inc(s["a_identr"], 1)
                pool.wait_ge(s["a_mask"], 32)
                pool.tensor_scalar(mbias[:], mask8[:], 1.0e30, -1.0e30, ALU.mult, ALU.add).then_inc(s["a_bias"], 1)
                for n in range(2):
                    pool.wait_ge(s["a_w"], 16)
                    pool.tensor_scalar(w.hi[:, n], w.raw[:, n], 1.0, None, ALU.mult).then_inc(s["a_split"], 1)
                for n in range(2):
                    pool.wait_ge(s["a_split"], n + 1)
                    pool.tensor_tensor(w.lo[:, n], w.raw[:, n], w.hi[:, n].bitcast(F32), ALU.subtract)

            @block.scalar
            def _(act):
                act.dma_start(mask8[:], ins["mask"].rearrange("b m -> (b m)").partition_broadcast(P)).then_inc(s["a_mask"], 16)
                act.dma_start(w.ln1[:], ins["ln1"]).then_inc(s["a_mask"], 16)
                for g in range(GROUPS):
                    act.wait_ge(s["a_xT"], g + 1)
                    for k in range(KT):
                        act.activation(lnT[:, k], xT_ps[k][:], ACT.Copy, scale=float(D) ** -0.5).then_inc(s["a_lnT"], 1)
                    act.wait_ge(s["a_max"], g + 1)
                    for b in range(GROUP):
                        act.activation(prob[:, b], sc_ps[:, b * P:(b + 1) * P], ACT.Exp, bias=nmax[:, b:b + 1],
                                       accum_out=sums[:, b:b + 1]).then_inc(s["a_prob"], 1)
                    act.wait_ge(s["a_pT"], g + 1)
                    act.activation(probT[:], pT_ps[:], ACT.Copy).then_inc(s["a_pTsb"], 1)
                    act.wait_ge(s["a_hT"], g + 1)
                    act.wait_ge(s["a_mask"], 32)
                    for k in range(KT):
                        act.activation(w.hT_hi[:, k, ds(g * GW, GW)], hT_ps[k][:], ACT.Copy,
                                       scale=w.ln1[:, k:k + 1]).then_inc(s["a_hhi"], 1)

            @block.tensor
            def _(pe):
                pe.wait_ge(s["a_ident"], 1)
                pe.wait_ge(s["a_identr"], 2)
                pe.wait_ge(s["a_ctxT"], 16)
                pe.wait_ge(s["a_ctx"], 16)
                pe.wait_ge(s["a_bias"], 1)
                for g in range(GROUPS):
                    pe.wait_ge(s["a_ln"], g + 1)
                    for k in range(KT):
                        for b in range(GROUP):
                            mm = pe.transpose(xT_ps[k][:, b * P:(b + 1) * P], xn[:, b, k * P:(k + 1) * P], e.ident[:])
                    mm.then_inc(s["a_xT"], 1)
                    pe.wait_ge(s["a_lnT"], KT * g + KT)
                    for b in range(GROUP):
                        for k in range(KT):
                            mm = pe.matmul(sc_ps[:, b * P:(b + 1) * P], lnT[:, k, b * P:(b + 1) * P],
                                           ctxT[:, k, ds(g * GW + b * P, P)], start=(b == 0 and k == 0),
                                           stop=False, skip_group_check=True)
                    mm = pe.matmul(sc_ps[:], e.ident_r[:], mbias[:, ds(g * GW, GW)], start=False, stop=True,
                                   skip_group_check=True)
                    mm.then_inc(s["a_scores"], 1)
                    pe.wait_ge(s["a_prob"], GROUP * g + GROUP)
                    for b in range(GROUP):
                        mm = pe.transpose(pT_ps[:, b * P:(b + 1) * P], prob[:, b], e.ident[:])
                    mm.then_inc(s["a_pT"], 1)
                    pe.wait_ge(s["a_pTsb"], g + 1)
                    for b in range(GROUP):
                        mm = pe.matmul(av_ps[b // 2][:, (b % 2) * D:(b % 2 + 1) * D], probT[:, b * P:(b + 1) * P],
                                       ctxn[:, ds(g * GROUP + b, 1), :], start=(b % 2 == 0), stop=True,
                                       skip_group_check=True)
                    mm.then_inc(s["a_av"], 1)
                    pe.wait_ge(s["a_h"], g + 1)
                    for k in range(KT):
                        for b in range(GROUP):
                            mm = pe.transpose(hT_ps[k][:, b * P:(b + 1) * P], xn[:, b, k * P:(k + 1) * P], e.ident[:])
                    mm.then_inc(s["a_hT"], 1)

            LINKS = 58

            @block.vector
            def _(ve):
                ve.wait_ge(s["a_mask"], 32)
                ve.tensor_reduce(valid[:], mask8[:].rearrange("p (b m) -> p b m", b=BATCHES), X_AXIS, ALU.max).then_inc(s["a_valid"], 1)
                ve.wait_ge(s["a_x"], 16)
                for g in range(GROUPS):
                    done = [0]

                    def link(instruction):
                        done[0] += 1
                        instruction.then_inc(s["a_dve"], 1)
                        ve.wait_ge(s["a_dve"], g * LINKS + done[0])

                    def layer_norm(out):
                        for b in range(GROUP):
                            link(ve.bn_stats(st[:, b], e.X[:, ds(g * GROUP + b, 1), :]))
                        for b in range(GROUP):
                            link(ve.bn_aggr(mv[:, b], st[:, b]))
                        link(ve.tensor_scalar(va[:], mv[:, :, 1], LN_EPS, None, ALU.add))
                        rsqrt_steps(ve, link, va[:], rs[:], nt[:], nu[:])
                        for b in range(GROUP):
                            last = ve.tensor_scalar(out(b), e.X[:, ds(g * GROUP + b, 1), :], mv[:, b, 0:1],
                                                    rs[:, b:b + 1], ALU.subtract, ALU.mult)
                        return last

                    layer_norm(lambda b: xn[:, b]).then_inc(s["a_ln"], 1)
                    ve.wait_ge(s["a_scores"], g + 1)
                    ve.tensor_reduce(nmax[:], sc_ps[:].rearrange("p (b m) -> p b m", b=GROUP), X_AXIS, ALU.max,
                                     negate=True).then_inc(s["a_max"], 1)
                    ve.wait_ge(s["a_prob"], GROUP * g + GROUP)
                    ve.wait_ge(s["a_valid"], 1)
                    link(ve.reciprocal(rec[:], sums[:]))
                    link(ve.tensor_tensor(rec[:], rec[:], valid[:, ds(g * GROUP, GROUP)], ALU.mult))
                    ve.wait_ge(s["a_av"], g + 1)
                    for b in range(GROUP):
                        xb = e.X[:, ds(g * GROUP + b, 1), :]
                        link(ve.scalar_tensor_tensor(out=xb, in0=av_ps[b // 2][:, (b % 2) * D:(b % 2 + 1) * D],
                                                     scalar=rec[:, b:b + 1], in1=xb, op0=ALU.mult, op1=ALU.add))
                    link(layer_norm(lambda b: e.Y[:, ds(g * GROUP + b, 1), :]))
                    link(ve.tensor_tensor(nt[:], rs[:], rs[:], ALU.mult))
                    link(ve.tensor_tensor(nt[:], nt[:], mv[:, :, 1], ALU.mult))
                    link(ve.tensor_scalar(va[:], nt[:], RMS_EPS, None, ALU.add))
                    rsqrt_steps(ve, link, va[:], rr[:], nt[:], nu[:])
                    for b in range(GROUP):
                        last = ve.tensor_scalar(xn[:, b], e.Y[:, ds(g * GROUP + b, 1), :], rr[:, b:b + 1], None, ALU.mult)
                    last.then_inc(s["a_h"], 1)
                    for k in range(KT):
                        ve.wait_ge(s["a_hhi"], KT * g + k + 1)
                        hi = w.hT_hi[:, k, ds(g * GW, GW)]
                        ve.scalar_tensor_tensor(out=w.hT_lo[:, k, ds(g * GW, GW)], in0=hT_ps[k][:],
                                                scalar=w.ln1[:, k:k + 1], in1=hi.bitcast(F32), op0=ALU.mult,
                                                op1=ALU.subtract).then_inc(s["a_hlo"], 1)
                    ve.wait_ge(s["a_hlo"], KT * g + KT)
                    assert done[0] == LINKS, done


def phase_attention(nc, e, ins, w):
    STEPS = 2 * GROUPS
    PASSES = PAIRS // 2
    UNITS = 6
    RING = 4
    with ExitStack() as ctx:
        def sb(name, shape, dt=F32):
            return ctx.enter_context(nc.sbuf_tensor(name, shape, dt))

        def sem(name):
            return ctx.enter_context(nc.semaphore(name))

        qk_hi = sb("qk_hi", [P, 4, GW], F32R)
        qk_lo = sb("qk_lo", [P, 4, GW], F32R)
        v_hi = sb("v_hi", [P, 2, GROUP, 2 * HD], F32R)
        v_lo = sb("v_lo", [P, 2, GROUP, 2 * HD], F32R)
        prob = sb("b_prob", [P, 2, GROUP, P])
        probT_hi = sb("probT_hi", [P, 2, GW], F32R)
        probT_lo = sb("probT_lo", [P, 2, GW], F32R)
        ao_hi = sb("ao_hi", [P, 2, GW], F32R)
        ao_lo = sb("ao_lo", [P, 2, GW], F32R)
        nmax = sb("b_nmax", [P, 2, 2, GROUP])
        sums = sb("b_sums", [P, 2, 2, GROUP])
        rec = sb("b_rec", [P, 2, 2, GROUP])
        ring = [ctx.enter_context(nc.psum_tensor(f"b_ring{i}", [P, GW], F32)) for i in range(RING)]
        sc_ps = [ctx.enter_context(nc.psum_tensor(f"b_sc{i}", [P, GW], F32)) for i in range(2)]
        wo_ps = [ctx.enter_context(nc.psum_tensor(f"b_wo{i}", [P, GW], F32)) for i in range(2)]

        proj_done, proj_hi, proj_lo = sem("proj_done"), sem("proj_hi"), sem("proj_lo")
        scores_done, max_done, exp_done = sem("scores_done"), sem("max_done"), sem("exp_done")
        rec_done, norm_done = sem("rec_done"), sem("norm_done")
        probT_done, probT_hid, probT_lod = sem("probT_done"), sem("probT_hid"), sem("probT_lod")
        pv_done, ao_hid, ao_lod = sem("pv_done"), sem("ao_hid"), sem("ao_lod")
        wo_done, y_added = sem("wo_done"), sem("y_added")
        raw_in = [sem("raw_in0"), sem("raw_in1")]
        qkv_hi_split, qkv_split = sem("qkv_hi_split"), sem("qkv_split")
        wo_hi_split, wo_split = sem("wo_hi_split"), sem("wo_split")

        def pe_project(pe, it, j, first=False):
            S = it * STEPS + j
            g, n = (j // 2) % GROUPS, j % 2
            if j in (1, STEPS) and not (isinstance(it, int) and _pair(it, j) < 2):
                pe.wait_ge(qkv_split, _pair(it, j) - 1)
            for u in range(UNITS):
                out = ring[u % RING]
                if not first:
                    if u in (0, 1):
                        pe.wait_ge(proj_lo, UNITS * (S - 1) + 4 + u + 1)
                    elif u in (2, 3):
                        if isinstance(it, int) and S < 2:
                            pe.wait_ge(proj_lo, UNITS * (S - 1) + u + 1)
                        else:
                            pe.wait_ge(ao_lod, 2 * (S - 2) + (u - 2) + 1)
                if u in (4, 5):
                    pe.wait_ge(proj_lo, UNITS * S + (u - 4) + 1)
                if u < 4:
                    c = (u // 2) * HD
                    for k in range(KT):
                        h_hi, h_lo = w.hT_hi[:, k, g * GW:(g + 1) * GW], w.hT_lo[:, k, g * GW:(g + 1) * GW]
                        mm = parts(pe, out[:], w.hi[:, n, u % 2, k, c:c + HD], w.lo[:, n, u % 2, k, c:c + HD],
                                   h_hi, h_lo, start=(k == 0), stop=(k == KT - 1))
                else:
                    for t in range(2):
                        tok = g * GW + ((u - 4) * 2 + t) * P
                        for k in range(KT):
                            mm = parts(pe, out[:, t * 2 * HD:(t + 1) * 2 * HD], w.hT_hi[:, k, tok:tok + P],
                                       w.hT_lo[:, k, tok:tok + P], w.hi[:, n, 2, k, :], w.lo[:, n, 2, k, :],
                                       start=(t == 0 and k == 0), stop=(k == KT - 1))
                mm.then_inc(proj_done, 1)

        def _pair(it, j):
            return 2 * it + 2 * (j // STEPS) + j % 2

        def pe_scores(pe, it, j):
            S = it * STEPS + j
            for h in range(2):
                if not (isinstance(it, int) and S < 1):
                    pe.wait_ge(probT_lod, 2 * (S - 1) + h + 1)
                pe.wait_ge(proj_lo, UNITS * S + 2 * h + 2)
                for b in range(GROUP):
                    c = slice(b * P, (b + 1) * P)
                    mm = parts(pe, sc_ps[h][:, c], qk_hi[:, 2 * h, c], qk_lo[:, 2 * h, c],
                               qk_hi[:, 2 * h + 1, c], qk_lo[:, 2 * h + 1, c], start=(b == 0))
                mm = pe.matmul(sc_ps[h][:].rearrange("p (b m) -> p b m", b=GROUP), e.ident_r[:],
                               w.causal[:].unsqueeze(1).broadcast_to([P, GROUP, P]), start=False, stop=True,
                               skip_group_check=True)
                mm.then_inc(scores_done, 1)

        def pe_transpose(pe, it, j):
            S = it * STEPS + j
            for h in range(2):
                pe.wait_ge(norm_done, 2 * S + h + 1)
                for b in range(GROUP):
                    mm = pe.transpose(sc_ps[h][:, b * P:(b + 1) * P], prob[:, h, b], e.ident[:])
                mm.then_inc(probT_done, 1)

        def pe_wo(pe, it, j):
            S = it * STEPS + j
            n = j % 2
            pe.wait_ge(ao_lod, 2 * S + 2)
            if j < 2 and not (isinstance(it, int) and it == 0):
                pe.wait_ge(wo_split, 2 * it + n - 1)
            if n == 0 and not (isinstance(it, int) and S < 2):
                pe.wait_ge(y_added, S)
            for b in range(GROUP):
                for h in range(2):
                    mm = parts(pe, wo_ps[b // 2][:, (b % 2) * D:(b % 2 + 1) * D], ao_hi[:, h, b * P:(b + 1) * P],
                               ao_lo[:, h, b * P:(b + 1) * P], w.hi[:, n, 3, h, :], w.lo[:, n, 3, h, :],
                               start=(n == 0 and h == 0 and b % 2 == 0), stop=(n == 1 and h == 1))
            mm.then_inc(wo_done, 1)

        def pe_pv(pe, it, j, last=False):
            S = it * STEPS + j
            for h in range(2):
                pe.wait_ge(probT_lod, 2 * S + h + 1)
                out = ring[2 + h]
                if not last:
                    pe.wait_ge(proj_lo, UNITS * (S + 1) + 2 + h + 1)
                elif last:
                    pe.wait_ge(ao_lod, 2 * (S - 1) + h + 1)
                for b in range(GROUP):
                    c = slice(b * P, (b + 1) * P)
                    mm = parts(pe, out[:, c], v_hi[:, j % 2, b, h * HD:(h + 1) * HD], v_lo[:, j % 2, b, h * HD:(h + 1) * HD],
                               probT_hi[:, h, c], probT_lo[:, h, c], start=(b == 0), stop=True)
                mm.then_inc(pv_done, 1)

        def pe_pass(pe, it, first=False, last=False):
            for j in range(STEPS):
                end = last and j == STEPS - 1
                pe_scores(pe, it, j)
                if not end:
                    pe_project(pe, it, j + 1)
                pe_transpose(pe, it, j)
                if j > 0:
                    pe_wo(pe, it, j - 1)
                elif not first:
                    pe_wo(pe, it - 1, STEPS - 1)
                pe_pv(pe, it, j, last=end)

        SCALE = float(HD) ** -0.5

        def unit_places(j, u):
            if u < 4:
                return (qk_hi[:, u], qk_lo[:, u], SCALE if u % 2 == 0 else 1.0)
            t = 2 * (u - 4)
            return (v_hi[:, j % 2, t:t + 2].rearrange("p t c -> p (t c)"),
                    v_lo[:, j % 2, t:t + 2].rearrange("p t c -> p (t c)"), 1.0)

        def act_project(act, it, j):
            S = it * STEPS + j
            for u in range(UNITS):
                hi, _, scale = unit_places(j, u)
                act.wait_ge(proj_done, UNITS * S + u + 1)
                act.activation(hi, ring[u % RING][:], ACT.Copy, scale=scale).then_inc(proj_hi, 1)

        def act_pass(act, it, last=False):
            for j in range(STEPS):
                S = it * STEPS + j
                for h in range(2):
                    act.wait_ge(max_done, 2 * S + h + 1)
                    for b in range(GROUP):
                        act.activation(prob[:, h, b], sc_ps[h][:, b * P:(b + 1) * P], ACT.Exp,
                                       bias=nmax[:, j % 2, h, b:b + 1],
                                       accum_out=sums[:, j % 2, h, b:b + 1]).then_inc(exp_done, 1)
                if not (last and j == STEPS - 1):
                    act_project(act, it, j + 1)
                for h in range(2):
                    act.wait_ge(probT_done, 2 * S + h + 1)
                    act.activation(probT_hi[:, h], sc_ps[h][:], ACT.Copy).then_inc(probT_hid, 1)
                for h in range(2):
                    act.wait_ge(pv_done, 2 * S + h + 1)
                    act.activation(ao_hi[:, h], ring[2 + h][:], ACT.Copy).then_inc(ao_hid, 1)

        def dve_project(ve, it, j, units):
            S = it * STEPS + j
            for u in units:
                hi, lo, scale = unit_places(j, u)
                ve.wait_ge(proj_hi, UNITS * S + u + 1)
                ve.scalar_tensor_tensor(out=lo, in0=ring[u % RING][:], scalar=scale, in1=hi.bitcast(F32),
                                        op0=ALU.mult, op1=ALU.subtract).then_inc(proj_lo, 1)

        def dve_ao(ve, it, j):
            S = it * STEPS + j
            for h in range(2):
                ve.wait_ge(ao_hid, 2 * S + h + 1)
                ve.tensor_tensor(ao_lo[:, h], ring[2 + h][:], ao_hi[:, h].bitcast(F32), ALU.subtract).then_inc(ao_lod, 1)

        def dve_add(ve, it, j):
            S = it * STEPS + j
            g = j // 2
            ve.wait_ge(wo_done, S + 1)
            for n in range(2):
                y = e.Y[:, g * GROUP + 2 * n:g * GROUP + 2 * n + 2].rearrange("p t d -> p (t d)")
                if not (isinstance(it, int) and it == 0):
                    ve.wait_ge(y_added, S - 1 + n)
                ve.tensor_tensor(y, wo_ps[n][:], y, ALU.add).then_inc(y_added, 1)

        def dve_pass(ve, it, first=False, last=False):
            for j in range(STEPS):
                S = it * STEPS + j
                before = (it, j - 1) if j > 0 else (it - 1, STEPS - 1)
                for h in range(2):
                    ve.wait_ge(scores_done, 2 * S + h + 1)
                    ve.tensor_reduce(nmax[:, j % 2, h], sc_ps[h][:].rearrange("p (b m) -> p b m", b=GROUP), X_AXIS,
                                     ALU.max, negate=True).then_inc(max_done, 1)
                if not (first and j == 0):
                    dve_ao(ve, *before)
                more = not (last and j == STEPS - 1)
                if more:
                    dve_project(ve, it, j + 1, [0])
                for h in range(2):
                    ve.wait_ge(exp_done, GROUP * (2 * S + h) + GROUP)
                    ve.reciprocal(rec[:, j % 2, h], sums[:, j % 2, h]).then_inc(rec_done, 1)
                if more:
                    dve_project(ve, it, j + 1, range(1, UNITS))
                for h in range(2):
                    ve.wait_ge(probT_hid, 2 * S + h + 1)
                    ve.tensor_tensor(probT_lo[:, h], sc_ps[h][:], probT_hi[:, h].bitcast(F32),
                                     ALU.subtract).then_inc(probT_lod, 1)
                if j % 2 == 0 and not (first and j == 0):
                    dve_add(ve, *before)

        def pool_split(pool, n, which, hi_sem, lo_sem, hi_at, lo_at):
            hi = w.hi[:, n, which].rearrange("p a k c -> p (a k c)")
            lo = w.lo[:, n, which].rearrange("p a k c -> p (a k c)")
            raw = w.raw[:, n, which].rearrange("p a k c -> p (a k c)")
            copy_pool(pool, e, hi, raw).then_inc(hi_sem, 1)
            pool.wait_ge(hi_sem, hi_at)
            pool.tensor_tensor(lo, raw, hi.bitcast(F32), ALU.subtract).then_inc(lo_sem, 1)

        def pool_pass(pool, it, first=False, last=False):
            for j in range(STEPS):
                S = it * STEPS + j
                for h in range(2):
                    pool.wait_ge(rec_done, 2 * S + h + 1)
                    pool.tensor_tensor(prob[:, h], prob[:, h], over_groups(rec[:, j % 2, h]), ALU.mult).then_inc(norm_done, 1)
                if not last and j >= STEPS - 3 and j < STEPS - 1:
                    n = j - (STEPS - 3)
                    pool.wait_ge(proj_done, UNITS * (S + 2))
                    pool.wait_ge(raw_in[n], 16 * (it + 1))
                    pool_split(pool, n, slice(0, 3), qkv_hi_split, qkv_split, 2 * it + n + 1, 2 * it + n + 1)
                if not last and j == STEPS - 1:
                    pool.wait_ge(wo_done, S)
                    pool_split(pool, 0, slice(3, 4), wo_hi_split, wo_split, 2 * it + 1, 2 * it + 1)
                if not first and j == 0:
                    pool.wait_ge(wo_done, S)
                    pool_split(pool, 1, slice(3, 4), wo_hi_split, wo_split, 2 * it, 2 * it)

        def sp_pass(sp, it):
            for n in range(2):
                if not (isinstance(it, int) and it == 0):
                    sp.wait_ge(wo_split, 2 * (it - 1) + n + 1)
                sp.dma_start(w.raw[:, n:n + 1], ins["w_attn"][:, ds(2 * it + 2 + n, 1)]).then_inc(raw_in[n], 16)

        with nc.Block() as block:
            @block.sync
            def _(sp):
                sp_pass(sp, 0)
                with sp.Fori(1, PASSES - 1) as it:
                    sp_pass(sp, it)

            @block.gpsimd
            def _(pool):
                pool_pass(pool, 0, first=True)
                with pool.Fori(1, PASSES - 1) as it:
                    pool_pass(pool, it)
                pool_pass(pool, PASSES - 1, last=True)

            @block.scalar
            def _(act):
                act_project(act, 0, 0)
                act_pass(act, 0)
                with act.Fori(1, PASSES - 1) as it:
                    act_pass(act, it)
                act_pass(act, PASSES - 1, last=True)

            @block.vector
            def _(ve):
                dve_project(ve, 0, 0, range(UNITS))
                dve_pass(ve, 0, first=True)
                with ve.Fori(1, PASSES - 1) as it:
                    dve_pass(ve, it)
                dve_pass(ve, PASSES - 1, last=True)
                dve_ao(ve, PASSES - 1, STEPS - 1)
                dve_add(ve, PASSES - 1, STEPS - 1)

            @block.tensor
            def _(pe):
                pe_project(pe, 0, 0, first=True)
                pe_pass(pe, 0, first=True)
                with pe.Fori(1, PASSES - 1) as it:
                    pe_pass(pe, it)
                pe_pass(pe, PASSES - 1, last=True)
                pe_wo(pe, PASSES - 1, STEPS - 1)



class Norm:

    def __init__(self, nc, ctx, tag, banks):
        def sb(name, shape, dt=F32):
            return ctx.enter_context(nc.sbuf_tensor(f"{tag}_{name}", shape, dt))

        self.st, self.mv = sb("st", [P, BATCHES, 6]), sb("mv", [P, BATCHES, 2])
        self.va, self.rs = sb("va", [P, BATCHES]), sb("rs", [P, BATCHES])
        self.nt, self.nu = sb("nt", [P, BATCHES]), sb("nu", [P, BATCHES])
        self.xn = sb("xn", [P, 2, GROUP, D])
        self.banks = banks
        self.chain, self.ready, self.turned, self.hi_done, self.lo_done = (
            ctx.enter_context(nc.semaphore(f"{tag}_{n}")) for n in ("chain", "ready", "turned", "hi", "lo"))


def norm_vector(ve, n, src, eps, centred, hT_hi, hT_lo, weight=None):
    links = [0]

    def link(instruction):
        links[0] += 1
        instruction.then_inc(n.chain, 1)
        ve.wait_ge(n.chain, links[0])

    for t in range(BATCHES):
        last = ve.bn_stats(n.st[:, t], src[:, t])
    link(last)
    for t in range(BATCHES):
        last = ve.bn_aggr(n.mv[:, t], n.st[:, t])
    link(last)
    if centred:
        link(ve.tensor_scalar(n.va[:], n.mv[:, :, 1], eps, None, ALU.add))
    else:
        link(ve.tensor_tensor(n.nt[:], n.mv[:, :, 0], n.mv[:, :, 0], ALU.mult))
        link(ve.scalar_tensor_tensor(out=n.va[:], in0=n.nt[:], scalar=eps, in1=n.mv[:, :, 1], op0=ALU.add, op1=ALU.add))
    rsqrt_steps(ve, link, n.va[:], n.rs[:], n.nt[:], n.nu[:])

    def low_parts(g):
        for k in range(KT):
            ve.wait_ge(n.hi_done, KT * g + k + 1)
            out = hT_lo[:, k, g * GW:(g + 1) * GW]
            hi = hT_hi[:, k, g * GW:(g + 1) * GW].bitcast(F32)
            ps = n.banks[2 * (g % 2) + k][:]
            if weight is None:
                ve.tensor_tensor(out, ps, hi, ALU.subtract).then_inc(n.lo_done, 1)
            else:
                ve.scalar_tensor_tensor(out=out, in0=ps, scalar=weight[:, k:k + 1], in1=hi, op0=ALU.mult,
                                        op1=ALU.subtract).then_inc(n.lo_done, 1)

    for g in range(GROUPS):
        if g >= 2:
            ve.wait_ge(n.turned, g - 1)
        for b in range(GROUP):
            t = g * GROUP + b
            if centred:
                last = ve.tensor_scalar(n.xn[:, g % 2, b], src[:, t], n.mv[:, t, 0:1], n.rs[:, t:t + 1],
                                        ALU.subtract, ALU.mult)
            else:
                last = ve.tensor_scalar(n.xn[:, g % 2, b], src[:, t], n.rs[:, t:t + 1], None, ALU.mult)
        last.then_inc(n.ready, 1)
        if g >= 1:
            low_parts(g - 1)
    low_parts(GROUPS - 1)


def norm_tensor(pe, n, ident):
    for g in range(GROUPS):
        pe.wait_ge(n.ready, g + 1)
        if g >= 2:
            pe.wait_ge(n.lo_done, KT * (g - 1))
        for k in range(KT):
            for b in range(GROUP):
                mm = pe.transpose(n.banks[2 * (g % 2) + k][:, b * P:(b + 1) * P], n.xn[:, g % 2, b, k * P:(k + 1) * P], ident)
        mm.then_inc(n.turned, 1)


def norm_scalar(act, n, hT_hi, weight=None):
    for g in range(GROUPS):
        act.wait_ge(n.turned, g + 1)
        for k in range(KT):
            scale = 1.0 if weight is None else weight[:, k:k + 1]
            act.activation(hT_hi[:, k, g * GW:(g + 1) * GW], n.banks[2 * (g % 2) + k][:], ACT.Copy,
                           scale=scale).then_inc(n.hi_done, 1)


def parts(pe, out, l_hi, l_lo, r_hi, r_lo, start, stop=False):
    pe.matmul(out, l_hi, r_hi, start=start, stop=False, skip_group_check=True)
    pe.matmul(out, l_hi, r_lo, start=False, stop=False, skip_group_check=True)
    return pe.matmul(out, l_lo, r_hi, start=False, stop=stop, skip_group_check=True)


EXPERTS = 16
TOP = 6
EI = 176
SI = 352
TILES = -(-(EXPERTS * EI + SI) // P)
SLOTS = 5
UP, DOWN, SEL, WCOLS = KT * P, 2 * KT * P, 2 * KT * P + D, 2 * KT * P + D + P


def phase_moe(nc, e, ins):
    STEPS = GROUPS * SLOTS
    PASSES = TILES // SLOTS
    LAG = 2
    RING = 4
    assert TILES % SLOTS == 0 and STEPS % RING == 0
    with ExitStack() as ctx:
        def sb(name, shape, dt=F32):
            return ctx.enter_context(nc.sbuf_tensor(name, shape, dt))

        def sem(name):
            return ctx.enter_context(nc.semaphore(name))

        hT_hi = sb("m_hT_hi", [P, KT, BATCHES * P], F32R)
        hT_lo = sb("m_hT_lo", [P, KT, BATCHES * P], F32R)
        raw = sb("m_raw", [P, SLOTS, WCOLS])
        hi = sb("m_hi", [P, SLOTS, WCOLS], F32R)
        lo = sb("m_lo", [P, SLOTS, SEL], F32R)
        ln2 = sb("ln2", [P, KT])
        gate = sb("gate", [P, KT, EXPERTS])
        gate_hi = sb("gate_hi", [P, KT, EXPERTS], F32R)
        gate_lo = sb("gate_lo", [P, KT, EXPERTS], F32R)
        cw = sb("cw", [P, BATCHES, EXPERTS + 1])
        cwT_hi = sb("cwT_hi", [EXPERTS + 1, BATCHES * P], F32R)
        cwT_lo = sb("cwT_lo", [EXPERTS + 1, BATCHES * P], F32R)
        silu = sb("silu", [P, 2, GW])
        gated = sb("gated", [P, 2, GW])
        inner = sb("inner", [P, 2, GW])
        in_hi = sb("in_hi", [P, RING, GW], F32R)
        in_lo = sb("in_lo", [P, RING, GW], F32R)
        bank = [ctx.enter_context(nc.psum_tensor(f"m_bank{i}", [P, GW], F32)) for i in range(8)]
        g_ps, u_ps, c_ps, o_ps = bank[0:2], bank[2:4], bank[4:6], bank[6:8]
        nrm = Norm(nc, ctx, "m", bank[0:4])
        PAD = EXPERTS // 2
        lg, pr, gt, eq, sel = (sb(n, [P, BATCHES, EXPERTS]) for n in ("lg", "pr", "gt", "eq", "g_sel"))
        pre = [sb(f"pre{i}", [P, BATCHES, PAD + EXPERTS]) for i in range(2)]
        top8 = sb("top8", [P, BATCHES, 8])
        gmx, cnt, need, tot, inv = (sb(n, [P, BATCHES]) for n in ("gmx", "cnt", "need", "tot", "inv"))

        small_in, x_plus, gate_split, gate_split2 = sem("small_in"), sem("x_plus"), sem("gate_split"), sem("gate_split2")
        logits_done, g_shift, g_exp, g_chain, cw_ready = (sem(n) for n in ("logits_done", "g_shift", "g_exp", "g_chain", "cw_ready"))
        cwT_done, cwT_hid, cwT_lod = sem("cwT_done"), sem("cwT_hid"), sem("cwT_lod")
        raw_in = [sem(f"m_raw_in{j}") for j in range(SLOTS)]
        up_hi_split, up_split, down_hi_split, down_split = (sem(n) for n in ("up_hi_split", "up_split", "down_hi_split", "down_split"))
        g_done, u_done, c_done, silu_done, gated_done, inner_done = (
            sem(n) for n in ("g_done", "u_done", "c_done", "silu_done", "gated_done", "inner_done"))
        in_hid, in_lod, down_done, added = (sem(n) for n in ("in_hid", "in_lod", "down_done", "added"))

        def spread(a):
            return a.unsqueeze(2).broadcast_to([P, BATCHES, EXPERTS])

        def gate_vector(ve):
            links = [0]

            def link(instruction):
                links[0] += 1
                instruction.then_inc(g_chain, 1)
                ve.wait_ge(g_chain, links[0])

            lps = o_ps[0][:, 0:BATCHES * EXPERTS].rearrange("p (t e) -> p t e", e=EXPERTS)
            ve.memset(cw[:, :, EXPERTS:EXPERTS + 1], 1.0)
            ve.memset(pre[0][:], 0.0)
            link(ve.memset(pre[1][:], 0.0))
            ve.wait_ge(logits_done, 1)
            link(ve.tensor_reduce(gmx[:], lps, X_AXIS, ALU.max))
            ve.tensor_tensor(lg[:], lps, spread(gmx[:]), ALU.subtract).then_inc(g_shift, 1)
            ve.wait_ge(g_exp, 1)
            for t in range(BATCHES):
                last = ve.max(top8[:, t], pr[:, t])
            link(last)
            sixth = spread(top8[:, :, TOP - 1])
            ve.tensor_tensor(eq[:], pr[:], sixth, ALU.is_equal)
            link(ve.tensor_tensor(gt[:], pr[:], sixth, ALU.is_gt))
            ve.tensor_copy(pre[0][:, :, PAD:], eq[:])
            link(ve.tensor_reduce(cnt[:], gt[:], X_AXIS, ALU.add))
            link(ve.tensor_scalar(need[:], cnt[:], -1.0, float(TOP), ALU.mult, ALU.add))
            for i, shift in enumerate((1, 2, 4, 8)):
                a, b = pre[i % 2], pre[(i + 1) % 2]
                link(ve.tensor_tensor(b[:, :, PAD:], a[:, :, PAD:], a[:, :, PAD - shift:PAD - shift + EXPERTS], ALU.add))
            link(ve.tensor_tensor(sel[:], pre[0][:, :, PAD:], spread(need[:]), ALU.is_le))
            link(ve.tensor_tensor(sel[:], sel[:], eq[:], ALU.mult))
            link(ve.tensor_tensor(sel[:], sel[:], gt[:], ALU.add))
            link(ve.tensor_tensor(sel[:], sel[:], pr[:], ALU.mult))
            link(ve.tensor_reduce(tot[:], sel[:], X_AXIS, ALU.add))
            link(ve.reciprocal(inv[:], tot[:]))
            ve.tensor_tensor(cw[:, :, 0:EXPERTS], sel[:], spread(inv[:]), ALU.mult).then_inc(cw_ready, 1)
            for g in range(GROUPS):
                ve.wait_ge(cwT_hid, g + 1)
                cols = slice(g * GW, (g + 1) * GW)
                ve.tensor_tensor(cwT_lo[:, cols], bank[g][0:EXPERTS + 1, :], cwT_hi[:, cols].bitcast(F32),
                                 ALU.subtract).then_inc(cwT_lod, 1)

        def pe_up(pe, it, i):
            S, g, j, par = it * STEPS + i, i // SLOTS, i % SLOTS, i % 2
            early = isinstance(it, int) and S < 2
            if g == 0 and not (isinstance(it, int) and it == 0):
                pe.wait_ge(up_split, (it - 1) * SLOTS + j + 1)
            cols = slice(g * GW, (g + 1) * GW)
            for base, out, done, free in ((0, g_ps[par], g_done, silu_done), (UP, u_ps[par], u_done, gated_done)):
                if not early:
                    pe.wait_ge(free, S - 1)
                for k in range(KT):
                    wc = slice(base + k * P, base + (k + 1) * P)
                    mm = parts(pe, out[:], hi[:, j, wc], lo[:, j, wc], hT_hi[:, k, cols], hT_lo[:, k, cols],
                               start=(k == 0), stop=(k == KT - 1))
                mm.then_inc(done, 1)
            if not early:
                pe.wait_ge(inner_done, S - 1)
            sel_rows = hi[0:EXPERTS + 1, j, SEL:WCOLS]
            pe.matmul(c_ps[par][:], sel_rows, cwT_hi[:, cols], start=True, stop=False)
            pe.matmul(c_ps[par][:], sel_rows, cwT_lo[:, cols], start=False, stop=True).then_inc(c_done, 1)

        def pe_down(pe, it, i):
            S, g, j = it * STEPS + i, i // SLOTS, i % SLOTS
            pe.wait_ge(in_lod, S + 1)
            if g == 0 and not (isinstance(it, int) and it == 0):
                pe.wait_ge(down_split, (it - 1) * SLOTS + j + 1)
            if j == 0 and not (isinstance(it, int) and it == 0 and g == 0):
                pe.wait_ge(added, 2 * (it * GROUPS + g))
            for b in range(GROUP):
                c = slice(b * P, (b + 1) * P)
                mm = parts(pe, o_ps[b // 2][:, (b % 2) * D:(b % 2 + 1) * D], in_hi[:, i % RING, c], in_lo[:, i % RING, c],
                           hi[:, j, DOWN:SEL], lo[:, j, DOWN:SEL], start=(j == 0 and b % 2 == 0), stop=(j == SLOTS - 1))
            mm.then_inc(down_done, 1)

        def lagging(it, i, first):
            return (it, i - LAG) if i >= LAG else None if first else (it - 1, i - LAG + STEPS)

        def pe_pass(pe, it, first=False):
            for i in range(STEPS):
                pe_up(pe, it, i)
                if (before := lagging(it, i, first)) is not None:
                    pe_down(pe, *before)

        def act_silu(act, it, i):
            S = it * STEPS + i
            act.wait_ge(g_done, S + 1)
            act.activation(silu[:, i % 2], g_ps[i % 2][:], ACT.Silu).then_inc(silu_done, 1)

        def act_hi(act, it, i):
            S = it * STEPS + i
            act.wait_ge(inner_done, S + 1)
            act.activation(in_hi[:, i % RING], inner[:, i % 2], ACT.Copy).then_inc(in_hid, 1)

        def act_pass(act, it, first=False):
            for i in range(STEPS):
                act_silu(act, it, i)
                if i > 0:
                    act_hi(act, it, i - 1)
                elif not first:
                    act_hi(act, it - 1, STEPS - 1)

        def ve_add(ve, it, i):
            S, g = it * STEPS + i, i // SLOTS
            ve.wait_ge(down_done, S + 1)
            for n in range(2):
                x = e.X[:, g * GROUP + 2 * n:g * GROUP + 2 * n + 2].rearrange("p t d -> p (t d)")
                if not (isinstance(it, int) and it == 0):
                    ve.wait_ge(added, 2 * (it * GROUPS + g) + n)
                ve.tensor_tensor(x, o_ps[n][:], x, ALU.add).then_inc(added, 1)

        def ve_pass(ve, it, first=False):
            for i in range(STEPS):
                S, par = it * STEPS + i, i % 2
                ve.wait_ge(silu_done, S + 1)
                ve.wait_ge(u_done, S + 1)
                ve.tensor_tensor(gated[:, par], u_ps[par][:], silu[:, par], ALU.mult).then_inc(gated_done, 1)
                ve.wait_ge(c_done, S + 1)
                ve.wait_ge(gated_done, S + 1)
                if not (isinstance(it, int) and S < 2):
                    ve.wait_ge(in_lod, S - 1)
                ve.tensor_tensor(inner[:, par], c_ps[par][:], gated[:, par], ALU.mult).then_inc(inner_done, 1)
                before = lagging(it, i, first)
                if before is not None and before[1] % SLOTS == SLOTS - 1:
                    ve_add(ve, *before)

        def pool_low(pool, it, i):
            S = it * STEPS + i
            pool.wait_ge(in_hid, S + 1)
            pool.tensor_tensor(in_lo[:, i % RING], inner[:, i % 2], in_hi[:, i % RING].bitcast(F32),
                               ALU.subtract).then_inc(in_lod, 1)

        def pool_refill_up(pool, it, j):
            pool.wait_ge(c_done, it * STEPS + STEPS - SLOTS + j + 1)
            pool.wait_ge(raw_in[j], 16 * (it + 2))
            copy_pool(pool, e, hi[:, j, SEL:WCOLS], raw[:, j, SEL:WCOLS])
            copy_pool(pool, e, hi[:, j, 0:DOWN], raw[:, j, 0:DOWN]).then_inc(up_hi_split, 1)
            pool.wait_ge(up_hi_split, it * SLOTS + j + 1)
            pool.tensor_tensor(lo[:, j, 0:DOWN], raw[:, j, 0:DOWN], hi[:, j, 0:DOWN].bitcast(F32),
                               ALU.subtract).then_inc(up_split, 1)

        def pool_refill_down(pool, it, j):
            pool.wait_ge(down_done, it * STEPS + STEPS - SLOTS + j + 1)
            copy_pool(pool, e, hi[:, j, DOWN:SEL], raw[:, j, DOWN:SEL]).then_inc(down_hi_split, 1)
            pool.wait_ge(down_hi_split, it * SLOTS + j + 1)
            pool.tensor_tensor(lo[:, j, DOWN:SEL], raw[:, j, DOWN:SEL], hi[:, j, DOWN:SEL].bitcast(F32),
                               ALU.subtract).then_inc(down_split, 1)

        def pool_pass(pool, it, first=False, last=False):
            for i in range(STEPS):
                pool_low(pool, it, i)
                if not last and i >= STEPS - SLOTS:
                    pool_refill_up(pool, it, i - (STEPS - SLOTS))
                back = i - (STEPS - SLOTS) - LAG
                if not last and back >= 0:
                    pool_refill_down(pool, it, back)
                if not first and i < LAG:
                    pool_refill_down(pool, it - 1, SLOTS - LAG + i)

        with nc.Block() as block:
            @block.sync
            def _(sp):
                sp.dma_start(ln2[:], ins["ln2"]).then_inc(small_in, 16)
                sp.dma_start(gate[:], ins["gate"]).then_inc(small_in, 16)
                for j in range(SLOTS):
                    sp.dma_start(raw[:, j], ins["w_moe"][:, j]).then_inc(raw_in[j], 16)
                for j in range(SLOTS):
                    sp.wait_ge(gate_split2, j + 1)
                    sp.dma_start(raw[:, j], ins["w_moe"][:, SLOTS + j]).then_inc(raw_in[j], 16)
                with sp.Fori(2, PASSES) as it:
                    for j in range(SLOTS):
                        sp.wait_ge(down_split, (it - 2) * SLOTS + j + 1)
                        sp.wait_ge(up_split, (it - 2) * SLOTS + j + 1)
                        sp.dma_start(raw[:, j:j + 1], ins["w_moe"][:, ds(it * SLOTS + j, 1)]).then_inc(raw_in[j], 16)

            @block.gpsimd
            def _(pool):
                pool.wait_ge(small_in, 32)
                pool.tensor_scalar(gate_hi[:], gate[:], 1.0, None, ALU.mult).then_inc(gate_split, 1)
                pool.wait_ge(gate_split, 1)
                pool.tensor_tensor(gate_lo[:], gate[:], gate_hi[:].bitcast(F32), ALU.subtract).then_inc(gate_split, 1)
                for j in range(SLOTS):
                    pool.wait_ge(raw_in[j], 16)
                    pool.tensor_scalar(hi[:, j], raw[:, j], 1.0, None, ALU.mult).then_inc(gate_split, 1)
                    pool.wait_ge(gate_split, 3 + j)
                    pool.tensor_tensor(lo[:, j], raw[:, j, 0:SEL], hi[:, j, 0:SEL].bitcast(F32),
                                       ALU.subtract).then_inc(gate_split2, 1)
                pool.tensor_tensor(e.X[:].rearrange("p t d -> p (t d)"), e.X[:].rearrange("p t d -> p (t d)"),
                                   e.Y[:].rearrange("p t d -> p (t d)"), ALU.add).then_inc(x_plus, 1)
                pool_pass(pool, 0, first=True)
                with pool.Fori(1, PASSES - 1) as it:
                    pool_pass(pool, it)
                pool_pass(pool, PASSES - 1, last=True)

            @block.scalar
            def _(act):
                act.wait_ge(small_in, 32)
                norm_scalar(act, nrm, hT_hi, ln2)
                act.wait_ge(g_shift, 1)
                act.activation(pr[:], lg[:], ACT.Exp).then_inc(g_exp, 1)
                for g in range(GROUPS):
                    act.wait_ge(cwT_done, g + 1)
                    act.activation(cwT_hi[:, g * GW:(g + 1) * GW], bank[g][0:EXPERTS + 1, :], ACT.Copy).then_inc(cwT_hid, 1)
                act_pass(act, 0, first=True)
                with act.Fori(1, PASSES) as it:
                    act_pass(act, it)
                act_hi(act, PASSES - 1, STEPS - 1)

            @block.vector
            def _(ve):
                ve.wait_ge(small_in, 32)
                norm_vector(ve, nrm, e.Y, RMS_EPS, False, hT_hi, hT_lo, ln2)
                gate_vector(ve)
                ve.wait_ge(x_plus, 1)
                ve_pass(ve, 0, first=True)
                with ve.Fori(1, PASSES) as it:
                    ve_pass(ve, it)
                ve_add(ve, PASSES - 1, STEPS - 1)

            @block.tensor
            def _(pe):
                norm_tensor(pe, nrm, e.ident[:])
                pe.wait_ge(gate_split, 2)
                pe.wait_ge(nrm.lo_done, KT * GROUPS)
                for t in range(BATCHES):
                    out = o_ps[0][:, t * EXPERTS:(t + 1) * EXPERTS]
                    for k in range(KT):
                        c = slice(t * P, (t + 1) * P)
                        mm = parts(pe, out, hT_hi[:, k, c], hT_lo[:, k, c], gate_hi[:, k], gate_lo[:, k],
                                   start=(t == 0 and k == 0), stop=(k == KT - 1))
                mm.then_inc(logits_done, 1)
                pe.wait_ge(cw_ready, 1)
                for g in range(GROUPS):
                    for b in range(GROUP):
                        mm = pe.transpose(bank[g][0:EXPERTS + 1, b * P:(b + 1) * P], cw[:, g * GROUP + b], e.ident[:])
                    mm.then_inc(cwT_done, 1)
                pe.wait_ge(cwT_lod, GROUPS)
                pe.wait_ge(gate_split2, SLOTS)
                pe_pass(pe, 0, first=True)
                with pe.Fori(1, PASSES) as it:
                    pe_pass(pe, it)
                for i in range(STEPS - LAG, STEPS):
                    pe_down(pe, PASSES - 1, i)


KVC, QC, ROPE = 64, 96, 64
HALF = ROPE // 2
LOOKBACK = 8
T_EVEN, T_ODD, T_SIN_Q, T_COS, T_SIN, T_KEY = range(6)


class LatentState:

    def __init__(self, nc, ctx):
        def sb(name, shape, dt=F32):
            return ctx.enter_context(nc.sbuf_tensor(f"l_{name}", shape, dt))

        self.key_hi = sb("key_hi", [P, 2, BATCHES * P], F32R)
        self.key_lo = sb("key_lo", [P, 2, BATCHES * P], F32R)
        self.val = sb("val", [P, BATCHES, 2, 3 * KVC], F32R)
        self.mask = sb("mask", [P, BATCHES, P], F32R)
        self.wa_hi = sb("wa_hi", [QC, HEADS, P], F32R)
        self.wa_lo = sb("wa_lo", [QC, HEADS, P], F32R)
        self.wb_hi = sb("wb_hi", [QC, PAIRS, P], F32R)
        self.wb_lo = sb("wb_lo", [QC, PAIRS, P], F32R)
        self.wv_hi = sb("wv_hi", [P, PAIRS, D], F32R)
        self.wv_lo = sb("wv_lo", [P, PAIRS, D], F32R)
        self.tab = sb("tab", [P, 6, P])


def phase_latent_keys(nc, e, ins, z):
    with ExitStack() as ctx:
        def sb(name, shape, dt=F32):
            return ctx.enter_context(nc.sbuf_tensor(f"k_{name}", shape, dt))

        def sem(name):
            return ctx.enter_context(nc.semaphore(f"k_{name}"))

        ctxT = sb("ctxT", [P, KT, BATCHES * P])
        wkvc = sb("wkvc", [P, KT, 2 * KVC])
        wkr = sb("wkr", [KVC, 2, P])
        uqT = sb("uqT", [P, HEADS, QC])
        ukT = sb("ukT", [P, HEADS, KVC])
        uvT = sb("uvT", [P, HEADS, KVC])
        wo = sb("wo", [P, HEADS, D])
        qr = sb("qr", [QC, HEADS, ROPE])
        qrb = sb("qrb", [QC, PAIRS, P])
        seg = sb("seg", [P, BATCHES], I32)
        segf = sb("segf", [P, BATCHES])
        dist = sb("dist", [P, BATCHES, P])
        near = sb("near", [P, BATCHES, P])
        kvT = sb("kvT", [P, GW])
        rot = sb("rot", [P, 2, GW])
        rot2 = sb("rot2", [P, GW])
        bank = [ctx.enter_context(nc.psum_tensor(f"k_bank{i}", [P, GW], F32)) for i in range(8)]

        w_in, ctx_in, tab_in, seg_in = sem("w_in"), sem("ctx_in"), sem("tab_in"), sem("seg_in")
        absorbed, a_hi, a_lo, wv_done, wv_hi, wv_lo = (sem(n) for n in ("absorbed", "a_hi", "a_lo", "wv_done", "wv_hi", "wv_lo"))
        qr_hi, pool_chain, val_zero = sem("qr_hi"), sem("pool"), sem("val_zero")
        kvT_done, kvT_sb, kr_done, kv_done = sem("kvT_done"), sem("kvT_sb"), sem("kr_done"), sem("kv_done")
        key_hi, key_lo, val_hi, val_lo, r1, r2, r3, rk_hi, rk_lo = (
            sem(n) for n in ("key_hi", "key_lo", "val_hi", "val_lo", "r1", "r2", "r3", "rk_hi", "rk_lo"))

        with nc.Block() as block:
            @block.sync
            def _(sp):
                for dst, name in ((uqT, "uqT"), (ukT, "ukT"), (wkvc, "wkvc"), (wkr, "wkr"), (uvT, "uvT"), (wo, "w_o2"),
                                  (qr, "qr"), (qrb, "qrb")):
                    sp.dma_start(dst[:], ins[name]).then_inc(w_in, 16)

            @block.gpsimd
            def _(pool):
                links = [0]

                def link(instruction):
                    links[0] += 1
                    instruction.then_inc(pool_chain, 1)
                    pool.wait_ge(pool_chain, links[0])

                pool.memset(z.val[:].bitcast(F32), 0.0).then_inc(val_zero, 1)
                pool.wait_ge(seg_in, 16)
                link(pool.tensor_copy(segf[:], seg[:]))
                pool.wait_ge(tab_in, 16)
                keys = z.tab[:, T_KEY].unsqueeze(1).broadcast_to([P, BATCHES, P])
                link(pool.tensor_tensor(dist[:], keys, segf[:].unsqueeze(2).broadcast_to([P, BATCHES, P]), ALU.subtract))
                pool.tensor_scalar(near[:], dist[:], float(-LOOKBACK), -1.0e30, ALU.is_lt, ALU.mult)
                link(pool.tensor_scalar(dist[:], dist[:], 0.0, -1.0e30, ALU.is_gt, ALU.mult))
                pool.tensor_tensor(z.mask[:], near[:], dist[:], ALU.add)
                pool.wait_ge(w_in, 16 * 8)
                link(pool.tensor_scalar(z.wb_hi[:], qrb[:], 1.0, None, ALU.mult))
                pool.tensor_tensor(z.wb_lo[:], qrb[:], z.wb_hi[:].bitcast(F32), ALU.subtract)
                for odd in range(2):
                    cols = slice(0, ROPE) if odd else slice(KVC, P)
                    link(pool.tensor_scalar(z.wa_hi[:, odd::2, cols], qr[:, odd::2], 1.0, None, ALU.mult))
                    pool.tensor_tensor(z.wa_lo[:, odd::2, cols], qr[:, odd::2], z.wa_hi[:, odd::2, cols].bitcast(F32), ALU.subtract)

            @block.tensor
            def _(pe):
                pe.wait_ge(w_in, 16 * 8)
                for h in range(HEADS):
                    mm = pe.matmul(bank[h // 8][0:QC, (h % 8) * KVC:(h % 8 + 1) * KVC], uqT[:, h], ukT[:, h],
                                   start=True, stop=True)
                mm.then_inc(absorbed, 1)
                for p in range(PAIRS):
                    for odd in range(2):
                        mm = pe.matmul(bank[2 + p // 2][odd * KVC:(odd + 1) * KVC, (p % 2) * D:(p % 2 + 1) * D],
                                       uvT[:, 2 * p + odd], wo[:, 2 * p + odd], start=True, stop=True)
                mm.then_inc(wv_done, 1)
                pe.wait_ge(ctx_in, 16)
                for g in range(GROUPS):
                    cols = slice(g * GW, (g + 1) * GW)
                    if g == 0:
                        pe.wait_ge(a_lo, 4)
                    else:
                        pe.wait_ge(key_lo, 2 * g)
                    for k in range(KT):
                        mm = pe.matmul(bank[0][:], wkvc[:, k], ctxT[:, k, cols], start=(k == 0), stop=(k == KT - 1))
                    mm.then_inc(kvT_done, 1)
                    if g > 0:
                        pe.wait_ge(val_lo, g)
                    for b in range(GROUP):
                        t = g * GROUP + b
                        for k in range(KT):
                            mm = pe.matmul(bank[1][:, b * KVC:(b + 1) * KVC], ctxT[:, k, t * P:(t + 1) * P],
                                           wkvc[:, k, 0:KVC], start=(b == 0 and k == 0), stop=(k == KT - 1),
                                           skip_group_check=True)
                    mm.then_inc(kv_done, 1)
                    pe.wait_ge(kvT_sb, g + 1)
                    if g == 0:
                        pe.wait_ge(wv_lo, 4)
                    else:
                        pe.wait_ge(r2, g)
                    pe.matmul(bank[2][:], wkr[:, 0], kvT[0:KVC, :], start=True, stop=True)
                    pe.matmul(bank[3][:], wkr[:, 1], kvT[0:KVC, :], start=True, stop=True).then_inc(kr_done, 1)

            @block.scalar
            def _(act):
                act.dma_start(seg[:], ins["seg"]).then_inc(seg_in, 16)
                act.dma_start(z.tab[:], ins["tab"]).then_inc(tab_in, 16)
                act.dma_start(ctxT[:], ins["ctxT"].rearrange("(k p) t -> p k t", p=P)).then_inc(ctx_in, 16)
                act.wait_ge(absorbed, 1)
                for half in range(2):
                    for odd in range(2):
                        cols = slice(KVC, P) if odd else slice(0, KVC)
                        src = bank[half][0:QC, :].rearrange("q (h c) -> q h c", c=KVC)[:, odd::2]
                        act.activation(z.wa_hi[:, 8 * half + odd:8 * half + 8:2, cols], src, ACT.Copy).then_inc(a_hi, 1)
                act.wait_ge(wv_done, 1)
                for i in range(4):
                    act.activation(z.wv_hi[:, 2 * i:2 * i + 2].rearrange("p a c -> p (a c)"), bank[2 + i][:], ACT.Copy).then_inc(wv_hi, 1)
                act.wait_ge(val_zero, 1)
                for g in range(GROUPS):
                    cols = slice(g * GW, (g + 1) * GW)
                    act.wait_ge(kvT_done, g + 1)
                    if g > 0:
                        act.wait_ge(kr_done, g)
                    act.activation(kvT[:], bank[0][:], ACT.Copy).then_inc(kvT_sb, 1)
                    act.activation(z.key_hi[0:KVC, 0, cols], bank[0][0:KVC, :], ACT.Copy).then_inc(key_hi, 1)
                    act.activation(z.key_hi[KVC:P, 1, cols], bank[0][KVC:P, :], ACT.Copy).then_inc(key_hi, 1)
                    act.wait_ge(kv_done, g + 1)
                    act.activation(z.val[:, g * GROUP:(g + 1) * GROUP, 0, KVC:2 * KVC],
                                   bank[1][:, 0:GROUP * KVC].rearrange("p (b c) -> p b c", b=GROUP), ACT.Copy).then_inc(val_hi, 1)
                    act.wait_ge(r3, g + 1)
                    act.activation(z.key_hi[KVC:P, 0, cols], rot[KVC:P, g % 2], ACT.Copy).then_inc(rk_hi, 1)
                    act.activation(z.key_hi[0:KVC, 1, cols], rot[0:KVC, g % 2], ACT.Copy).then_inc(rk_hi, 1)

            @block.vector
            def _(ve):
                for half in range(2):
                    for odd in range(2):
                        cols = slice(KVC, P) if odd else slice(0, KVC)
                        src = bank[half][0:QC, :].rearrange("q (h c) -> q h c", c=KVC)[:, odd::2]
                        heads = slice(8 * half + odd, 8 * half + 8, 2)
                        ve.wait_ge(a_hi, 2 * half + 2)
                        ve.tensor_tensor(z.wa_lo[:, heads, cols], src, z.wa_hi[:, heads, cols].bitcast(F32),
                                         ALU.subtract).then_inc(a_lo, 1)
                for i in range(4):
                    ve.wait_ge(wv_hi, i + 1)
                    ve.tensor_tensor(z.wv_lo[:, 2 * i:2 * i + 2].rearrange("p a c -> p (a c)"), bank[2 + i][:],
                                     z.wv_hi[:, 2 * i:2 * i + 2].rearrange("p a c -> p (a c)").bitcast(F32),
                                     ALU.subtract).then_inc(wv_lo, 1)
                ve.wait_ge(tab_in, 16)
                for g in range(GROUPS):
                    cols = slice(g * GW, (g + 1) * GW)
                    for odd in range(2):
                        rows = slice(KVC, P) if odd else slice(0, KVC)
                        ve.wait_ge(key_hi, 2 * g + odd + 1)
                        ve.tensor_tensor(z.key_lo[rows, odd, cols], bank[0][rows, :], z.key_hi[rows, odd, cols].bitcast(F32),
                                         ALU.subtract).then_inc(key_lo, 1)
                    ve.wait_ge(val_hi, g + 1)
                    tiles = slice(g * GROUP, (g + 1) * GROUP)
                    ve.tensor_tensor(z.val[:, tiles, 1, KVC:2 * KVC], bank[1][:, 0:GROUP * KVC].rearrange("p (b c) -> p b c", b=GROUP),
                                     z.val[:, tiles, 0, KVC:2 * KVC].bitcast(F32), ALU.subtract).then_inc(val_lo, 1)
                    ve.wait_ge(kr_done, g + 1)

                    def table(n):
                        return z.tab[:, n].unsqueeze(1).broadcast_to([P, GROUP, P])

                    def by_batch(a):
                        return a.rearrange("p (b c) -> p b c", b=GROUP)

                    if g >= 1:
                        ve.wait_ge(rk_lo, 2 * g)
                    ve.tensor_tensor(by_batch(rot2[:]), by_batch(bank[3][:]), table(T_SIN), ALU.mult).then_inc(r1, 1)
                    ve.tensor_tensor(by_batch(rot[:, g % 2]), by_batch(bank[2][:]), table(T_COS), ALU.mult).then_inc(r2, 1)
                    ve.wait_ge(r1, g + 1)
                    ve.wait_ge(r2, g + 1)
                    ve.tensor_tensor(rot[:, g % 2], rot[:, g % 2], rot2[:], ALU.add).then_inc(r3, 1)
                    for odd in range(2):
                        rows = slice(0, KVC) if odd else slice(KVC, P)
                        ve.wait_ge(rk_hi, 2 * g + odd + 1)
                        ve.tensor_tensor(z.key_lo[rows, odd, cols], rot[rows, g % 2], z.key_hi[rows, odd, cols].bitcast(F32),
                                         ALU.subtract).then_inc(rk_lo, 1)


def phase_latent_queries(nc, e, ins, z, qc_hi, qc_lo):
    with ExitStack() as ctx:
        def sb(name, shape, dt=F32):
            return ctx.enter_context(nc.sbuf_tensor(f"q_{name}", shape, dt))

        def sem(name):
            return ctx.enter_context(nc.semaphore(f"q_{name}"))

        hT_hi = sb("hT_hi", [P, KT, BATCHES * P], F32R)
        hT_lo = sb("hT_lo", [P, KT, BATCHES * P], F32R)
        wdq = sb("wdq", [P, KT, QC])
        wdq_hi = sb("wdq_hi", [P, KT, QC], F32R)
        wdq_lo = sb("wdq_lo", [P, KT, QC], F32R)
        bank = [ctx.enter_context(nc.psum_tensor(f"q_bank{i}", [P, GW], F32)) for i in range(6)]
        nrm = Norm(nc, ctx, "q", bank[0:4])
        w_in, w_hi, w_lo, qc_done, qc_hid, qc_lod = (sem(n) for n in ("w_in", "w_hi", "w_lo", "qc_done", "qc_hid", "qc_lod"))

        with nc.Block() as block:
            @block.sync
            def _(sp):
                sp.dma_start(wdq[:], ins["wdq"]).then_inc(w_in, 16)

            @block.gpsimd
            def _(pool):
                pool.wait_ge(w_in, 16)
                pool.tensor_scalar(wdq_hi[:], wdq[:], 1.0, None, ALU.mult).then_inc(w_hi, 1)
                pool.wait_ge(w_hi, 1)
                pool.tensor_tensor(wdq_lo[:], wdq[:], wdq_hi[:].bitcast(F32), ALU.subtract).then_inc(w_lo, 1)

            @block.tensor
            def _(pe):
                norm_tensor(pe, nrm, e.ident[:])
                pe.wait_ge(w_lo, 1)
                for g in range(GROUPS):
                    cols = slice(g * GW, (g + 1) * GW)
                    pe.wait_ge(nrm.lo_done, KT * (g + 1))
                    if g >= 2:
                        pe.wait_ge(qc_lod, g - 1)
                    for k in range(KT):
                        mm = parts(pe, bank[4 + g % 2][0:QC, :], wdq_hi[:, k], wdq_lo[:, k], hT_hi[:, k, cols],
                                   hT_lo[:, k, cols], start=(k == 0), stop=(k == KT - 1))
                    mm.then_inc(qc_done, 1)

            @block.scalar
            def _(act):
                norm_scalar(act, nrm, hT_hi)
                for g in range(GROUPS):
                    act.wait_ge(qc_done, g + 1)
                    act.activation(qc_hi[:, g * GW:(g + 1) * GW], bank[4 + g % 2][0:QC, :], ACT.Copy).then_inc(qc_hid, 1)

            @block.vector
            def _(ve):
                norm_vector(ve, nrm, e.X, LN_EPS, True, hT_hi, hT_lo)
                for g in range(GROUPS):
                    cols = slice(g * GW, (g + 1) * GW)
                    ve.wait_ge(qc_hid, g + 1)
                    ve.tensor_tensor(qc_lo[:, cols], bank[4 + g % 2][0:QC, :], qc_hi[:, cols].bitcast(F32),
                                     ALU.subtract).then_inc(qc_lod, 1)


def phase_latent_attention(nc, e, z, qc_hi, qc_lo):
    AHEAD = 2
    with ExitStack() as ctx:
        def sb(name, shape, dt=F32):
            return ctx.enter_context(nc.sbuf_tensor(f"t_{name}", shape, dt))

        def sem(name):
            return ctx.enter_context(nc.semaphore(f"t_{name}"))

        val = sb("val", [P, GROUP, 2, 3 * KVC], F32R)
        rot = sb("rot", [P, GW])
        q32 = sb("q32", [P, 2, GW])
        q_hi = sb("q_hi", [P, 2, 2, GW], F32R)
        q_lo = sb("q_lo", [P, 2, 2, GW], F32R)
        prob = sb("prob", [P, 2, 2, GROUP, P])
        pT_hi = sb("pT_hi", [P, 2, GW], F32R)
        pT_lo = sb("pT_lo", [P, 2, GW], F32R)
        c_hi = sb("c_hi", [P, 2, GW], F32R)
        c_lo = sb("c_lo", [P, 2, GW], F32R)
        nmax, sums, rec = (sb(n, [P, 2, 2, GROUP]) for n in ("nmax", "sums", "rec"))
        bank = [ctx.enter_context(nc.psum_tensor(f"t_bank{i}", [P, GW], F32)) for i in range(8)]
        b_ps, a_ps, pT_ps, sc_ps, wo_ps = bank[0], bank[1:3], bank[3], bank[4:6], bank[6:8]
        c_ps = b_ps

        rot_proj, rot_done, q_proj, cos_done, q_sum, q_hid, q_lod = (
            sem(n) for n in ("rot_proj", "rot_done", "q_proj", "cos_done", "q_sum", "q_hid", "q_lod"))
        scores_done, max_done, exp_done, rec_done, norm_even, norm_odd = (
            sem(n) for n in ("scores_done", "max_done", "exp_done", "rec_done", "norm_even", "norm_odd"))
        pT_done, pT_hid, pT_lod, pv_done, c_hid, c_lod, wo_done, added, val_in = (
            sem(n) for n in ("pT_done", "pT_hid", "pT_lod", "pv_done", "c_hid", "c_lod", "wo_done", "added", "val_in"))

        def shifted(it, i, by, first, last):
            n = i + by
            if n < 0:
                return None if first else (it - 1, n + PAIRS)
            if n >= PAIRS:
                return None if last else (it + 1, n - PAIRS)
            return it, n

        def known_before(it, i, n):
            return isinstance(it, int) and it * PAIRS + i < n

        def columns(it):
            return slice(it * GW, (it + 1) * GW) if isinstance(it, int) else ds(it * GW, GW)

        def pe_rot(pe, it, i):
            S = it * PAIRS + i
            if not known_before(it, i, AHEAD + 2):
                pe.wait_ge(c_lod, S - AHEAD - 1)
            elif S > 0:
                pe.wait_ge(rot_done, S)
            parts(pe, b_ps[:], z.wb_hi[:, i], z.wb_lo[:, i], qc_hi[:, columns(it)], qc_lo[:, columns(it)],
                  start=True, stop=True).then_inc(rot_proj, 1)

        def pe_query(pe, it, i, h):
            S = it * PAIRS + i
            if not known_before(it, i, 1):
                pe.wait_ge(cos_done, 2 * S - 1 + h)
            parts(pe, a_ps[h][:], z.wa_hi[:, 2 * i + h], z.wa_lo[:, 2 * i + h], qc_hi[:, columns(it)],
                  qc_lo[:, columns(it)], start=True, stop=True).then_inc(q_proj, 1)

        def pe_scores(pe, it, i):
            S = it * PAIRS + i
            for h in range(2):
                pe.wait_ge(q_lod, 2 * S + h + 1)
                if not known_before(it, i, 1):
                    pe.wait_ge(exp_done, GROUP * (2 * S - 1 + h))
                for b in range(GROUP):
                    c = slice(b * P, (b + 1) * P)
                    keys = (it * GROUP + b) * P
                    at = slice(keys, keys + P) if isinstance(it, int) else ds(keys, P)
                    parts(pe, sc_ps[h][:, c], q_hi[:, i % 2, h, c], q_lo[:, i % 2, h, c], z.key_hi[:, h, at],
                          z.key_lo[:, h, at], start=(b == 0))
                pe.matmul(sc_ps[h][:].rearrange("p (b k) -> p b k", b=GROUP), e.ident_r[:],
                          z.mask[:, ds(it * GROUP, GROUP)], start=False, stop=True, skip_group_check=True)\
                    .then_inc(scores_done, 1)

        def pe_turn(pe, it, i, h):
            S = it * PAIRS + i
            pe.wait_ge((norm_even, norm_odd)[h], S + 1)
            if h == 1:
                pe.wait_ge(pT_lod, 2 * S + 1)
            elif not known_before(it, i, 1):
                pe.wait_ge(pT_lod, 2 * S)
            for b in range(GROUP):
                mm = pe.transpose(pT_ps[:, b * P:(b + 1) * P], prob[:, i % 2, h, b], e.ident[:])
            mm.then_inc(pT_done, 1)

        def pe_values(pe, it, i, ahead):
            S = it * PAIRS + i
            if i == 0:
                pe.wait_ge(val_in, it + 1)
            if ahead:
                pe.wait_ge(rot_done, S + AHEAD + 2)
            else:
                pe.wait_ge(c_lod, S)
            for h in range(2):
                pe.wait_ge(pT_lod, 2 * S + h + 1)
                block_of = slice(KVC, 3 * KVC) if h == 0 else slice(0, 2 * KVC)
                for b in range(GROUP):
                    c = slice(b * P, (b + 1) * P)
                    mm = parts(pe, c_ps[:, c], val[:, b, 0, block_of], val[:, b, 1, block_of], pT_hi[:, h, c],
                               pT_lo[:, h, c], start=(h == 0 and b == 0), stop=(h == 1))
            mm.then_inc(pv_done, 1)

        def pe_out(pe, it, i):
            S = it * PAIRS + i
            pe.wait_ge(c_lod, S + 1)
            if i == 0 and not known_before(it, i, 1):
                pe.wait_ge(added, 2 * it)
            for b in range(GROUP):
                c = slice(b * P, (b + 1) * P)
                mm = parts(pe, wo_ps[b // 2][:, (b % 2) * D:(b % 2 + 1) * D], c_hi[:, i % 2, c], c_lo[:, i % 2, c],
                           z.wv_hi[:, i], z.wv_lo[:, i], start=(i == 0 and b % 2 == 0), stop=(i == PAIRS - 1))
            mm.then_inc(wo_done, 1)

        def pe_pass(pe, it, first=False, last=False):
            for i in range(PAIRS):
                before, before2 = shifted(it, i, -1, first, last), shifted(it, i, -2, first, last)
                ahead = shifted(it, i, AHEAD, first, last)
                pe_scores(pe, it, i)
                if before:
                    pe_turn(pe, *before, 0)
                if ahead:
                    pe_rot(pe, *ahead)
                    pe_query(pe, *ahead, 0)
                if before:
                    pe_turn(pe, *before, 1)
                if ahead:
                    pe_query(pe, *ahead, 1)
                if before:
                    pe_values(pe, *before, ahead=ahead is not None)
                if before2:
                    pe_out(pe, *before2)

        def act_q(act, it, i):
            S = it * PAIRS + i
            for h in range(2):
                act.wait_ge(q_sum, 2 * S + h + 1)
                act.activation(q_hi[:, i % 2, h], q32[:, h], ACT.Copy).then_inc(q_hid, 1)

        def act_exp(act, it, i, h):
            S = it * PAIRS + i
            act.wait_ge(max_done, 2 * S + h + 1)
            for b in range(GROUP):
                act.activation(prob[:, i % 2, h, b], sc_ps[h][:, b * P:(b + 1) * P], ACT.Exp, bias=nmax[:, i % 2, h, b:b + 1],
                               accum_out=sums[:, i % 2, h, b:b + 1]).then_inc(exp_done, 1)

        def act_turn(act, it, i, h):
            act.wait_ge(pT_done, 2 * (it * PAIRS + i) + h + 1)
            act.activation(pT_hi[:, h], pT_ps[:], ACT.Copy).then_inc(pT_hid, 1)

        def act_values(act, it, i):
            act.wait_ge(pv_done, it * PAIRS + i + 1)
            act.activation(c_hi[:, i % 2], c_ps[:], ACT.Copy).then_inc(c_hid, 1)

        def act_pass(act, it, first=False, last=False):
            for i in range(PAIRS):
                before, ahead = shifted(it, i, -1, first, last), shifted(it, i, AHEAD, first, last)
                act_exp(act, it, i, 0)
                if before:
                    act_turn(act, *before, 0)
                    act_turn(act, *before, 1)
                act_exp(act, it, i, 1)
                if ahead:
                    act_q(act, *ahead)
                if before:
                    act_values(act, *before)

        def ve_rot(ve, it, i):
            S = it * PAIRS + i
            ve.wait_ge(rot_proj, S + 1)
            if not known_before(it, i, 1):
                ve.wait_ge(q_sum, 2 * S)
            ve.tensor_tensor(by_batch(rot[:]), by_batch(b_ps[:]), table(T_SIN_Q), ALU.mult).then_inc(rot_done, 1)

        def ve_cos(ve, it, i, h):
            S = it * PAIRS + i
            ve.wait_ge(q_proj, 2 * S + h + 1)
            if not known_before(it, i, 1):
                ve.wait_ge(q_lod, 2 * S - 1 + h)
            ve.tensor_tensor(by_batch(q32[:, h]), by_batch(a_ps[h][:]), table((T_EVEN, T_ODD)[h]), ALU.mult).then_inc(cos_done, 1)

        def table(n):
            return z.tab[:, n].unsqueeze(1).broadcast_to([P, GROUP, P])

        def by_batch(a):
            return a.rearrange("p (b c) -> p b c", b=GROUP)

        def ve_turn(ve, it, i, h):
            ve.wait_ge(pT_hid, 2 * (it * PAIRS + i) + h + 1)
            ve.tensor_tensor(pT_lo[:, h], pT_ps[:], pT_hi[:, h].bitcast(F32), ALU.subtract).then_inc(pT_lod, 1)

        def ve_rec(ve, it, i, h):
            S = it * PAIRS + i
            ve.wait_ge(exp_done, GROUP * (2 * S + h + 1))
            ve.reciprocal(rec[:, i % 2, h], sums[:, i % 2, h]).then_inc(rec_done, 1)

        def ve_norm_odd(ve, it, i):
            ve.wait_ge(rec_done, 2 * (it * PAIRS + i) + 2)
            ve.tensor_tensor(prob[:, i % 2, 1], prob[:, i % 2, 1], over_groups(rec[:, i % 2, 1]), ALU.mult).then_inc(norm_odd, 1)

        def ve_values(ve, it, i):
            ve.wait_ge(c_hid, it * PAIRS + i + 1)
            ve.tensor_tensor(c_lo[:, i % 2], c_ps[:], c_hi[:, i % 2].bitcast(F32), ALU.subtract).then_inc(c_lod, 1)

        def ve_group_values(ve, it, first):
            if not first:
                ve.wait_ge(pv_done, it * PAIRS)
            ve.tensor_scalar(val[:].rearrange("p b a c -> p (b a c)"),
                             z.val[:, ds(it * GROUP, GROUP)].rearrange("p b a c -> p (b a c)").bitcast(F32), 1.0, None,
                             ALU.mult).then_inc(val_in, 1)

        def ve_add(ve, it):
            ve.wait_ge(wo_done, it * PAIRS + PAIRS)
            for n in range(2):
                x = e.X[:, ds(it * GROUP + 2 * n, 2)].rearrange("p t d -> p (t d)")
                ve.tensor_tensor(x, wo_ps[n][:], x, ALU.add).then_inc(added, 1)

        def ve_pass(ve, it, first=False, last=False):
            for i in range(PAIRS):
                S = it * PAIRS + i
                before, ahead = shifted(it, i, -1, first, last), shifted(it, i, AHEAD, first, last)
                for h in range(2):
                    ve.wait_ge(scores_done, 2 * S + h + 1)
                    ve.tensor_reduce(nmax[:, i % 2, h], by_batch(sc_ps[h][:]), X_AXIS, ALU.max, negate=True).then_inc(max_done, 1)
                if before:
                    ve_turn(ve, *before, 0)
                if ahead:
                    ve_rot(ve, *ahead)
                    ve_cos(ve, *ahead, 0)
                ve_rec(ve, it, i, 0)
                if before:
                    ve_turn(ve, *before, 1)
                if ahead:
                    ve_cos(ve, *ahead, 1)
                ve_rec(ve, it, i, 1)
                ve_norm_odd(ve, it, i)
                if before:
                    ve_values(ve, *before)
                if i == 0:
                    ve_group_values(ve, it, first)
                if i == 1 and not first:
                    ve_add(ve, it - 1)

        def pool_sum(pool, it, i, h):
            S = it * PAIRS + i
            rows = slice(KVC, P) if h == 0 else slice(0, ROPE)
            pool.wait_ge(rot_done, S + 1)
            pool.wait_ge(cos_done, 2 * S + h + 1)
            if h == 1:
                pool.wait_ge(q_sum, 2 * S + 1)
            elif not known_before(it, i, 1):
                pool.wait_ge(q_lod, 2 * S)
                if not known_before(it, i, AHEAD):
                    pool.wait_ge(norm_even, S - AHEAD + 1)
            pool.tensor_tensor(q32[rows, h], q32[rows, h], rot[rows, :], ALU.add).then_inc(q_sum, 1)

        def pool_low(pool, it, i, h):
            S = it * PAIRS + i
            pool.wait_ge(q_hid, 2 * S + h + 1)
            pool.wait_ge(q_sum, 2 * S + 2)
            pool.tensor_tensor(q_lo[:, i % 2, h], q32[:, h], q_hi[:, i % 2, h].bitcast(F32), ALU.subtract).then_inc(q_lod, 1)

        def pool_pass(pool, it, first=False, last=False):
            for i in range(PAIRS):
                S = it * PAIRS + i
                ahead = shifted(it, i, AHEAD, first, last)
                pool.wait_ge(rec_done, 2 * S + 1)
                pool.tensor_tensor(prob[:, i % 2, 0], prob[:, i % 2, 0], over_groups(rec[:, i % 2, 0]), ALU.mult).then_inc(norm_even, 1)
                if ahead:
                    pool_sum(pool, *ahead, 0)
                    pool_sum(pool, *ahead, 1)
                    pool_low(pool, *ahead, 0)
                    pool_low(pool, *ahead, 1)

        with nc.Block() as block:
            @block.gpsimd
            def _(pool):
                for i in range(AHEAD):
                    for h in range(2):
                        pool_sum(pool, 0, i, h)
                    for h in range(2):
                        pool_low(pool, 0, i, h)
                pool_pass(pool, 0, first=True)
                with pool.Fori(1, GROUPS - 1) as it:
                    pool_pass(pool, it)
                pool_pass(pool, GROUPS - 1, last=True)

            @block.scalar
            def _(act):
                for i in range(AHEAD):
                    act_q(act, 0, i)
                act_pass(act, 0, first=True)
                with act.Fori(1, GROUPS - 1) as it:
                    act_pass(act, it)
                act_pass(act, GROUPS - 1, last=True)
                for h in range(2):
                    act_turn(act, GROUPS - 1, PAIRS - 1, h)
                act_values(act, GROUPS - 1, PAIRS - 1)

            @block.vector
            def _(ve):
                for i in range(AHEAD):
                    ve_rot(ve, 0, i)
                    ve_cos(ve, 0, i, 0)
                    ve_cos(ve, 0, i, 1)
                ve_pass(ve, 0, first=True)
                with ve.Fori(1, GROUPS - 1) as it:
                    ve_pass(ve, it)
                ve_pass(ve, GROUPS - 1, last=True)
                for h in range(2):
                    ve_turn(ve, GROUPS - 1, PAIRS - 1, h)
                ve_values(ve, GROUPS - 1, PAIRS - 1)
                ve_add(ve, GROUPS - 1)

            @block.tensor
            def _(pe):
                for i in range(AHEAD):
                    pe_rot(pe, 0, i)
                    pe_query(pe, 0, i, 0)
                    pe_query(pe, 0, i, 1)
                pe_pass(pe, 0, first=True)
                with pe.Fori(1, GROUPS - 1) as it:
                    pe_pass(pe, it)
                pe_pass(pe, GROUPS - 1, last=True)
                for h in range(2):
                    pe_turn(pe, GROUPS - 1, PAIRS - 1, h)
                pe_values(pe, GROUPS - 1, PAIRS - 1, ahead=False)
                pe_out(pe, GROUPS - 1, PAIRS - 2)
                pe_out(pe, GROUPS - 1, PAIRS - 1)


FFN = 1024
BLOCK = 32
FP8_MAX = 448.0
FP8_EPS = 1e-30
FP8_LEAST = 2.0 ** -6
TO_EIGHTHS = 1.5 * 2.0 ** 20
EXPONENT = 0x7F800000


class Quantizer:

    def __init__(self, nc, ctx, tag, width):
        def sb(name, shape, dt=F32):
            return ctx.enter_context(nc.sbuf_tensor(f"{tag}_{name}", shape, dt))

        n = width // BLOCK
        self.n = n
        self.top, self.scale, self.inverse = sb("top", [P, n]), sb("scale", [P, n]), sb("inverse", [P, n])
        self.quot, self.magic = sb("quot", [P, width]), sb("magic", [P, width])
        self.scaled, self.quotients, self.rounded, self.restored, self.chain = (
            ctx.enter_context(nc.semaphore(f"{tag}_{s}")) for s in ("scaled", "quotients", "rounded", "restored", "chain"))

    def blocks(self, a):
        return a.rearrange("p (n w) -> p n w", w=BLOCK)

    def spread(self, a):
        return a.unsqueeze(2).broadcast_to([P, self.n, BLOCK])

    LINKS = 5

    def link(self, ve, at, k, instruction):
        instruction.then_inc(self.chain, 1)
        ve.wait_ge(self.chain, at * self.LINKS + k)

    def scales(self, ve, at, src):
        self.link(ve, at, 1, ve.tensor_reduce(self.top[:], self.blocks(src), X_AXIS, ALU.max, apply_absolute_value=True))
        if not (isinstance(at, int) and at == 0):
            ve.wait_ge(self.restored, at)
        self.link(ve, at, 2, ve.tensor_scalar(self.scale[:], self.top[:], 1.0 / FP8_MAX, FP8_EPS, ALU.mult, ALU.max))
        ve.reciprocal(self.inverse[:], self.scale[:]).then_inc(self.scaled, 1)

    def quotient(self, pool, at, src):
        pool.wait_ge(self.scaled, at + 1)
        pool.tensor_tensor(self.blocks(self.quot[:]), self.blocks(src), self.spread(self.inverse[:]),
                           ALU.mult).then_inc(self.quotients, 1)

    def round(self, ve, at):
        ve.wait_ge(self.quotients, at + 1)
        self.link(ve, at, 3, ve.tensor_single_scalar(self.magic[:].bitcast(I32), self.quot[:].bitcast(I32), EXPONENT,
                                                     ALU.bitwise_and))
        self.link(ve, at, 4, ve.tensor_scalar(self.magic[:], self.magic[:], FP8_LEAST, TO_EIGHTHS, ALU.max, ALU.mult))
        self.link(ve, at, 5, ve.tensor_tensor(self.quot[:], self.quot[:], self.magic[:], ALU.add))
        ve.tensor_tensor(self.quot[:], self.quot[:], self.magic[:], ALU.subtract).then_inc(self.rounded, 1)

    def restore(self, pool, at, out):
        pool.wait_ge(self.rounded, at + 1)
        pool.tensor_tensor(self.blocks(out), self.blocks(self.quot[:]), self.spread(self.scale[:]),
                           ALU.mult).then_inc(self.restored, 1)


class FfnWeights:
    def __init__(self, nc, ctx):
        def sb(name, shape):
            return ctx.enter_context(nc.sbuf_tensor(f"f_{name}", shape, F32R))

        self.gu_hi, self.gu_lo = sb("gu_hi", [P, 2, KT, FFN]), sb("gu_lo", [P, 2, KT, FFN])
        self.down_hi, self.down_lo = sb("down_hi", [P, FFN // P, D]), sb("down_lo", [P, FFN // P, D])


def phase_ffn_weights(nc, e, ins, w):
    CHUNKS = 6
    WIDTH = 1024
    with ExitStack() as ctx:
        raw = ctx.enter_context(nc.sbuf_tensor("fw_raw", [P, CHUNKS, WIDTH], F32))
        bank = [ctx.enter_context(nc.psum_tensor(f"fw_bank{i}", [P, GW], F32)) for i in range(4)]
        qz = Quantizer(nc, ctx, "fw", WIDTH)
        w_in, turned, hi_done, lo_done = (ctx.enter_context(nc.semaphore(f"fw_{n}")) for n in ("w_in", "turned", "hi_done", "lo_done"))

        def target(t, c, m):
            if c < 4:
                half = (c % 2) * GW
                return t[0][:, c // 2, m, half:half + GW].rearrange("p (a b) -> p a b", a=GROUP)
            return t[1][:, 4 * m:4 * m + 4, (c - 4) * P:(c - 3) * P]

        his, los = (w.gu_hi, w.down_hi), (w.gu_lo, w.down_lo)

        def halves(c):
            return [(m, bank[2 * (c % 2) + m][:].rearrange("p (a b) -> p a b", a=GROUP)) for m in range(2)]

        with nc.Block() as block:
            @block.sync
            def _(sp):
                for c in range(CHUNKS):
                    sp.dma_start(raw[:, c], ins["w_ffn"][:, c]).then_inc(w_in, 16)

            @block.gpsimd
            def _(pool):
                pool.wait_ge(w_in, 16 * CHUNKS)
                for c in range(CHUNKS):
                    qz.quotient(pool, c, raw[:, c])
                    qz.restore(pool, c, raw[:, c])

            @block.vector
            def _(ve):
                ve.wait_ge(w_in, 16 * CHUNKS)
                for c in range(CHUNKS + 1):
                    if c < CHUNKS:
                        qz.scales(ve, c, raw[:, c])
                    if c >= 1:
                        for m, ps in halves(c - 1):
                            ve.wait_ge(hi_done, 2 * (c - 1) + m + 1)
                            ve.tensor_tensor(target(los, c - 1, m), ps, target(his, c - 1, m).bitcast(F32),
                                             ALU.subtract).then_inc(lo_done, 1)
                    if c < CHUNKS:
                        qz.round(ve, c)

            @block.tensor
            def _(pe):
                for c in range(CHUNKS):
                    pe.wait_ge(qz.restored, c + 1)
                    if c >= 2:
                        pe.wait_ge(lo_done, 2 * (c - 1))
                    for m in range(2):
                        for a in range(GROUP):
                            at = (a * KT + m) * P if c < 4 else (4 * m + a) * P
                            mm = pe.transpose(bank[2 * (c % 2) + m][:, a * P:(a + 1) * P], raw[:, c, at:at + P], e.ident[:])
                    mm.then_inc(turned, 1)

            @block.scalar
            def _(act):
                for c in range(CHUNKS):
                    act.wait_ge(turned, c + 1)
                    for m, ps in halves(c):
                        act.activation(target(his, c, m), ps, ACT.Copy).then_inc(hi_done, 1)


def phase_ffn(nc, e, w, out):
    PASSES = BATCHES // 2
    with ExitStack() as ctx:
        def sb(name, shape, dt=F32):
            return ctx.enter_context(nc.sbuf_tensor(f"o_{name}", shape, dt))

        def sem(name):
            return ctx.enter_context(nc.semaphore(f"o_{name}"))

        st, mv = sb("st", [P, BATCHES, 6]), sb("mv", [P, BATCHES, 2])
        va, rs, nt, nu = (sb(n, [P, BATCHES]) for n in ("va", "rs", "nt", "nu"))
        xn = sb("xn", [P, 2, D])
        xT_hi, xT_lo = sb("xT_hi", [P, 2, KT, P], F32R), sb("xT_lo", [P, 2, KT, P], F32R)
        act_out = sb("act_out", [P, FFN])
        inner = sb("inner", [P, 2, FFN])
        iT_hi, iT_lo = sb("iT_hi", [P, FFN // P, P], F32R), sb("iT_lo", [P, FFN // P, P], F32R)
        bank = [ctx.enter_context(nc.psum_tensor(f"o_bank{i}", [P, GW], F32)) for i in range(8)]
        g_ps, u_ps, xT_ps, iT_ps, o_ps = bank[0:2], bank[2:4], bank[4], bank[5:7], bank[7]
        qx, qi = Quantizer(nc, ctx, "ox", D), Quantizer(nc, ctx, "oi", FFN)

        stats_chain, ready, x_turned, x_hid, x_lod = (sem(n) for n in ("stats", "ready", "x_turned", "x_hid", "x_lod"))
        up_done, silu_done, inner_done = sem("up_done"), sem("silu_done"), sem("inner_done")
        i_turned, i_hid, i_lod, down_done, added, stored = (sem(n) for n in ("i_turned", "i_hid", "i_lod", "down_done", "added", "stored"))

        def tile_of(x, t):
            return x[:, ds(t, 1)].rearrange("p a d -> p (a d)")

        def first_tile(t):
            return isinstance(t, int) and t == 0

        def ve_input_a(ve, t, par):
            if not (isinstance(t, int) and t < 2):
                ve.wait_ge(x_turned, t - 1)
            ve.tensor_scalar(xn[:, par], tile_of(e.X, t), mv[:, ds(t, 1), 0], rs[:, ds(t, 1)], ALU.subtract, ALU.mult)\
                .then_inc(ready, 1)
            ve.wait_ge(ready, t + 1)
            qx.scales(ve, t, xn[:, par])

        def ve_input_b(ve, t, par):
            qx.round(ve, t)

        def ve_input_c(ve, t, par):
            ve.wait_ge(x_hid, t + 1)
            ve.tensor_tensor(xT_lo[:, par].rearrange("p k c -> p (k c)"), xT_ps[:, 0:D],
                             xT_hi[:, par].rearrange("p k c -> p (k c)").bitcast(F32), ALU.subtract).then_inc(x_lod, 1)

        def pool_input_a(pool, t, par):
            qx.quotient(pool, t, xn[:, par])

        def pool_input_b(pool, t, par):
            qx.restore(pool, t, xn[:, par])

        def pe_input(pe, t, par):
            pe.wait_ge(qx.restored, t + 1)
            if not first_tile(t):
                pe.wait_ge(x_lod, t)
            for k in range(KT):
                mm = pe.transpose(xT_ps[:, k * P:(k + 1) * P], xn[:, par, k * P:(k + 1) * P], e.ident[:])
            mm.then_inc(x_turned, 1)

        def act_input(act, t, par):
            act.wait_ge(x_turned, t + 1)
            act.activation(xT_hi[:, par].rearrange("p k c -> p (k c)"), xT_ps[:, 0:D], ACT.Copy).then_inc(x_hid, 1)

        def pe_up(pe, t, par):
            pe.wait_ge(x_lod, t + 1)
            if not first_tile(t):
                pe.wait_ge(silu_done, 2 * t)
                pe.wait_ge(inner_done, 2 * t)
            for half in range(2):
                cols = slice(half * GW, (half + 1) * GW)
                for a, ps in ((0, g_ps[half]), (1, u_ps[half])):
                    for k in range(KT):
                        mm = parts(pe, ps[:], xT_hi[:, par, k], xT_lo[:, par, k], w.gu_hi[:, a, k, cols], w.gu_lo[:, a, k, cols],
                                   start=(k == 0), stop=(k == KT - 1))
                mm.then_inc(up_done, 1)

        def act_silu(act, t, par):
            for half in range(2):
                act.wait_ge(up_done, 2 * t + half + 1)
                if not first_tile(t):
                    act.wait_ge(inner_done, 2 * t - 1 + half)
                act.activation(act_out[:, half * GW:(half + 1) * GW], g_ps[half][:], ACT.Silu).then_inc(silu_done, 1)

        def ve_inner(ve, t, par):
            if not (isinstance(t, int) and t < 2):
                ve.wait_ge(i_turned, t - 1)
            for half in range(2):
                cols = slice(half * GW, (half + 1) * GW)
                ve.wait_ge(silu_done, 2 * t + half + 1)
                ve.tensor_tensor(inner[:, par, cols], u_ps[half][:], act_out[:, cols], ALU.mult).then_inc(inner_done, 1)
            ve.wait_ge(inner_done, 2 * t + 2)
            qi.scales(ve, t, inner[:, par])

        def pe_turn(pe, t, par):
            pe.wait_ge(qi.restored, t + 1)
            if not first_tile(t):
                pe.wait_ge(i_lod, 2 * t)
            for half in range(2):
                for a in range(GROUP):
                    i = half * GROUP + a
                    mm = pe.transpose(iT_ps[half][:, a * P:(a + 1) * P], inner[:, par, i * P:(i + 1) * P], e.ident[:])
            mm.then_inc(i_turned, 1)

        def act_turn(act, t):
            act.wait_ge(i_turned, t + 1)
            if not first_tile(t):
                act.wait_ge(down_done, t)
            for half in range(2):
                act.activation(iT_hi[:, 4 * half:4 * half + 4].rearrange("p a c -> p (a c)"), iT_ps[half][:], ACT.Copy).then_inc(i_hid, 1)

        def ve_turn(ve, t):
            for half in range(2):
                ve.wait_ge(i_hid, 2 * t + half + 1)
                ve.tensor_tensor(iT_lo[:, 4 * half:4 * half + 4].rearrange("p a c -> p (a c)"), iT_ps[half][:],
                                 iT_hi[:, 4 * half:4 * half + 4].rearrange("p a c -> p (a c)").bitcast(F32),
                                 ALU.subtract).then_inc(i_lod, 1)

        def pe_down(pe, t):
            if not first_tile(t):
                pe.wait_ge(added, t)
            for i in range(FFN // P):
                if i % GROUP == 0:
                    pe.wait_ge(i_lod, 2 * t + i // GROUP + 1)
                mm = parts(pe, o_ps[:, 0:D], iT_hi[:, i], iT_lo[:, i], w.down_hi[:, i], w.down_lo[:, i],
                           start=(i == 0), stop=(i == FFN // P - 1))
            mm.then_inc(down_done, 1)

        def ve_add(ve, t):
            ve.wait_ge(down_done, t + 1)
            x = tile_of(e.X, t)
            ve.tensor_tensor(x, o_ps[:, 0:D], x, ALU.add).then_inc(added, 1)

        def each(it, first, last):
            for par in range(2):
                t = 2 * it + par
                yield t, par, None if first else t - 2, None if last and par == 1 else t + 1

        def pe_pass(pe, it, first=False, last=False):
            for t, par, before, after in each(it, first, last):
                pe_up(pe, t, par)
                if before is not None:
                    pe_turn(pe, before, par)
                if after is not None:
                    pe_input(pe, after, 1 - par)
                if before is not None:
                    pe_down(pe, before)

        def act_pass(act, it, first=False, last=False):
            for t, par, before, after in each(it, first, last):
                act_silu(act, t, par)
                if before is not None:
                    act_turn(act, before)
                if after is not None:
                    act_input(act, after, 1 - par)

        def ve_pass(ve, it, first=False, last=False):
            for t, par, before, after in each(it, first, last):
                if after is not None:
                    ve_input_a(ve, after, 1 - par)
                    ve_input_b(ve, after, 1 - par)
                ve_inner(ve, t, par)
                if before is not None:
                    ve_turn(ve, before)
                if after is not None:
                    ve_input_c(ve, after, 1 - par)
                qi.round(ve, t)
                if before is not None:
                    ve_add(ve, before)

        def pool_pass(pool, it, first=False, last=False):
            for t, par, before, after in each(it, first, last):
                if after is not None:
                    pool_input_a(pool, after, 1 - par)
                    pool_input_b(pool, after, 1 - par)
                qi.quotient(pool, t, inner[:, par])
                qi.restore(pool, t, inner[:, par])

        def passes(engine, one_pass):
            one_pass(engine, 0, first=True)
            one_pass(engine, 1)
            with engine.Fori(2, PASSES - 1) as it:
                one_pass(engine, it)
            one_pass(engine, PASSES - 1, last=True)

        with nc.Block() as block:
            @block.vector
            def _(ve):
                links = [0]

                def link(instruction):
                    links[0] += 1
                    instruction.then_inc(stats_chain, 1)
                    ve.wait_ge(stats_chain, links[0])

                for t in range(BATCHES):
                    last = ve.bn_stats(st[:, t], e.X[:, t])
                link(last)
                for t in range(BATCHES):
                    last = ve.bn_aggr(mv[:, t], st[:, t])
                link(last)
                link(ve.tensor_scalar(va[:], mv[:, :, 1], LN_EPS, None, ALU.add))
                rsqrt_steps(ve, link, va[:], rs[:], nt[:], nu[:])
                ve_input_a(ve, 0, 0)
                ve_input_b(ve, 0, 0)
                ve_input_c(ve, 0, 0)
                passes(ve, ve_pass)
                for t in range(BATCHES - 2, BATCHES):
                    ve_turn(ve, t)
                    ve_add(ve, t)

            @block.gpsimd
            def _(pool):
                pool_input_a(pool, 0, 0)
                pool_input_b(pool, 0, 0)
                passes(pool, pool_pass)

            @block.scalar
            def _(act):
                act_input(act, 0, 0)
                passes(act, act_pass)
                for t in range(BATCHES - 2, BATCHES):
                    act_turn(act, t)

            @block.tensor
            def _(pe):
                pe_input(pe, 0, 0)
                passes(pe, pe_pass)
                for t in range(BATCHES - 2, BATCHES):
                    pe_turn(pe, t, t % 2)
                    pe_down(pe, t)

            @block.sync
            def _(sp):
                with sp.Fori(0, BATCHES) as t:
                    sp.wait_ge(added, t + 1)
                    sp.dma_start(out[ds(t, 1)].rearrange("a p d -> p (a d)"), tile_of(e.X, t)).then_inc(stored, 16)
                sp.wait_ge(stored, 16 * BATCHES)


def attention_state(nc, ctx):
    w = Env()

    def sb(name, shape, dt=F32):
        return ctx.enter_context(nc.sbuf_tensor(name, shape, dt))

    w.hT_hi = sb("hT_hi", [P, KT, BATCHES * P], F32R)
    w.hT_lo = sb("hT_lo", [P, KT, BATCHES * P], F32R)
    w.raw = sb("w_raw", [P, 2, 4, KT, D])
    w.hi = sb("w_hi", [P, 2, 4, KT, D], F32R)
    w.lo = sb("w_lo", [P, 2, 4, KT, D], F32R)
    w.causal32 = sb("causal32", [P, P])
    w.causal = sb("causal", [P, P], F32R)
    w.ln1 = sb("ln1", [P, KT])
    return w


def clear_semaphores(nc):
    used = sorted(nc.released_uncleared_semaphores)
    with nc.Block() as block:
        @block.gpsimd
        def _(pool):
            pool.sem_clear(range(used[0], used[-1] + 1))


def build_program(nc, ins, out):
    with ExitStack() as ctx:
        e = constants_and_state(nc, ctx, ins)
        cy = ctx.enter_context(ExitStack())
        e.Y = cy.enter_context(nc.sbuf_tensor("Y", [P, BATCHES, D], F32))
        with ExitStack() as c1:
            w = attention_state(nc, c1)
            phase_a(nc, e, ins, w)
            phase_attention(nc, e, ins, w)
        phase_moe(nc, e, ins)
        cy.close()
        with ExitStack() as c2:
            z = LatentState(nc, c2)
            phase_latent_keys(nc, e, ins, z)
            qc_hi = c2.enter_context(nc.sbuf_tensor("qc_hi", [QC, BATCHES * P], F32R))
            qc_lo = c2.enter_context(nc.sbuf_tensor("qc_lo", [QC, BATCHES * P], F32R))
            phase_latent_queries(nc, e, ins, z, qc_hi, qc_lo)
            phase_latent_attention(nc, e, z, qc_hi, qc_lo)
        with ExitStack() as c3:
            wf = FfnWeights(nc, c3)
            clear_semaphores(nc)
            phase_ffn_weights(nc, e, ins, wf)
            phase_ffn(nc, e, wf, out)


def layouts(i):
    import numpy as np

    def by_pair(m):
        return m.reshape(KT, P, PAIRS, 2 * HD).transpose(1, 2, 0, 3)

    fill = np.zeros((TILES * P - EXPERTS * EI - SI, D), np.float32)

    def rows(experts, shared):
        return np.concatenate([experts.reshape(EXPERTS * EI, D), shared, fill]).reshape(TILES, P, D)

    up = [rows(i["L0_ffn_eg_w"], i["L0_ffn_sg_w"]), rows(i["L0_ffn_eu_w"], i["L0_ffn_su_w"])]
    up = [m.reshape(TILES, P, KT, P).transpose(3, 0, 2, 1).reshape(P, TILES, KT * P) for m in up]
    down = rows(i["L0_ffn_ed_w"].transpose(0, 2, 1), i["L0_ffn_sd_w"].T).transpose(1, 0, 2)
    owner = np.minimum(np.arange(TILES * P) // EI, EXPERTS)
    sel = (np.arange(P)[:, None] == owner[None]).astype(np.float32).reshape(P, TILES, P)
    w_moe = np.concatenate([*up, down, sel], axis=2)
    wo = i["L0_ffn_wo"].reshape(PAIRS, 2, P, D).transpose(2, 0, 1, 3)
    inv = (1.0 / np.float32(10000.0) ** (np.arange(HALF, dtype=np.float32) / np.float32(HALF))).astype(np.float32)
    ang = (inv[:, None] * np.arange(P, dtype=np.float32)[None]).astype(np.float32)
    cos = np.tile(np.cos(ang), (2 * P // ROPE, 1))
    sin = np.tile(np.concatenate([-np.sin(ang), np.sin(ang)]), (P // ROPE, 1))
    one = np.ones((KVC, P), np.float32)
    scale = np.float32(1.0) / np.sqrt(np.float32(HD + ROPE))
    key = np.tile(np.arange(P, dtype=np.float32), (P, 1))
    tab = np.stack([scale * np.concatenate([one, cos[KVC:]]), scale * np.concatenate([cos[:ROPE], one]), scale * sin,
                    cos, sin, key], axis=1).astype(np.float32)

    def swap(m):
        return np.concatenate([m[..., HALF:], m[..., :HALF]], axis=-1)

    qr = i["L1_xattn_W_qr"].reshape(QC, HEADS, ROPE)
    kr = i["L1_xattn_W_kr"]
    kvc = i["L1_xattn_W_kvc"].reshape(KT, P, KVC).transpose(1, 0, 2)
    gate, up = (i[f"L1_ffn_{n}_w"].reshape(2, GROUP, P, D).transpose(2, 0, 1, 3).reshape(P, 2, GROUP * D)
                for n in ("gate", "up"))
    down = i["L1_ffn_down_w"].reshape(KT, P, FFN).transpose(1, 0, 2)
    return {
        "w_ffn": np.concatenate([gate, up, down], axis=1),
        "uqT": i["L1_xattn_W_uq"].reshape(QC, HEADS, HD).transpose(2, 1, 0),
        "ukT": i["L1_xattn_W_uk"].reshape(KVC, HEADS, HD).transpose(2, 1, 0),
        "uvT": i["L1_xattn_W_uv"].reshape(KVC, HEADS, HD).transpose(2, 1, 0),
        "w_o2": i["L1_xattn_W_o"].reshape(HEADS, HD, D).transpose(1, 0, 2),
        "wkvc": np.concatenate([kvc, kvc], axis=2),
        "wkr": np.stack([np.concatenate([kr, kr], axis=1), np.concatenate([swap(kr), swap(kr)], axis=1)], axis=1),
        "qr": qr,
        "qrb": np.concatenate([swap(qr[:, 1::2]), swap(qr[:, 0::2])], axis=2),
        "wdq": i["L1_xattn_W_dq"].reshape(KT, P, QC).transpose(1, 0, 2),
        "seg": i["itok_BxS_0_1023"].T,
        "tab": tab,
        "ln2": i["L0_ffn_ln2_w"].reshape(KT, P).T,
        "gate": i["L0_ffn_gate_w"].T.reshape(KT, P, EXPERTS).transpose(1, 0, 2),
        "w_moe": w_moe,
        "x": i["x"],
        "ctx": i["ctx_2048"],
        "ctxT": i["ctx_2048"].reshape(-1, D).T,
        "mask": i["mask_BxS2_bk0"],
        "ln1": i["L0_ffn_ln1_w"].reshape(KT, P).T,
        "w_attn": np.stack([by_pair(i["L0_ffn_wq"]), by_pair(i["L0_ffn_wk"]), by_pair(i["L0_ffn_wv"]), wo], axis=2),
    }


def kernel(**inputs):
    import numpy as _np
    import concourse.bacc as _bacc
    from concourse import mybir as _mybir
    from concourse.bass_utils import run_bass_kernel_spmd as _run

    nc = _bacc.Bacc("TRN2", target_bir_lowering=False, num_devices=1)
    arrays = {"in_" + k: _np.ascontiguousarray(v) for k, v in layouts({k: _np.asarray(v) for k, v in inputs.items()}).items()}
    ins = {k[3:]: nc.dram_tensor(k, v.shape, _mybir.dt.from_np(v.dtype), kind="ExternalInput").ap()
           for k, v in arrays.items()}
    out = nc.dram_tensor("out_x", (BATCHES, P, D), F32, kind="ExternalOutput").ap()
    build_program(nc, ins, out)
    r = _run(nc, [arrays], core_ids=[0])
    return r.results[0]["out_x"]
```

```python
from contextlib import ExitStack

import concourse.bass as bass
from concourse import mybir

F32 = mybir.dt.float32
F32R = mybir.dt.float32r
I32 = mybir.dt.int32
U8 = mybir.dt.uint8
ALU = mybir.AluOpType
ACT = mybir.ActivationFunctionType
X_AXIS = mybir.AxisListType.X
ds = bass.ds

P = 128
BATCHES = 16
D = 256
KT = D // P
GROUP = 4
GROUPS = BATCHES // GROUP
GW = GROUP * P

HEADS = 16
HD = 128
PAIRS = HEADS // 2
LN_EPS = 1e-5
RMS_EPS = 1e-6


class Env:
    pass


def constants_and_state(nc, ctx, ins):
    e = Env()

    def sb(name, shape, dt=F32):
        return ctx.enter_context(nc.sbuf_tensor(name, shape, dt))

    e.X = sb("X", [P, BATCHES, D])
    e.ident = sb("ident", [P, P])
    e.ident_r = sb("ident_r", [P, P], F32R)
    e.one = sb("one", [P, 1])
    return e


def copy_pool(pool, e, out, src):
    return pool.tensor_tensor(out, src, e.one[:, 0:1].broadcast_to(list(src.shape)), ALU.mult)


def rsqrt_steps(ve, link, var, y, t, u, last=None):
    link(ve.tensor_scalar(y.bitcast(I32), var.bitcast(I32), -0.5, 1597463007.0, ALU.mult, ALU.add))
    for n in range(3):
        link(ve.scalar_tensor_tensor(out=t, in0=y, scalar=-0.5, in1=y, op0=ALU.mult, op1=ALU.mult))
        link(ve.tensor_tensor(u, t, var, ALU.mult))
        (last if last and n == 2 else link)(
            ve.scalar_tensor_tensor(out=y, in0=u, scalar=1.5, in1=y, op0=ALU.add, op1=ALU.mult))


def over_groups(a):
    return a.unsqueeze(2).broadcast_to([P, GROUP, P])


def phase_a(nc, e, ins, w, mw, fw):
    HALF_TILES = BATCHES // 2
    with ExitStack() as ctx:
        def sb(name, shape, dt=F32):
            return ctx.enter_context(nc.sbuf_tensor(f"a_{name}", shape, dt))

        def sem(name):
            return ctx.enter_context(nc.semaphore(f"a_{name}"))

        ctxn = sb("ctxn", [P, BATCHES, D])
        later = fw.raw[:].rearrange("p c w -> p (c w)")
        ctxT = later[:, 0:KT * BATCHES * P].rearrange("p (k t) -> p k t", k=KT)
        mask8 = sb("mask8", [P, BATCHES * P], U8)
        mbias = mw.hi[:].rearrange("p j c -> p (j c)")[:, 0:BATCHES * P]
        valid = sb("valid", [P, BATCHES])
        st, mv = sb("st", [P, BATCHES, 6]), sb("mv", [P, BATCHES, 2])
        va, rs, rr, nt, nu, nmax, sums, rec = (
            sb(n, [P, BATCHES]) for n in ("va", "rs", "rr", "nt", "nu", "nmax", "sums", "rec"))
        xn = sb("xn", [P, 2, GROUP, D])
        lnT = later[:, KT * BATCHES * P:KT * (BATCHES * P + 2 * GW)].rearrange("p (a k c) -> p a k c", a=2, k=KT)
        prob = sb("prob", [P, 2, GROUP, P])
        probT = sb("probT", [P, 2, GW])
        bank = [ctx.enter_context(nc.psum_tensor(f"a_bank{i}", [P, GW], F32)) for i in range(8)]
        xT_ps, sc_ps, pT_ps, av_ps = bank[0:2], bank[2:4], bank[6:8], bank[4:6]
        hT_ps = (bank[0:2], bank[2:4])

        x_in = [sem(f"x_in{g}") for g in range(GROUPS)]
        ctx_in, ctxT_in, small_in, w_in = sem("ctx_in"), sem("ctxT_in"), sem("small_in"), sem("w_in")
        zeroed, ident_done, consts, bias_done, w_hi = (sem(n) for n in ("zeroed", "ident", "consts", "bias", "w_hi"))
        chain, valid_done, ln_ready, ln_out, x_turned, lnT_out = (
            sem(n) for n in ("chain", "valid_done", "ln_ready", "ln_out", "x_turned", "lnT_out"))
        scores_done, max_done, exp_done, pT_done, pT_out, av_done, x_added = (
            sem(n) for n in ("scores", "max", "exp", "pT_done", "pT_out", "av", "x_added"))
        y_ready, rms_ready, h_in, h_turned, h_hi, h_lo = (
            sem(n) for n in ("y_ready", "rms_ready", "h_in", "h_turned", "h_hi", "h_lo"))

        with nc.Block() as block:
            @block.sync
            def _(sp):
                for g in range(GROUPS):
                    tiles = slice(g * GROUP, (g + 1) * GROUP)
                    sp.dma_start(e.X[:, tiles], ins["x"][tiles].rearrange("b p d -> p b d")).then_inc(x_in[g], 16)
                sp.dma_start(ctxn[:], ins["ctx"].rearrange("b p d -> p b d")).then_inc(ctx_in, 16)
                sp.dma_start(w.raw[:], ins["w_attn"][:, 0:2]).then_inc(w_in, 16)

            @block.gpsimd
            def _(pool):
                pool.memset(e.one[:], 1.0)
                pool.memset(e.ident[:], 0.0).then_inc(zeroed, 1)
                pool.wait_ge(zeroed, 1)
                pool.affine_select(out=e.ident[:], in_=e.ident[:], compare_op=ALU.not_equal, fill=1.0, base=0,
                                   pattern=[[-1, P]], channel_multiplier=1).then_inc(ident_done, 1)
                pool.memset(w.causal32[:], 0.0).then_inc(zeroed, 1)
                pool.wait_ge(zeroed, 2)
                pool.affine_select(out=w.causal32[:], in_=w.causal32[:], compare_op=ALU.is_ge, fill=-1.0e9, base=0,
                                   pattern=[[-1, P]], channel_multiplier=1).then_inc(zeroed, 1)
                pool.wait_ge(zeroed, 3)
                pool.tensor_scalar(w.causal[:], w.causal32[:], 1.0, None, ALU.mult)
                pool.wait_ge(ident_done, 1)
                pool.tensor_scalar(e.ident_r[:], e.ident[:], 1.0, None, ALU.mult).then_inc(consts, 1)
                pool.wait_ge(small_in, 32)
                pool.tensor_scalar(mbias, mask8[:], 1.0e30, -1.0e30, ALU.mult, ALU.add).then_inc(bias_done, 1)
                pool.wait_ge(w_in, 16)
                for n in range(2):
                    pool.tensor_scalar(w.hi[:, n], w.raw[:, n], 1.0, None, ALU.mult).then_inc(w_hi, 1)
                for n in range(2):
                    pool.wait_ge(w_hi, n + 1)
                    pool.tensor_tensor(w.lo[:, n], w.raw[:, n], w.hi[:, n].bitcast(F32), ALU.subtract)

            def act_lnT(act, g):
                act.wait_ge(x_turned, g + 1)
                if g >= 2:
                    act.wait_ge(scores_done, g - 1)
                for k in range(KT):
                    act.activation(lnT[:, g % 2, k], xT_ps[k][:], ACT.Copy, scale=float(D) ** -0.5).then_inc(lnT_out, 1)

            def act_exp(act, g):
                act.wait_ge(max_done, g + 1)
                if g >= 2:
                    act.wait_ge(pT_done, g - 1)
                for b in range(GROUP):
                    t = g * GROUP + b
                    act.activation(prob[:, g % 2, b], sc_ps[g % 2][:, b * P:(b + 1) * P], ACT.Exp, bias=nmax[:, t:t + 1],
                                   accum_out=sums[:, t:t + 1]).then_inc(exp_done, 1)

            def act_pT(act, g):
                act.wait_ge(pT_done, g + 1)
                if g >= 2:
                    act.wait_ge(av_done, g - 1)
                act.activation(probT[:, g % 2], pT_ps[g % 2][:], ACT.Copy).then_inc(pT_out, 1)

            def act_h(act, g):
                act.wait_ge(y_ready, g // 2 + 1)
                act.wait_ge(rms_ready, g // 2 + 1)
                if g < 2:
                    act.wait_ge(x_turned, GROUPS - 1 + g)
                else:
                    act.wait_ge(h_turned, g - 1)
                for b in range(GROUP):
                    t = g * GROUP + b
                    last = act.activation(xn[:, g % 2, b], e.Y[:, t], ACT.Copy, scale=rr[:, t:t + 1])
                last.then_inc(h_in, 1)

            @block.scalar
            def _(act):
                act.dma_start(mask8[:], ins["mask"].rearrange("b m -> (b m)").partition_broadcast(P)).then_inc(small_in, 16)
                act.dma_start(w.ln1[:], ins["ln1"]).then_inc(small_in, 16)
                act.dma_start(ctxT, ins["ctxT"].rearrange("(k p) t -> p k t", p=P)).then_inc(ctxT_in, 16)
                for i in range(GROUPS + 2):
                    for step, g in ((act_lnT, i), (act_exp, i - 1), (act_pT, i - 2)):
                        if 0 <= g < GROUPS:
                            step(act, g)
                act.wait_ge(small_in, 32)
                act_h(act, 0)
                for g in range(GROUPS):
                    if g + 1 < GROUPS:
                        act_h(act, g + 1)
                    act.wait_ge(h_turned, g + 1)
                    for k in range(KT):
                        act.activation(w.hT_hi[:, k, g * GW:(g + 1) * GW], hT_ps[g % 2][k][:], ACT.Copy,
                                       scale=w.ln1[:, k:k + 1]).then_inc(h_hi, 1)

            def pe_turn_x(pe, g):
                pe.wait_ge(ln_out, g + 1)
                if g >= 1:
                    pe.wait_ge(lnT_out, KT * g)
                for k in range(KT):
                    for b in range(GROUP):
                        mm = pe.transpose(xT_ps[k][:, b * P:(b + 1) * P], xn[:, g % 2, b, k * P:(k + 1) * P], e.ident[:])
                mm.then_inc(x_turned, 1)

            def pe_scores(pe, g):
                pe.wait_ge(lnT_out, KT * g + KT)
                if g == 0:
                    pe.wait_ge(ctxT_in, 16)
                    pe.wait_ge(bias_done, 1)
                if g >= 2:
                    pe.wait_ge(exp_done, GROUP * (g - 1))
                for b in range(GROUP):
                    t = g * GROUP + b
                    for k in range(KT):
                        pe.matmul(sc_ps[g % 2][:, b * P:(b + 1) * P], lnT[:, g % 2, k, b * P:(b + 1) * P],
                                  ctxT[:, k, t * P:(t + 1) * P], start=(b == 0 and k == 0), stop=False,
                                  skip_group_check=True)
                pe.matmul(sc_ps[g % 2][:], e.ident_r[:], mbias[:, g * GW:(g + 1) * GW], start=False, stop=True,
                          skip_group_check=True).then_inc(scores_done, 1)

            def pe_turn_p(pe, g):
                pe.wait_ge(exp_done, GROUP * g + GROUP)
                if g >= 2:
                    pe.wait_ge(pT_out, g - 1)
                for b in range(GROUP):
                    mm = pe.transpose(pT_ps[g % 2][:, b * P:(b + 1) * P], prob[:, g % 2, b], e.ident[:])
                mm.then_inc(pT_done, 1)

            def pe_av(pe, g):
                pe.wait_ge(pT_out, g + 1)
                if g == 0:
                    pe.wait_ge(ctx_in, 16)
                if g >= 1:
                    pe.wait_ge(x_added, g)
                for b in range(GROUP):
                    mm = pe.matmul(av_ps[b // 2][:, (b % 2) * D:(b % 2 + 1) * D], probT[:, g % 2, b * P:(b + 1) * P],
                                   ctxn[:, g * GROUP + b], start=(b % 2 == 0), stop=True, skip_group_check=True)
                mm.then_inc(av_done, 1)

            @block.tensor
            def _(pe):
                pe.wait_ge(ident_done, 1)
                pe.wait_ge(consts, 1)
                for i in range(GROUPS + 3):
                    for step, g in ((pe_turn_x, i), (pe_scores, i - 1), (pe_turn_p, i - 2), (pe_av, i - 3)):
                        if 0 <= g < GROUPS:
                            step(pe, g)
                for g in range(GROUPS):
                    pe.wait_ge(h_in, g + 1)
                    if g >= 2:
                        pe.wait_ge(h_lo, KT * (g - 1))
                    for k in range(KT):
                        for b in range(GROUP):
                            mm = pe.transpose(hT_ps[g % 2][k][:, b * P:(b + 1) * P], xn[:, g % 2, b, k * P:(k + 1) * P],
                                              e.ident[:])
                    mm.then_inc(h_turned, 1)

            @block.vector
            def _(ve):
                links = [0]

                def link(instruction):
                    links[0] += 1
                    instruction.then_inc(chain, 1)
                    ve.wait_ge(chain, links[0])

                def statistics(half, last):
                    tiles = range(half * HALF_TILES, (half + 1) * HALF_TILES)
                    cols = slice(half * HALF_TILES, (half + 1) * HALF_TILES)
                    for t in tiles:
                        if last is not None and t % GROUP == 0:
                            ve.wait_ge(x_in[t // GROUP], 16)
                        done = ve.bn_stats(st[:, t], e.X[:, t])
                    link(done)
                    for t in tiles:
                        done = ve.bn_aggr(mv[:, t], st[:, t])
                    link(done)
                    link(ve.tensor_scalar(va[:, cols], mv[:, cols, 1], LN_EPS, None, ALU.add))
                    rsqrt_steps(ve, link, va[:, cols], rs[:, cols], nt[:, cols], nu[:, cols], last)

                def finish(g):
                    cols = slice(g * GROUP, (g + 1) * GROUP)
                    ve.wait_ge(exp_done, GROUP * g + GROUP)
                    link(ve.reciprocal(rec[:, cols], sums[:, cols]))
                    link(ve.tensor_tensor(rec[:, cols], rec[:, cols], valid[:, cols], ALU.mult))
                    ve.wait_ge(av_done, g + 1)
                    for b in range(GROUP):
                        t = g * GROUP + b
                        done = ve.scalar_tensor_tensor(out=e.X[:, t], in0=av_ps[b // 2][:, (b % 2) * D:(b % 2 + 1) * D],
                                                       scalar=rec[:, t:t + 1], in1=e.X[:, t], op0=ALU.mult, op1=ALU.add)
                    done.then_inc(x_added, 1)

                def normalise(half):
                    cols = slice(half * HALF_TILES, (half + 1) * HALF_TILES)
                    ve.wait_ge(x_added, 2 * half + 2)
                    statistics(half, None)
                    for t in range(half * HALF_TILES, (half + 1) * HALF_TILES):
                        done = ve.tensor_scalar(e.Y[:, t], e.X[:, t], mv[:, t, 0:1], rs[:, t:t + 1], ALU.subtract, ALU.mult)
                    done.then_inc(y_ready, 1)
                    link(ve.tensor_tensor(nt[:, cols], rs[:, cols], rs[:, cols], ALU.mult))
                    link(ve.tensor_tensor(nt[:, cols], nt[:, cols], mv[:, cols, 1], ALU.mult))
                    link(ve.tensor_scalar(va[:, cols], nt[:, cols], RMS_EPS, None, ALU.add))
                    rsqrt_steps(ve, link, va[:, cols], rr[:, cols], nt[:, cols], nu[:, cols],
                                lambda instruction: instruction.then_inc(rms_ready, 1))

                for half in range(2):
                    statistics(half, lambda instruction: instruction.then_inc(ln_ready, 1))
                    ve.wait_ge(ln_ready, half + 1)
                    for g in (2 * half, 2 * half + 1):
                        if g >= 2:
                            ve.wait_ge(x_turned, g - 1)
                        for b in range(GROUP):
                            t = g * GROUP + b
                            done = ve.tensor_scalar(xn[:, g % 2, b], e.X[:, t], mv[:, t, 0:1], rs[:, t:t + 1],
                                                    ALU.subtract, ALU.mult)
                        done.then_inc(ln_out, 1)
                ve.wait_ge(small_in, 32)
                ve.tensor_reduce(valid[:], mask8[:].rearrange("p (b m) -> p b m", b=BATCHES), X_AXIS, ALU.max).then_inc(valid_done, 1)
                ve.wait_ge(valid_done, 1)
                for g in range(GROUPS + 1):
                    if g < GROUPS:
                        ve.wait_ge(scores_done, g + 1)
                        ve.tensor_reduce(nmax[:, g * GROUP:(g + 1) * GROUP], sc_ps[g % 2][:].rearrange("p (b m) -> p b m", b=GROUP),
                                         X_AXIS, ALU.max, negate=True).then_inc(max_done, 1)
                    if g >= 1:
                        finish(g - 1)
                    if g == 2:
                        normalise(0)
                normalise(1)
                for g in range(GROUPS):
                    for k in range(KT):
                        ve.wait_ge(h_hi, KT * g + k + 1)
                        hi = w.hT_hi[:, k, g * GW:(g + 1) * GW]
                        ve.scalar_tensor_tensor(out=w.hT_lo[:, k, g * GW:(g + 1) * GW], in0=hT_ps[g % 2][k][:],
                                                scalar=w.ln1[:, k:k + 1], in1=hi.bitcast(F32), op0=ALU.mult,
                                                op1=ALU.subtract).then_inc(h_lo, 1)


def phase_attention(nc, e, ins, w, mw, fw):
    STEPS = 2 * GROUPS
    PASSES = PAIRS // 2
    UNITS = 6
    RING = 4
    with ExitStack() as ctx:
        def sb(name, shape, dt=F32):
            return ctx.enter_context(nc.sbuf_tensor(name, shape, dt))

        def sem(name):
            return ctx.enter_context(nc.semaphore(name))

        qk = sb("qk", [P, 4, GW])
        v = sb("v", [P, 2, GROUP, 2 * HD])
        prob = sb("b_prob", [P, 2, GROUP, P])
        b_probT = sb("b_probT", [P, 2, GW])
        ao_hi = sb("ao_hi", [P, 2, GW], F32R)
        ao_lo = sb("ao_lo", [P, 2, GW], F32R)
        nmax = sb("b_nmax", [P, 2, 2, GROUP])
        sums = sb("b_sums", [P, 2, 2, GROUP])
        rec = sb("b_rec", [P, 2, 2, GROUP])
        ring = [ctx.enter_context(nc.psum_tensor(f"b_ring{i}", [P, GW], F32)) for i in range(RING)]
        sc_ps = [ctx.enter_context(nc.psum_tensor(f"b_sc{i}", [P, GW], F32)) for i in range(2)]
        wo_ps = [ctx.enter_context(nc.psum_tensor(f"b_wo{i}", [P, GW], F32)) for i in range(2)]

        proj_done, qk_out, v_out = sem("proj_done"), sem("qk_out"), sem("v_out")
        scores_done, max_done, exp_done = sem("scores_done"), sem("max_done"), sem("exp_done")
        rec_done, norm_done = sem("rec_done"), sem("norm_done")
        probT_done, probT_out = sem("probT_done"), sem("probT_out")
        pv_done, ao_hid, ao_lod = sem("pv_done"), sem("ao_hid"), sem("ao_lod")
        wo_done, y_added = sem("wo_done"), sem("y_added")
        raw_in = [sem("raw_in0"), sem("raw_in1")]
        qkv_hi_split, qkv_split = sem("qkv_hi_split"), sem("qkv_split")
        wo_hi_split, wo_split = sem("wo_hi_split"), sem("wo_split")
        moe_raw_in, moe_hi = sem("moe_raw_in"), sem("moe_hi")
        moe_raw = fw.raw[:].rearrange("p c w -> p (c w)")[:, 0:SLOTS * WCOLS].rearrange("p (j c) -> p j c", j=SLOTS)
        moe_split = sem("moe_split")
        qz = Quantizer(nc, ctx, "fw", fw.WIDTH, w.raw[:, 0].rearrange("p a k c -> p (a k c)"))

        def pe_project(pe, it, j, first=False):
            S = it * STEPS + j
            g, n = (j // 2) % GROUPS, j % 2
            if j in (1, STEPS) and not (isinstance(it, int) and _pair(it, j) < 2):
                pe.wait_ge(qkv_split, _pair(it, j) - 1)
            for u in range(UNITS):
                out = ring[u % RING]
                if not first:
                    if u in (0, 1):
                        pe.wait_ge(v_out, 2 * (S - 1) + u + 1)
                    elif u in (2, 3):
                        if isinstance(it, int) and S < 2:
                            pe.wait_ge(qk_out, 4 * (S - 1) + u + 1)
                        else:
                            pe.wait_ge(ao_lod, 2 * (S - 2) + (u - 2) + 1)
                if u in (4, 5):
                    pe.wait_ge(qk_out, 4 * S + (u - 4) + 1)
                if u < 4:
                    c = (u // 2) * HD
                    for k in range(KT):
                        h_hi, h_lo = w.hT_hi[:, k, g * GW:(g + 1) * GW], w.hT_lo[:, k, g * GW:(g + 1) * GW]
                        mm = parts(pe, out[:], w.hi[:, n, u % 2, k, c:c + HD], w.lo[:, n, u % 2, k, c:c + HD],
                                   h_hi, h_lo, start=(k == 0), stop=(k == KT - 1))
                else:
                    for t in range(2):
                        tok = g * GW + ((u - 4) * 2 + t) * P
                        for k in range(KT):
                            mm = parts(pe, out[:, t * 2 * HD:(t + 1) * 2 * HD], w.hT_hi[:, k, tok:tok + P],
                                       w.hT_lo[:, k, tok:tok + P], w.hi[:, n, 2, k, :], w.lo[:, n, 2, k, :],
                                       start=(t == 0 and k == 0), stop=(k == KT - 1))
                mm.then_inc(proj_done, 1)

        def _pair(it, j):
            return 2 * it + 2 * (j // STEPS) + j % 2

        def pe_scores(pe, it, j):
            S = it * STEPS + j
            for h in range(2):
                if not (isinstance(it, int) and S < 1):
                    pe.wait_ge(probT_out, 2 * (S - 1) + h + 1)
                pe.wait_ge(qk_out, 4 * S + 2 * h + 2)
                for b in range(GROUP):
                    c = slice(b * P, (b + 1) * P)
                    pe.matmul(sc_ps[h][:, c], qk[:, 2 * h, c], qk[:, 2 * h + 1, c], start=(b == 0), stop=False,
                              skip_group_check=True)
                mm = pe.matmul(sc_ps[h][:].rearrange("p (b m) -> p b m", b=GROUP), e.ident_r[:],
                               w.causal[:].unsqueeze(1).broadcast_to([P, GROUP, P]), start=False, stop=True,
                               skip_group_check=True)
                mm.then_inc(scores_done, 1)

        def pe_transpose(pe, it, j):
            S = it * STEPS + j
            for h in range(2):
                pe.wait_ge(norm_done, 2 * S + h + 1)
                for b in range(GROUP):
                    mm = pe.transpose(sc_ps[h][:, b * P:(b + 1) * P], prob[:, h, b], e.ident[:])
                mm.then_inc(probT_done, 1)

        def pe_wo(pe, it, j):
            S = it * STEPS + j
            n = j % 2
            pe.wait_ge(ao_lod, 2 * S + 2)
            if j < 2 and not (isinstance(it, int) and it == 0):
                pe.wait_ge(wo_split, 2 * it + n - 1)
            if n == 0 and not (isinstance(it, int) and S < 2):
                pe.wait_ge(y_added, S)
            for b in range(GROUP):
                for h in range(2):
                    mm = parts(pe, wo_ps[b // 2][:, (b % 2) * D:(b % 2 + 1) * D], ao_hi[:, h, b * P:(b + 1) * P],
                               ao_lo[:, h, b * P:(b + 1) * P], w.hi[:, n, 3, h, :], w.lo[:, n, 3, h, :],
                               start=(n == 0 and h == 0 and b % 2 == 0), stop=(n == 1 and h == 1))
            mm.then_inc(wo_done, 1)

        def pe_pv(pe, it, j, last=False):
            S = it * STEPS + j
            pe.wait_ge(v_out, 2 * S + 2)
            for h in range(2):
                pe.wait_ge(probT_out, 2 * S + h + 1)
                out = ring[2 + h]
                if not last:
                    pe.wait_ge(qk_out, 4 * (S + 1) + 2 + h + 1)
                elif last:
                    pe.wait_ge(ao_lod, 2 * (S - 1) + h + 1)
                for b in range(GROUP):
                    c = slice(b * P, (b + 1) * P)
                    mm = pe.matmul(out[:, c], v[:, j % 2, b, h * HD:(h + 1) * HD], b_probT[:, h, c], start=(b == 0),
                                   stop=True, skip_group_check=True)
                mm.then_inc(pv_done, 1)

        def pe_pass(pe, it, first=False, last=False):
            for j in range(STEPS):
                end = last and j == STEPS - 1
                pe_scores(pe, it, j)
                if not end:
                    pe_project(pe, it, j + 1)
                pe_transpose(pe, it, j)
                if j > 0:
                    pe_wo(pe, it, j - 1)
                elif not first:
                    pe_wo(pe, it - 1, STEPS - 1)
                pe_pv(pe, it, j, last=end)

        SCALE = float(HD) ** -0.5

        def act_project(act, it, j):
            S = it * STEPS + j
            for u in range(4):
                act.wait_ge(proj_done, UNITS * S + u + 1)
                act.activation(qk[:, u], ring[u][:], ACT.Copy, scale=SCALE if u % 2 == 0 else 1.0).then_inc(qk_out, 1)

        def act_pass(act, it, last=False):
            for j in range(STEPS):
                S = it * STEPS + j
                for h in range(2):
                    act.wait_ge(max_done, 2 * S + h + 1)
                    for b in range(GROUP):
                        act.activation(prob[:, h, b], sc_ps[h][:, b * P:(b + 1) * P], ACT.Exp,
                                       bias=nmax[:, j % 2, h, b:b + 1],
                                       accum_out=sums[:, j % 2, h, b:b + 1]).then_inc(exp_done, 1)
                if not (last and j == STEPS - 1):
                    act_project(act, it, j + 1)
                for h in range(2):
                    act.wait_ge(probT_done, 2 * S + h + 1)
                    act.activation(b_probT[:, h], sc_ps[h][:], ACT.Copy).then_inc(probT_out, 1)
                for h in range(2):
                    act.wait_ge(pv_done, 2 * S + h + 1)
                    act.activation(ao_hi[:, h], ring[2 + h][:], ACT.Copy).then_inc(ao_hid, 1)

        def dve_project(ve, it, j):
            S = it * STEPS + j
            for u in (4, 5):
                ve.wait_ge(proj_done, UNITS * S + u + 1)
                t = 2 * (u - 4)
                ve.tensor_copy(v[:, j % 2, t:t + 2].rearrange("p t c -> p (t c)"), ring[u % RING][:]).then_inc(v_out, 1)

        def dve_ao(ve, it, j):
            S = it * STEPS + j
            for h in range(2):
                ve.wait_ge(ao_hid, 2 * S + h + 1)
                ve.tensor_tensor(ao_lo[:, h], ring[2 + h][:], ao_hi[:, h].bitcast(F32), ALU.subtract).then_inc(ao_lod, 1)

        def dve_add(ve, it, j):
            S = it * STEPS + j
            g = j // 2
            ve.wait_ge(wo_done, S + 1)
            for n in range(2):
                y = e.Y[:, g * GROUP + 2 * n:g * GROUP + 2 * n + 2].rearrange("p t d -> p (t d)")
                if not (isinstance(it, int) and it == 0):
                    ve.wait_ge(y_added, S - 1 + n)
                ve.tensor_tensor(y, wo_ps[n][:], y, ALU.add).then_inc(y_added, 1)

        def dve_pass(ve, it, first=False, last=False):
            for j in range(STEPS):
                S = it * STEPS + j
                before = (it, j - 1) if j > 0 else (it - 1, STEPS - 1)
                for h in range(2):
                    ve.wait_ge(scores_done, 2 * S + h + 1)
                    ve.tensor_reduce(nmax[:, j % 2, h], sc_ps[h][:].rearrange("p (b m) -> p b m", b=GROUP), X_AXIS,
                                     ALU.max, negate=True).then_inc(max_done, 1)
                if not (first and j == 0):
                    dve_ao(ve, *before)
                more = not (last and j == STEPS - 1)
                for h in range(2):
                    ve.wait_ge(exp_done, GROUP * (2 * S + h) + GROUP)
                    ve.reciprocal(rec[:, j % 2, h], sums[:, j % 2, h]).then_inc(rec_done, 1)
                chunk = j - 1 if last and 0 <= j - 1 < fw.CHUNKS else None
                if chunk is not None:
                    if chunk == 0:
                        ve.wait_ge(fw.w_in, 16)
                    qz.scales(ve, chunk, fw.raw[:, chunk])
                if more:
                    dve_project(ve, it, j + 1)
                if chunk is not None:
                    qz.round(ve, chunk)
                if j % 2 == 0 and not (first and j == 0):
                    dve_add(ve, *before)

        def pool_split(pool, n, which, hi_sem, lo_sem, hi_at, lo_at):
            hi = w.hi[:, n, which].rearrange("p a k c -> p (a k c)")
            lo = w.lo[:, n, which].rearrange("p a k c -> p (a k c)")
            raw = w.raw[:, n, which].rearrange("p a k c -> p (a k c)")
            copy_pool(pool, e, hi, raw).then_inc(hi_sem, 1)
            pool.wait_ge(hi_sem, hi_at)
            pool.tensor_tensor(lo, raw, hi.bitcast(F32), ALU.subtract).then_inc(lo_sem, 1)

        def pool_pass(pool, it, first=False, last=False):
            for j in range(STEPS):
                S = it * STEPS + j
                for h in range(2):
                    pool.wait_ge(rec_done, 2 * S + h + 1)
                    pool.tensor_tensor(prob[:, h], prob[:, h], over_groups(rec[:, j % 2, h]), ALU.mult).then_inc(norm_done, 1)
                if first and j < SLOTS:
                    pool.wait_ge(moe_raw_in, 16 * SLOTS)
                    pool.tensor_scalar(mw.hi[:, j], moe_raw[:, j], 1.0, None, ALU.mult).then_inc(moe_hi, 1)
                    pool.wait_ge(moe_hi, j + 1)
                    pool.tensor_tensor(mw.lo[:, j], moe_raw[:, j, 0:SEL], mw.hi[:, j, 0:SEL].bitcast(F32),
                                       ALU.subtract).then_inc(moe_split, 1)
                if last and 0 <= j - 1 < fw.CHUNKS:
                    if j == 1:
                        pool.wait_ge(fw.w_in, 16)
                    qz.quotient(pool, j - 1, fw.raw[:, j - 1])
                    qz.restore(pool, j - 1, fw.raw[:, j - 1])
                if not last and j >= STEPS - 3 and j < STEPS - 1:
                    n = j - (STEPS - 3)
                    pool.wait_ge(proj_done, UNITS * (S + 2))
                    pool.wait_ge(raw_in[n], 16 * (it + 1))
                    pool_split(pool, n, slice(0, 3), qkv_hi_split, qkv_split, 2 * it + n + 1, 2 * it + n + 1)
                if not last and j == STEPS - 1:
                    pool.wait_ge(wo_done, S)
                    pool_split(pool, 0, slice(3, 4), wo_hi_split, wo_split, 2 * it + 1, 2 * it + 1)
                if not first and j == 0:
                    pool.wait_ge(wo_done, S)
                    pool_split(pool, 1, slice(3, 4), wo_hi_split, wo_split, 2 * it, 2 * it)

        def sp_pass(sp, it):
            for n in range(2):
                if not (isinstance(it, int) and it == 0):
                    sp.wait_ge(wo_split, 2 * (it - 1) + n + 1)
                sp.dma_start(w.raw[:, n:n + 1], ins["w_attn"][:, ds(2 * it + 2 + n, 1)]).then_inc(raw_in[n], 16)

        with nc.Block() as block:
            @block.sync
            def _(sp):
                sp_pass(sp, 0)
                for j in range(SLOTS):
                    sp.dma_start(moe_raw[:, j], ins["w_moe"][:, j]).then_inc(moe_raw_in, 16)
                sp.wait_ge(moe_split, SLOTS)
                sp.dma_start(fw.raw[:], ins["w_ffn"]).then_inc(fw.w_in, 16)
                with sp.Fori(1, PASSES - 1) as it:
                    sp_pass(sp, it)

            @block.gpsimd
            def _(pool):
                pool_pass(pool, 0, first=True)
                with pool.Fori(1, PASSES - 1) as it:
                    pool_pass(pool, it)
                pool_pass(pool, PASSES - 1, last=True)

            @block.scalar
            def _(act):
                act_project(act, 0, 0)
                act_pass(act, 0)
                with act.Fori(1, PASSES - 1) as it:
                    act_pass(act, it)
                act_pass(act, PASSES - 1, last=True)

            @block.vector
            def _(ve):
                dve_project(ve, 0, 0)
                dve_pass(ve, 0, first=True)
                with ve.Fori(1, PASSES - 1) as it:
                    dve_pass(ve, it)
                dve_pass(ve, PASSES - 1, last=True)
                dve_ao(ve, PASSES - 1, STEPS - 1)
                dve_add(ve, PASSES - 1, STEPS - 1)

            @block.tensor
            def _(pe):
                pe_project(pe, 0, 0, first=True)
                pe_pass(pe, 0, first=True)
                with pe.Fori(1, PASSES - 1) as it:
                    pe_pass(pe, it)
                pe_pass(pe, PASSES - 1, last=True)
                pe_wo(pe, PASSES - 1, STEPS - 1)



class Norm:

    def __init__(self, nc, ctx, tag, banks):
        def sb(name, shape, dt=F32):
            return ctx.enter_context(nc.sbuf_tensor(f"{tag}_{name}", shape, dt))

        self.st, self.mv = sb("st", [P, BATCHES, 6]), sb("mv", [P, BATCHES, 2])
        self.va, self.rs, self.shift = sb("va", [P, BATCHES]), sb("rs", [P, BATCHES]), sb("shift", [P, BATCHES])
        self.nt, self.nu = sb("nt", [P, BATCHES]), sb("nu", [P, BATCHES])
        self.xn = sb("xn", [P, 2, GROUP, D])
        self.banks = banks
        self.chain, self.stats_done, self.ready, self.turned, self.hi_done, self.lo_done = (
            ctx.enter_context(nc.semaphore(f"{tag}_{n}")) for n in ("chain", "stats_done", "ready", "turned", "hi", "lo"))


def norm_vector(ve, n, src, eps, centred, hT_hi, hT_lo, weight=None):
    links = [0]

    def link(instruction):
        links[0] += 1
        instruction.then_inc(n.chain, 1)
        ve.wait_ge(n.chain, links[0])

    for half in range(2):
        tiles = range(half * BATCHES // 2, (half + 1) * BATCHES // 2)
        c = slice(half * BATCHES // 2, (half + 1) * BATCHES // 2)
        va, rs, nt, nu, shift = (a[:, c] for a in (n.va, n.rs, n.nt, n.nu, n.shift))
        for t in tiles:
            last = ve.bn_stats(n.st[:, t], src[:, t])
        link(last)
        for t in tiles:
            last = ve.bn_aggr(n.mv[:, t], n.st[:, t])
        link(last)
        if centred:
            link(ve.tensor_scalar(va, n.mv[:, c, 1], eps, None, ALU.add))
            rsqrt_steps(ve, link, va, rs, nt, nu)
            ve.scalar_tensor_tensor(out=shift, in0=n.mv[:, c, 0], scalar=-1.0, in1=rs, op0=ALU.mult,
                                    op1=ALU.mult).then_inc(n.stats_done, 1)
        else:
            link(ve.tensor_tensor(nt, n.mv[:, c, 0], n.mv[:, c, 0], ALU.mult))
            link(ve.scalar_tensor_tensor(out=va, in0=nt, scalar=eps, in1=n.mv[:, c, 1], op0=ALU.add, op1=ALU.add))
            rsqrt_steps(ve, link, va, rs, nt, nu, lambda instruction: instruction.then_inc(n.stats_done, 1))

    for g in range(GROUPS):
        for k in range(KT):
            ve.wait_ge(n.hi_done, KT * g + k + 1)
            out = hT_lo[:, k, g * GW:(g + 1) * GW]
            hi = hT_hi[:, k, g * GW:(g + 1) * GW].bitcast(F32)
            ps = n.banks[2 * (g % 2) + k][:]
            if weight is None:
                ve.tensor_tensor(out, ps, hi, ALU.subtract).then_inc(n.lo_done, 1)
            else:
                ve.scalar_tensor_tensor(out=out, in0=ps, scalar=weight[:, k:k + 1], in1=hi, op0=ALU.mult,
                                        op1=ALU.subtract).then_inc(n.lo_done, 1)


def norm_tensor(pe, n, ident, g):
    pe.wait_ge(n.ready, g + 1)
    if g >= 2:
        pe.wait_ge(n.lo_done, KT * (g - 1))
    for k in range(KT):
        for b in range(GROUP):
            mm = pe.transpose(n.banks[2 * (g % 2) + k][:, b * P:(b + 1) * P], n.xn[:, g % 2, b, k * P:(k + 1) * P], ident)
    mm.then_inc(n.turned, 1)


def norm_scalar(act, n, src, centred, hT_hi, weight=None):
    for g in range(GROUPS + 1):
        if g < GROUPS:
            act.wait_ge(n.stats_done, g // 2 + 1)
            if g >= 2:
                act.wait_ge(n.turned, g - 1)
            for b in range(GROUP):
                t = g * GROUP + b
                if centred:
                    last = act.activation(n.xn[:, g % 2, b], src[:, t], ACT.Identity, scale=n.rs[:, t:t + 1],
                                          bias=n.shift[:, t:t + 1])
                else:
                    last = act.activation(n.xn[:, g % 2, b], src[:, t], ACT.Copy, scale=n.rs[:, t:t + 1])
            last.then_inc(n.ready, 1)
        if g >= 1:
            act.wait_ge(n.turned, g)
            for k in range(KT):
                scale = 1.0 if weight is None else weight[:, k:k + 1]
                act.activation(hT_hi[:, k, (g - 1) * GW:g * GW], n.banks[2 * ((g - 1) % 2) + k][:], ACT.Copy,
                               scale=scale).then_inc(n.hi_done, 1)


def parts(pe, out, l_hi, l_lo, r_hi, r_lo, start, stop=False):
    pe.matmul(out, l_hi, r_hi, start=start, stop=False, skip_group_check=True)
    pe.matmul(out, l_hi, r_lo, start=False, stop=False, skip_group_check=True)
    return pe.matmul(out, l_lo, r_hi, start=False, stop=stop, skip_group_check=True)


EXPERTS = 16
TOP = 6
EI = 176
SI = 352
TILES = -(-(EXPERTS * EI + SI) // P)
SLOTS = 5
UP, DOWN, SEL, WCOLS = KT * P, 2 * KT * P, 2 * KT * P + D, 2 * KT * P + D + P


class MoeWeights:

    def __init__(self, nc, ctx):
        def sb(name, shape, dt=F32):
            return ctx.enter_context(nc.sbuf_tensor(f"m_{name}", shape, dt))

        self.hi = sb("hi", [P, SLOTS, WCOLS], F32R)
        self.lo = sb("lo", [P, SLOTS, SEL], F32R)


def phase_moe(nc, e, ins, mw):
    STEPS = GROUPS * SLOTS
    PASSES = TILES // SLOTS
    LAG = 2
    RING = 4
    assert TILES % SLOTS == 0 and STEPS % RING == 0
    with ExitStack() as ctx:
        def sb(name, shape, dt=F32):
            return ctx.enter_context(nc.sbuf_tensor(name, shape, dt))

        def sem(name):
            return ctx.enter_context(nc.semaphore(name))

        hT_hi = sb("m_hT_hi", [P, KT, BATCHES * P], F32R)
        hT_lo = sb("m_hT_lo", [P, KT, BATCHES * P], F32R)
        raw = sb("m_raw", [P, SLOTS, WCOLS])
        hi, lo = mw.hi, mw.lo
        ln2 = sb("ln2", [P, KT])
        gate = sb("gate", [P, KT, EXPERTS])
        gate_parts = sb("gate_parts", [P, KT, 2, EXPERTS], F32R)
        cw = sb("cw", [P, BATCHES, EXPERTS + 1])
        cwT_hi = sb("cwT_hi", [EXPERTS + 1, BATCHES * P], F32R)
        cwT_lo = sb("cwT_lo", [EXPERTS + 1, BATCHES * P], F32R)
        silu = sb("silu", [P, 2, GW])
        gated = sb("gated", [P, 2, GW])
        inner = sb("inner", [P, 2, GW])
        in_hi = sb("in_hi", [P, RING, GW], F32R)
        in_lo = sb("in_lo", [P, RING, GW], F32R)
        bank = [ctx.enter_context(nc.psum_tensor(f"m_bank{i}", [P, GW], F32)) for i in range(8)]
        g_ps, u_ps, c_ps, o_ps = bank[0:2], bank[2:4], bank[4:6], bank[6:8]
        cwT_ps = (bank[4], bank[5], bank[7], bank[6])
        nrm = Norm(nc, ctx, "m", bank[0:4])
        PAD = EXPERTS // 2
        lg, pr, gt, eq, sel = (sb(n, [P, BATCHES, EXPERTS]) for n in ("lg", "pr", "gt", "eq", "g_sel"))
        pre = [sb(f"pre{i}", [P, BATCHES, PAD + EXPERTS]) for i in range(2)]
        top8 = sb("top8", [P, BATCHES, 8])
        gmx, cnt, need, tot, inv = (sb(n, [P, BATCHES]) for n in ("gmx", "cnt", "need", "tot", "inv"))

        small_in, x_plus, gate_split = sem("small_in"), sem("x_plus"), sem("gate_split")
        logits_done, g_shift, g_exp, g_chain, cw_ready = (sem(n) for n in ("logits_done", "g_shift", "g_exp", "g_chain", "cw_ready"))
        cwT_done, cwT_hid, cwT_lod = sem("cwT_done"), sem("cwT_hid"), sem("cwT_lod")
        up_hi_split, up_split, down_hi_split, down_split = (sem(n) for n in ("up_hi_split", "up_split", "down_hi_split", "down_split"))
        raw_in = [sem(f"m_raw_in{j}") for j in range(SLOTS)]
        g_done, u_done, c_done, silu_done, gated_done, inner_done = (
            sem(n) for n in ("g_done", "u_done", "c_done", "silu_done", "gated_done", "inner_done"))
        in_hid, in_lod, down_done, added = (sem(n) for n in ("in_hid", "in_lod", "down_done", "added"))

        def spread(a):
            return a.unsqueeze(2).broadcast_to([P, BATCHES, EXPERTS])

        def gate_vector(ve):
            links = [0]

            def link(instruction):
                links[0] += 1
                instruction.then_inc(g_chain, 1)
                ve.wait_ge(g_chain, links[0])

            lps = o_ps[0][:].rearrange("p (t a e) -> p t a e", a=2, e=EXPERTS)
            ve.memset(cw[:, :, EXPERTS:EXPERTS + 1], 1.0)
            ve.memset(pre[0][:], 0.0)
            link(ve.memset(pre[1][:], 0.0))
            ve.wait_ge(logits_done, 1)
            link(ve.tensor_copy(lg[:], lps[:, :, 0]))
            link(ve.tensor_tensor(lg[:], lps[:, :, 1], lg[:], ALU.add))
            link(ve.tensor_reduce(gmx[:], lg[:], X_AXIS, ALU.max))
            ve.tensor_tensor(lg[:], lg[:], spread(gmx[:]), ALU.subtract).then_inc(g_shift, 1)
            ve.wait_ge(g_exp, 1)
            for t in range(BATCHES):
                last = ve.max(top8[:, t], pr[:, t])
            link(last)
            sixth = spread(top8[:, :, TOP - 1])
            ve.tensor_tensor(eq[:], pr[:], sixth, ALU.is_equal)
            link(ve.tensor_tensor(gt[:], pr[:], sixth, ALU.is_gt))
            ve.tensor_copy(pre[0][:, :, PAD:], eq[:])
            link(ve.tensor_reduce(cnt[:], gt[:], X_AXIS, ALU.add))
            link(ve.tensor_scalar(need[:], cnt[:], -1.0, float(TOP), ALU.mult, ALU.add))
            for i, shift in enumerate((1, 2, 4, 8)):
                a, b = pre[i % 2], pre[(i + 1) % 2]
                link(ve.tensor_tensor(b[:, :, PAD:], a[:, :, PAD:], a[:, :, PAD - shift:PAD - shift + EXPERTS], ALU.add))
            link(ve.tensor_tensor(sel[:], pre[0][:, :, PAD:], spread(need[:]), ALU.is_le))
            link(ve.tensor_tensor(sel[:], sel[:], eq[:], ALU.mult))
            link(ve.tensor_tensor(sel[:], sel[:], gt[:], ALU.add))
            link(ve.tensor_tensor(sel[:], sel[:], pr[:], ALU.mult))
            link(ve.tensor_reduce(tot[:], sel[:], X_AXIS, ALU.add))
            link(ve.reciprocal(inv[:], tot[:]))
            ve.tensor_tensor(cw[:, :, 0:EXPERTS], sel[:], spread(inv[:]), ALU.mult).then_inc(cw_ready, 1)
            for g in range(GROUPS):
                ve.wait_ge(cwT_hid, g + 1)
                cols = slice(g * GW, (g + 1) * GW)
                ve.tensor_tensor(cwT_lo[:, cols], cwT_ps[g][0:EXPERTS + 1, :], cwT_hi[:, cols].bitcast(F32),
                                 ALU.subtract).then_inc(cwT_lod, 1)

        def pe_logits(pe, g):
            if g == 0:
                pe.wait_ge(gate_split, 2)
            pe.wait_ge(nrm.lo_done, KT * (g + 1))
            for t in range(g * GROUP, (g + 1) * GROUP):
                out = o_ps[0][:, t * 2 * EXPERTS:(t + 1) * 2 * EXPERTS]
                for k in range(KT):
                    for h in (hT_hi, hT_lo):
                        mm = pe.matmul(out, h[:, k, t * P:(t + 1) * P], gate_parts[:, k].rearrange("p a e -> p (a e)"),
                                       start=(t == 0 and k == 0 and h is hT_hi), stop=(k == KT - 1 and h is hT_lo),
                                       skip_group_check=True)
            if g == GROUPS - 1:
                mm.then_inc(logits_done, 1)

        def pe_gate_up(pe, it, i):
            S, g, j, par = it * STEPS + i, i // SLOTS, i % SLOTS, i % 2
            early = isinstance(it, int) and S < 2
            if g == 0 and not (isinstance(it, int) and it == 0):
                pe.wait_ge(up_split, (it - 1) * SLOTS + j + 1)
            cols = slice(g * GW, (g + 1) * GW)
            for base, out, done, free in ((0, g_ps[par], g_done, silu_done), (UP, u_ps[par], u_done, gated_done)):
                if not early:
                    pe.wait_ge(free, S - 1)
                for k in range(KT):
                    wc = slice(base + k * P, base + (k + 1) * P)
                    mm = parts(pe, out[:], hi[:, j, wc], lo[:, j, wc], hT_hi[:, k, cols], hT_lo[:, k, cols],
                               start=(k == 0), stop=(k == KT - 1))
                mm.then_inc(done, 1)

        def pe_weights(pe, it, i):
            S, g, j, par = it * STEPS + i, i // SLOTS, i % SLOTS, i % 2
            cols = slice(g * GW, (g + 1) * GW)
            if not (isinstance(it, int) and S < 2):
                pe.wait_ge(inner_done, S - 1)
            sel_rows = hi[0:EXPERTS + 1, j, SEL:WCOLS]
            pe.matmul(c_ps[par][:], sel_rows, cwT_hi[:, cols], start=True, stop=False)
            pe.matmul(c_ps[par][:], sel_rows, cwT_lo[:, cols], start=False, stop=True).then_inc(c_done, 1)

        def pe_down(pe, it, i):
            S, g, j = it * STEPS + i, i // SLOTS, i % SLOTS
            pe.wait_ge(in_lod, S + 1)
            if g == 0 and not (isinstance(it, int) and it == 0):
                pe.wait_ge(down_split, (it - 1) * SLOTS + j + 1)
            if j == 0 and not (isinstance(it, int) and it == 0 and g == 0):
                pe.wait_ge(added, 2 * (it * GROUPS + g))
            for b in range(GROUP):
                c = slice(b * P, (b + 1) * P)
                mm = parts(pe, o_ps[b // 2][:, (b % 2) * D:(b % 2 + 1) * D], in_hi[:, i % RING, c], in_lo[:, i % RING, c],
                           hi[:, j, DOWN:SEL], lo[:, j, DOWN:SEL], start=(j == 0 and b % 2 == 0), stop=(j == SLOTS - 1))
            mm.then_inc(down_done, 1)

        def lagging(it, i, first):
            return (it, i - LAG) if i >= LAG else None if first else (it - 1, i - LAG + STEPS)

        def pe_pass(pe, it, first=False):
            for i in range(STEPS):
                if not (first and i < 2):
                    pe_gate_up(pe, it, i)
                pe_weights(pe, it, i)
                if (before := lagging(it, i, first)) is not None:
                    pe_down(pe, *before)

        def act_silu(act, it, i):
            S = it * STEPS + i
            act.wait_ge(g_done, S + 1)
            act.activation(silu[:, i % 2], g_ps[i % 2][:], ACT.Silu).then_inc(silu_done, 1)

        def act_hi(act, it, i):
            S = it * STEPS + i
            act.wait_ge(inner_done, S + 1)
            act.activation(in_hi[:, i % RING], inner[:, i % 2], ACT.Copy).then_inc(in_hid, 1)

        def act_pass(act, it, first=False):
            for i in range(STEPS):
                act_silu(act, it, i)
                if i > 0:
                    act_hi(act, it, i - 1)
                elif not first:
                    act_hi(act, it - 1, STEPS - 1)

        def ve_add(ve, it, i):
            S, g = it * STEPS + i, i // SLOTS
            ve.wait_ge(down_done, S + 1)
            for n in range(2):
                x = e.X[:, g * GROUP + 2 * n:g * GROUP + 2 * n + 2].rearrange("p t d -> p (t d)")
                if not (isinstance(it, int) and it == 0):
                    ve.wait_ge(added, 2 * (it * GROUPS + g) + n)
                ve.tensor_tensor(x, o_ps[n][:], x, ALU.add).then_inc(added, 1)

        def ve_pass(ve, it, first=False):
            for i in range(STEPS):
                S, par = it * STEPS + i, i % 2
                ve.wait_ge(silu_done, S + 1)
                ve.wait_ge(u_done, S + 1)
                ve.tensor_tensor(gated[:, par], u_ps[par][:], silu[:, par], ALU.mult).then_inc(gated_done, 1)
                ve.wait_ge(c_done, S + 1)
                ve.wait_ge(gated_done, S + 1)
                if not (isinstance(it, int) and S < 2):
                    ve.wait_ge(in_lod, S - 1)
                ve.tensor_tensor(inner[:, par], c_ps[par][:], gated[:, par], ALU.mult).then_inc(inner_done, 1)
                before = lagging(it, i, first)
                if before is not None and before[1] % SLOTS == SLOTS - 1:
                    ve_add(ve, *before)

        def pool_low(pool, it, i):
            S = it * STEPS + i
            pool.wait_ge(in_hid, S + 1)
            pool.tensor_tensor(in_lo[:, i % RING], inner[:, i % 2], in_hi[:, i % RING].bitcast(F32),
                               ALU.subtract).then_inc(in_lod, 1)

        def pool_refill_up(pool, it, j):
            pool.wait_ge(c_done, it * STEPS + STEPS - SLOTS + j + 1)
            pool.wait_ge(raw_in[j], 16 * (it + 1))
            copy_pool(pool, e, hi[:, j, SEL:WCOLS], raw[:, j, SEL:WCOLS])
            copy_pool(pool, e, hi[:, j, 0:DOWN], raw[:, j, 0:DOWN]).then_inc(up_hi_split, 1)
            pool.wait_ge(up_hi_split, it * SLOTS + j + 1)
            pool.tensor_tensor(lo[:, j, 0:DOWN], raw[:, j, 0:DOWN], hi[:, j, 0:DOWN].bitcast(F32),
                               ALU.subtract).then_inc(up_split, 1)

        def pool_refill_down(pool, it, j):
            pool.wait_ge(down_done, it * STEPS + STEPS - SLOTS + j + 1)
            copy_pool(pool, e, hi[:, j, DOWN:SEL], raw[:, j, DOWN:SEL]).then_inc(down_hi_split, 1)
            pool.wait_ge(down_hi_split, it * SLOTS + j + 1)
            pool.tensor_tensor(lo[:, j, DOWN:SEL], raw[:, j, DOWN:SEL], hi[:, j, DOWN:SEL].bitcast(F32),
                               ALU.subtract).then_inc(down_split, 1)

        def pool_pass(pool, it, first=False, last=False):
            for i in range(STEPS):
                pool_low(pool, it, i)
                if not last and i >= STEPS - SLOTS:
                    pool_refill_up(pool, it, i - (STEPS - SLOTS))
                back = i - (STEPS - SLOTS) - LAG
                if not last and back >= 0:
                    pool_refill_down(pool, it, back)
                if not first and i < LAG:
                    pool_refill_down(pool, it - 1, SLOTS - LAG + i)

        with nc.Block() as block:
            @block.sync
            def _(sp):
                sp.dma_start(ln2[:], ins["ln2"]).then_inc(small_in, 16)
                sp.dma_start(gate[:], ins["gate"]).then_inc(small_in, 16)
                for j in range(SLOTS):
                    sp.dma_start(raw[:, j], ins["w_moe"][:, SLOTS + j]).then_inc(raw_in[j], 16)
                with sp.Fori(2, PASSES) as it:
                    for j in range(SLOTS):
                        sp.wait_ge(down_split, (it - 2) * SLOTS + j + 1)
                        sp.wait_ge(up_split, (it - 2) * SLOTS + j + 1)
                        sp.dma_start(raw[:, j:j + 1], ins["w_moe"][:, ds(it * SLOTS + j, 1)]).then_inc(raw_in[j], 16)

            @block.gpsimd
            def _(pool):
                pool.wait_ge(small_in, 32)
                pool.tensor_scalar(gate_parts[:, :, 0], gate[:], 1.0, None, ALU.mult).then_inc(gate_split, 1)
                pool.wait_ge(gate_split, 1)
                pool.tensor_tensor(gate_parts[:, :, 1], gate[:], gate_parts[:, :, 0].bitcast(F32),
                                   ALU.subtract).then_inc(gate_split, 1)
                pool.tensor_tensor(e.X[:].rearrange("p t d -> p (t d)"), e.X[:].rearrange("p t d -> p (t d)"),
                                   e.Y[:].rearrange("p t d -> p (t d)"), ALU.add).then_inc(x_plus, 1)
                pool_pass(pool, 0, first=True)
                with pool.Fori(1, PASSES - 1) as it:
                    pool_pass(pool, it)
                pool_pass(pool, PASSES - 1, last=True)

            @block.scalar
            def _(act):
                act.wait_ge(small_in, 32)
                norm_scalar(act, nrm, e.Y, False, hT_hi, ln2)
                act.wait_ge(g_shift, 1)
                act.activation(pr[:], lg[:], ACT.Exp).then_inc(g_exp, 1)
                for g in range(GROUPS):
                    act.wait_ge(cwT_done, g + 1)
                    act.activation(cwT_hi[:, g * GW:(g + 1) * GW], cwT_ps[g][0:EXPERTS + 1, :], ACT.Copy).then_inc(cwT_hid, 1)
                act_pass(act, 0, first=True)
                with act.Fori(1, PASSES) as it:
                    act_pass(act, it)
                act_hi(act, PASSES - 1, STEPS - 1)

            @block.vector
            def _(ve):
                ve.wait_ge(small_in, 32)
                norm_vector(ve, nrm, e.Y, RMS_EPS, False, hT_hi, hT_lo, ln2)
                gate_vector(ve)
                ve.wait_ge(x_plus, 1)
                ve_pass(ve, 0, first=True)
                with ve.Fori(1, PASSES) as it:
                    ve_pass(ve, it)
                ve_add(ve, PASSES - 1, STEPS - 1)

            @block.tensor
            def _(pe):
                for g in range(GROUPS + 1):
                    if g < GROUPS:
                        norm_tensor(pe, nrm, e.ident[:], g)
                    if g >= 1:
                        pe_logits(pe, g - 1)
                for i in range(2):
                    pe_gate_up(pe, 0, i)
                pe.wait_ge(cw_ready, 1)
                for g in range(GROUPS):
                    for b in range(GROUP):
                        mm = pe.transpose(cwT_ps[g][0:EXPERTS + 1, b * P:(b + 1) * P], cw[:, g * GROUP + b], e.ident[:])
                    mm.then_inc(cwT_done, 1)
                pe.wait_ge(cwT_lod, GROUPS)
                pe_pass(pe, 0, first=True)
                with pe.Fori(1, PASSES) as it:
                    pe_pass(pe, it)
                for i in range(STEPS - LAG, STEPS):
                    pe_down(pe, PASSES - 1, i)


KVC, QC, ROPE = 64, 96, 64
HALF = ROPE // 2
LOOKBACK = 8
T_EVEN, T_ODD, T_SIN_Q, T_COS, T_SIN, T_KEY = range(6)


class LatentState:

    def __init__(self, nc, ctx):
        def sb(name, shape, dt=F32):
            return ctx.enter_context(nc.sbuf_tensor(f"l_{name}", shape, dt))

        self.key = sb("key", [P, 2, BATCHES * P])
        self.val = sb("val", [P, BATCHES, 3 * KVC])
        self.mask = sb("mask", [P, BATCHES, P], F32R)
        self.wa_hi = sb("wa_hi", [QC, HEADS, P], F32R)
        self.wa_lo = sb("wa_lo", [QC, HEADS, P], F32R)
        self.wb_hi = sb("wb_hi", [QC, PAIRS, P], F32R)
        self.wb_lo = sb("wb_lo", [QC, PAIRS, P], F32R)
        self.wv_hi = sb("wv_hi", [P, PAIRS, D], F32R)
        self.wv_lo = sb("wv_lo", [P, PAIRS, D], F32R)
        self.tab = sb("tab", [P, 6, P])


def phase_latent_keys(nc, e, ins, z):
    with ExitStack() as ctx:
        def sb(name, shape, dt=F32):
            return ctx.enter_context(nc.sbuf_tensor(f"k_{name}", shape, dt))

        def sem(name):
            return ctx.enter_context(nc.semaphore(f"k_{name}"))

        ctxT = sb("ctxT", [P, KT, BATCHES * P])
        wkvc = sb("wkvc", [P, KT, 2 * KVC])
        wkr = sb("wkr", [KVC, 2, P])
        uqT = sb("uqT", [P, HEADS, QC])
        ukT = sb("ukT", [P, HEADS, KVC])
        uvT = sb("uvT", [P, HEADS, KVC])
        wo = sb("wo", [P, HEADS, D])
        qr = sb("qr", [QC, HEADS, ROPE])
        qrb = sb("qrb", [QC, PAIRS, P])
        seg = sb("seg", [P, BATCHES], I32)
        segf = sb("segf", [P, BATCHES])
        dist = sb("dist", [P, BATCHES, P])
        near = sb("near", [P, BATCHES, P])
        kvT = sb("kvT", [P, GW])
        rot = sb("rot", [P, 2, GW])
        rot2 = sb("rot2", [P, GW])
        bank = [ctx.enter_context(nc.psum_tensor(f"k_bank{i}", [P, GW], F32)) for i in range(8)]

        w_in, ctx_in, tab_in, seg_in = sem("w_in"), sem("ctx_in"), sem("tab_in"), sem("seg_in")
        absorbed, a_hi, a_lo, wv_done, wv_hi, wv_lo = (sem(n) for n in ("absorbed", "a_hi", "a_lo", "wv_done", "wv_hi", "wv_lo"))
        qr_hi, pool_chain, val_zero = sem("qr_hi"), sem("pool"), sem("val_zero")
        kvT_done, kvT_sb, kr_done, kv_done = sem("kvT_done"), sem("kvT_sb"), sem("kr_done"), sem("kv_done")
        key_out, val_out, r1, r2, r3, rk_out = (sem(n) for n in ("key_out", "val_out", "r1", "r2", "r3", "rk_out"))

        with nc.Block() as block:
            @block.sync
            def _(sp):
                for dst, name in ((uqT, "uqT"), (ukT, "ukT"), (wkvc, "wkvc"), (wkr, "wkr"), (uvT, "uvT"), (wo, "w_o2"),
                                  (qr, "qr"), (qrb, "qrb")):
                    sp.dma_start(dst[:], ins[name]).then_inc(w_in, 16)

            @block.gpsimd
            def _(pool):
                links = [0]

                def link(instruction):
                    links[0] += 1
                    instruction.then_inc(pool_chain, 1)
                    pool.wait_ge(pool_chain, links[0])

                pool.memset(z.val[:], 0.0).then_inc(val_zero, 1)
                pool.wait_ge(seg_in, 16)
                link(pool.tensor_copy(segf[:], seg[:]))
                pool.wait_ge(tab_in, 16)
                keys = z.tab[:, T_KEY].unsqueeze(1).broadcast_to([P, BATCHES, P])
                link(pool.tensor_tensor(dist[:], keys, segf[:].unsqueeze(2).broadcast_to([P, BATCHES, P]), ALU.subtract))
                pool.tensor_scalar(near[:], dist[:], float(-LOOKBACK), -1.0e30, ALU.is_lt, ALU.mult)
                link(pool.tensor_scalar(dist[:], dist[:], 0.0, -1.0e30, ALU.is_gt, ALU.mult))
                pool.tensor_tensor(z.mask[:], near[:], dist[:], ALU.add)
                pool.wait_ge(w_in, 16 * 8)
                link(pool.tensor_scalar(z.wb_hi[:], qrb[:], 1.0, None, ALU.mult))
                pool.tensor_tensor(z.wb_lo[:], qrb[:], z.wb_hi[:].bitcast(F32), ALU.subtract)
                for odd in range(2):
                    cols = slice(0, ROPE) if odd else slice(KVC, P)
                    link(pool.tensor_scalar(z.wa_hi[:, odd::2, cols], qr[:, odd::2], 1.0, None, ALU.mult))
                    pool.tensor_tensor(z.wa_lo[:, odd::2, cols], qr[:, odd::2], z.wa_hi[:, odd::2, cols].bitcast(F32), ALU.subtract)

            @block.tensor
            def _(pe):
                pe.wait_ge(w_in, 16 * 8)
                for h in range(HEADS):
                    mm = pe.matmul(bank[h // 8][0:QC, (h % 8) * KVC:(h % 8 + 1) * KVC], uqT[:, h], ukT[:, h],
                                   start=True, stop=True)
                mm.then_inc(absorbed, 1)
                for p in range(PAIRS):
                    for odd in range(2):
                        mm = pe.matmul(bank[2 + p // 2][odd * KVC:(odd + 1) * KVC, (p % 2) * D:(p % 2 + 1) * D],
                                       uvT[:, 2 * p + odd], wo[:, 2 * p + odd], start=True, stop=True)
                mm.then_inc(wv_done, 1)
                pe.wait_ge(ctx_in, 16)
                for g in range(GROUPS):
                    cols = slice(g * GW, (g + 1) * GW)
                    if g == 0:
                        pe.wait_ge(a_lo, 4)
                    else:
                        pe.wait_ge(key_out, 2 * g)
                    for k in range(KT):
                        mm = pe.matmul(bank[0][:], wkvc[:, k], ctxT[:, k, cols], start=(k == 0), stop=(k == KT - 1))
                    mm.then_inc(kvT_done, 1)
                    if g > 0:
                        pe.wait_ge(val_out, g)
                    for b in range(GROUP):
                        t = g * GROUP + b
                        for k in range(KT):
                            mm = pe.matmul(bank[1][:, b * KVC:(b + 1) * KVC], ctxT[:, k, t * P:(t + 1) * P],
                                           wkvc[:, k, 0:KVC], start=(b == 0 and k == 0), stop=(k == KT - 1),
                                           skip_group_check=True)
                    mm.then_inc(kv_done, 1)
                    pe.wait_ge(kvT_sb, g + 1)
                    if g == 0:
                        pe.wait_ge(wv_lo, 4)
                    else:
                        pe.wait_ge(r2, g)
                    pe.matmul(bank[2][:], wkr[:, 0], kvT[0:KVC, :], start=True, stop=True)
                    pe.matmul(bank[3][:], wkr[:, 1], kvT[0:KVC, :], start=True, stop=True).then_inc(kr_done, 1)

            @block.scalar
            def _(act):
                act.dma_start(seg[:], ins["seg"]).then_inc(seg_in, 16)
                act.dma_start(z.tab[:], ins["tab"]).then_inc(tab_in, 16)
                act.dma_start(ctxT[:], ins["ctxT"].rearrange("(k p) t -> p k t", p=P)).then_inc(ctx_in, 16)
                act.wait_ge(absorbed, 1)
                for half in range(2):
                    for odd in range(2):
                        cols = slice(KVC, P) if odd else slice(0, KVC)
                        src = bank[half][0:QC, :].rearrange("q (h c) -> q h c", c=KVC)[:, odd::2]
                        act.activation(z.wa_hi[:, 8 * half + odd:8 * half + 8:2, cols], src, ACT.Copy).then_inc(a_hi, 1)
                act.wait_ge(wv_done, 1)
                for i in range(4):
                    act.activation(z.wv_hi[:, 2 * i:2 * i + 2].rearrange("p a c -> p (a c)"), bank[2 + i][:], ACT.Copy).then_inc(wv_hi, 1)
                act.wait_ge(val_zero, 1)
                for g in range(GROUPS):
                    cols = slice(g * GW, (g + 1) * GW)
                    act.wait_ge(kvT_done, g + 1)
                    if g > 0:
                        act.wait_ge(kr_done, g)
                    act.activation(kvT[:], bank[0][:], ACT.Copy).then_inc(kvT_sb, 1)
                    act.activation(z.key[0:KVC, 0, cols], bank[0][0:KVC, :], ACT.Copy).then_inc(key_out, 1)
                    act.activation(z.key[KVC:P, 1, cols], bank[0][KVC:P, :], ACT.Copy).then_inc(key_out, 1)
                    act.wait_ge(kv_done, g + 1)
                    act.activation(z.val[:, g * GROUP:(g + 1) * GROUP, KVC:2 * KVC],
                                   bank[1][:, 0:GROUP * KVC].rearrange("p (b c) -> p b c", b=GROUP), ACT.Copy).then_inc(val_out, 1)

            @block.vector
            def _(ve):
                for half in range(2):
                    for odd in range(2):
                        cols = slice(KVC, P) if odd else slice(0, KVC)
                        src = bank[half][0:QC, :].rearrange("q (h c) -> q h c", c=KVC)[:, odd::2]
                        heads = slice(8 * half + odd, 8 * half + 8, 2)
                        ve.wait_ge(a_hi, 2 * half + 2)
                        ve.tensor_tensor(z.wa_lo[:, heads, cols], src, z.wa_hi[:, heads, cols].bitcast(F32),
                                         ALU.subtract).then_inc(a_lo, 1)
                for i in range(4):
                    ve.wait_ge(wv_hi, i + 1)
                    ve.tensor_tensor(z.wv_lo[:, 2 * i:2 * i + 2].rearrange("p a c -> p (a c)"), bank[2 + i][:],
                                     z.wv_hi[:, 2 * i:2 * i + 2].rearrange("p a c -> p (a c)").bitcast(F32),
                                     ALU.subtract).then_inc(wv_lo, 1)
                ve.wait_ge(tab_in, 16)
                for g in range(GROUPS):
                    cols = slice(g * GW, (g + 1) * GW)
                    ve.wait_ge(kr_done, g + 1)

                    def table(n):
                        return z.tab[:, n].unsqueeze(1).broadcast_to([P, GROUP, P])

                    def by_batch(a):
                        return a.rearrange("p (b c) -> p b c", b=GROUP)

                    if g >= 1:
                        ve.wait_ge(rk_out, 2 * g)
                    ve.tensor_tensor(by_batch(rot2[:]), by_batch(bank[3][:]), table(T_SIN), ALU.mult).then_inc(r1, 1)
                    ve.tensor_tensor(by_batch(rot[:, g % 2]), by_batch(bank[2][:]), table(T_COS), ALU.mult).then_inc(r2, 1)
                    ve.wait_ge(r1, g + 1)
                    ve.wait_ge(r2, g + 1)
                    ve.tensor_tensor(rot[:, g % 2], rot[:, g % 2], rot2[:], ALU.add).then_inc(r3, 1)
                    ve.wait_ge(r3, g + 1)
                    ve.tensor_copy(z.key[KVC:P, 0, cols], rot[KVC:P, g % 2]).then_inc(rk_out, 1)
                    ve.tensor_copy(z.key[0:KVC, 1, cols], rot[0:KVC, g % 2]).then_inc(rk_out, 1)


def phase_latent_queries(nc, e, ins, z, qc_hi, qc_lo):
    with ExitStack() as ctx:
        def sb(name, shape, dt=F32):
            return ctx.enter_context(nc.sbuf_tensor(f"q_{name}", shape, dt))

        def sem(name):
            return ctx.enter_context(nc.semaphore(f"q_{name}"))

        hT_hi = sb("hT_hi", [P, KT, BATCHES * P], F32R)
        hT_lo = sb("hT_lo", [P, KT, BATCHES * P], F32R)
        wdq = sb("wdq", [P, KT, QC])
        wdq_hi = sb("wdq_hi", [P, KT, QC], F32R)
        wdq_lo = sb("wdq_lo", [P, KT, QC], F32R)
        bank = [ctx.enter_context(nc.psum_tensor(f"q_bank{i}", [P, GW], F32)) for i in range(6)]
        nrm = Norm(nc, ctx, "q", bank[0:4])
        w_in, w_hi, w_lo, qc_done, qc_hid, qc_lod = (sem(n) for n in ("w_in", "w_hi", "w_lo", "qc_done", "qc_hid", "qc_lod"))

        with nc.Block() as block:
            @block.sync
            def _(sp):
                sp.dma_start(wdq[:], ins["wdq"]).then_inc(w_in, 16)

            @block.gpsimd
            def _(pool):
                pool.wait_ge(w_in, 16)
                pool.tensor_scalar(wdq_hi[:], wdq[:], 1.0, None, ALU.mult).then_inc(w_hi, 1)
                pool.wait_ge(w_hi, 1)
                pool.tensor_tensor(wdq_lo[:], wdq[:], wdq_hi[:].bitcast(F32), ALU.subtract).then_inc(w_lo, 1)

            @block.tensor
            def _(pe):
                norm_tensor(pe, nrm, e.ident[:], 0)
                pe.wait_ge(w_lo, 1)
                for g in range(GROUPS):
                    if g + 1 < GROUPS:
                        norm_tensor(pe, nrm, e.ident[:], g + 1)
                    cols = slice(g * GW, (g + 1) * GW)
                    pe.wait_ge(nrm.lo_done, KT * (g + 1))
                    if g >= 2:
                        pe.wait_ge(qc_lod, g - 1)
                    for k in range(KT):
                        mm = parts(pe, bank[4 + g % 2][0:QC, :], wdq_hi[:, k], wdq_lo[:, k], hT_hi[:, k, cols],
                                   hT_lo[:, k, cols], start=(k == 0), stop=(k == KT - 1))
                    mm.then_inc(qc_done, 1)

            @block.scalar
            def _(act):
                norm_scalar(act, nrm, e.X, True, hT_hi)
                for g in range(GROUPS):
                    act.wait_ge(qc_done, g + 1)
                    act.activation(qc_hi[:, g * GW:(g + 1) * GW], bank[4 + g % 2][0:QC, :], ACT.Copy).then_inc(qc_hid, 1)

            @block.vector
            def _(ve):
                norm_vector(ve, nrm, e.X, LN_EPS, True, hT_hi, hT_lo)
                for g in range(GROUPS):
                    cols = slice(g * GW, (g + 1) * GW)
                    ve.wait_ge(qc_hid, g + 1)
                    ve.tensor_tensor(qc_lo[:, cols], bank[4 + g % 2][0:QC, :], qc_hi[:, cols].bitcast(F32),
                                     ALU.subtract).then_inc(qc_lod, 1)


def phase_latent_attention(nc, e, z, qc_hi, qc_lo):
    AHEAD = 2
    with ExitStack() as ctx:
        def sb(name, shape, dt=F32):
            return ctx.enter_context(nc.sbuf_tensor(f"t_{name}", shape, dt))

        def sem(name):
            return ctx.enter_context(nc.semaphore(f"t_{name}"))

        val = sb("val", [P, GROUP, 3 * KVC])
        rot = sb("rot", [P, GW])
        q = sb("q", [P, 2, 2, GW])
        prob = sb("prob", [P, 2, 2, GROUP, P])
        pT = sb("pT", [P, 2, GW])
        c_hi = sb("c_hi", [P, 2, GW], F32R)
        c_lo = sb("c_lo", [P, 2, GW], F32R)
        nmax, sums, rec = (sb(n, [P, 2, 2, GROUP]) for n in ("nmax", "sums", "rec"))
        bank = [ctx.enter_context(nc.psum_tensor(f"t_bank{i}", [P, GW], F32)) for i in range(8)]
        b_ps, a_ps, pT_ps, sc_ps, wo_ps = bank[0], bank[1:3], bank[3], bank[4:6], bank[6:8]
        c_ps = b_ps

        rot_proj, rot_done, q_proj, cos_done, q_sum = (sem(n) for n in ("rot_proj", "rot_done", "q_proj", "cos_done", "q_sum"))
        scores_done, max_done, exp_done, rec_done, norm_even, norm_odd = (
            sem(n) for n in ("scores_done", "max_done", "exp_done", "rec_done", "norm_even", "norm_odd"))
        pT_done, pT_out, pv_done, c_hid, c_lod, wo_done, added, val_in = (
            sem(n) for n in ("pT_done", "pT_out", "pv_done", "c_hid", "c_lod", "wo_done", "added", "val_in"))

        def shifted(it, i, by, first, last):
            n = i + by
            if n < 0:
                return None if first else (it - 1, n + PAIRS)
            if n >= PAIRS:
                return None if last else (it + 1, n - PAIRS)
            return it, n

        def known_before(it, i, n):
            return isinstance(it, int) and it * PAIRS + i < n

        def columns(it):
            return slice(it * GW, (it + 1) * GW) if isinstance(it, int) else ds(it * GW, GW)

        def pe_rot(pe, it, i):
            S = it * PAIRS + i
            if not known_before(it, i, AHEAD + 2):
                pe.wait_ge(c_lod, S - AHEAD - 1)
            elif S > 0:
                pe.wait_ge(rot_done, S)
            parts(pe, b_ps[:], z.wb_hi[:, i], z.wb_lo[:, i], qc_hi[:, columns(it)], qc_lo[:, columns(it)],
                  start=True, stop=True).then_inc(rot_proj, 1)

        def pe_query(pe, it, i, h):
            S = it * PAIRS + i
            if not known_before(it, i, 1):
                pe.wait_ge(cos_done, 2 * S - 1 + h)
            parts(pe, a_ps[h][:], z.wa_hi[:, 2 * i + h], z.wa_lo[:, 2 * i + h], qc_hi[:, columns(it)],
                  qc_lo[:, columns(it)], start=True, stop=True).then_inc(q_proj, 1)

        def pe_scores(pe, it, i):
            S = it * PAIRS + i
            for h in range(2):
                pe.wait_ge(q_sum, 2 * S + h + 1)
                if not known_before(it, i, 1):
                    pe.wait_ge(exp_done, GROUP * (2 * S - 1 + h))
                for b in range(GROUP):
                    c = slice(b * P, (b + 1) * P)
                    keys = (it * GROUP + b) * P
                    at = slice(keys, keys + P) if isinstance(it, int) else ds(keys, P)
                    pe.matmul(sc_ps[h][:, c], q[:, i % 2, h, c], z.key[:, h, at], start=(b == 0), stop=False,
                              skip_group_check=True)
                pe.matmul(sc_ps[h][:].rearrange("p (b k) -> p b k", b=GROUP), e.ident_r[:],
                          z.mask[:, ds(it * GROUP, GROUP)], start=False, stop=True, skip_group_check=True)\
                    .then_inc(scores_done, 1)

        def pe_turn(pe, it, i, h):
            S = it * PAIRS + i
            pe.wait_ge((norm_even, norm_odd)[h], S + 1)
            if h == 1:
                pe.wait_ge(pT_out, 2 * S + 1)
            elif not known_before(it, i, 1):
                pe.wait_ge(pT_out, 2 * S)
            for b in range(GROUP):
                mm = pe.transpose(pT_ps[:, b * P:(b + 1) * P], prob[:, i % 2, h, b], e.ident[:])
            mm.then_inc(pT_done, 1)

        def pe_values(pe, it, i, ahead):
            S = it * PAIRS + i
            if i == 0:
                pe.wait_ge(val_in, it + 1)
            if ahead:
                pe.wait_ge(rot_done, S + AHEAD + 2)
            else:
                pe.wait_ge(c_lod, S)
            for h in range(2):
                pe.wait_ge(pT_out, 2 * S + h + 1)
                block_of = slice(KVC, 3 * KVC) if h == 0 else slice(0, 2 * KVC)
                for b in range(GROUP):
                    c = slice(b * P, (b + 1) * P)
                    mm = pe.matmul(c_ps[:, c], val[:, b, block_of], pT[:, h, c], start=(h == 0 and b == 0), stop=(h == 1),
                                   skip_group_check=True)
            mm.then_inc(pv_done, 1)

        def pe_out(pe, it, i):
            S = it * PAIRS + i
            pe.wait_ge(c_lod, S + 1)
            if i == 0 and not known_before(it, i, 1):
                pe.wait_ge(added, 2 * it)
            for b in range(GROUP):
                c = slice(b * P, (b + 1) * P)
                mm = parts(pe, wo_ps[b // 2][:, (b % 2) * D:(b % 2 + 1) * D], c_hi[:, i % 2, c], c_lo[:, i % 2, c],
                           z.wv_hi[:, i], z.wv_lo[:, i], start=(i == 0 and b % 2 == 0), stop=(i == PAIRS - 1))
            mm.then_inc(wo_done, 1)

        def pe_pass(pe, it, first=False, last=False):
            for i in range(PAIRS):
                before, before2 = shifted(it, i, -1, first, last), shifted(it, i, -2, first, last)
                ahead = shifted(it, i, AHEAD, first, last)
                pe_scores(pe, it, i)
                if before:
                    pe_turn(pe, *before, 0)
                if ahead:
                    pe_rot(pe, *ahead)
                    pe_query(pe, *ahead, 0)
                if before:
                    pe_turn(pe, *before, 1)
                if ahead:
                    pe_query(pe, *ahead, 1)
                if before:
                    pe_values(pe, *before, ahead=ahead is not None)
                if before2:
                    pe_out(pe, *before2)

        def act_exp(act, it, i, h):
            S = it * PAIRS + i
            act.wait_ge(max_done, 2 * S + h + 1)
            for b in range(GROUP):
                act.activation(prob[:, i % 2, h, b], sc_ps[h][:, b * P:(b + 1) * P], ACT.Exp, bias=nmax[:, i % 2, h, b:b + 1],
                               accum_out=sums[:, i % 2, h, b:b + 1]).then_inc(exp_done, 1)

        def act_turn(act, it, i, h):
            act.wait_ge(pT_done, 2 * (it * PAIRS + i) + h + 1)
            act.activation(pT[:, h], pT_ps[:], ACT.Copy).then_inc(pT_out, 1)

        def act_values(act, it, i):
            act.wait_ge(pv_done, it * PAIRS + i + 1)
            act.activation(c_hi[:, i % 2], c_ps[:], ACT.Copy).then_inc(c_hid, 1)

        def act_pass(act, it, first=False, last=False):
            for i in range(PAIRS):
                before = shifted(it, i, -1, first, last)
                act_exp(act, it, i, 0)
                if before:
                    act_turn(act, *before, 0)
                    act_turn(act, *before, 1)
                act_exp(act, it, i, 1)
                if before:
                    act_values(act, *before)

        def ve_rot(ve, it, i):
            S = it * PAIRS + i
            ve.wait_ge(rot_proj, S + 1)
            if not known_before(it, i, 1):
                ve.wait_ge(q_sum, 2 * S)
            ve.tensor_tensor(by_batch(rot[:]), by_batch(b_ps[:]), table(T_SIN_Q), ALU.mult).then_inc(rot_done, 1)

        def ve_cos(ve, it, i, h):
            S = it * PAIRS + i
            ve.wait_ge(q_proj, 2 * S + h + 1)
            if not known_before(it, i, AHEAD):
                ve.wait_ge(scores_done, 2 * (S - AHEAD) + h + 1)
            ve.tensor_tensor(by_batch(q[:, i % 2, h]), by_batch(a_ps[h][:]), table((T_EVEN, T_ODD)[h]), ALU.mult).then_inc(cos_done, 1)

        def table(n):
            return z.tab[:, n].unsqueeze(1).broadcast_to([P, GROUP, P])

        def by_batch(a):
            return a.rearrange("p (b c) -> p b c", b=GROUP)

        def ve_rec(ve, it, i, h):
            S = it * PAIRS + i
            ve.wait_ge(exp_done, GROUP * (2 * S + h + 1))
            ve.reciprocal(rec[:, i % 2, h], sums[:, i % 2, h]).then_inc(rec_done, 1)

        def ve_norm_odd(ve, it, i):
            ve.wait_ge(rec_done, 2 * (it * PAIRS + i) + 2)
            ve.tensor_tensor(prob[:, i % 2, 1], prob[:, i % 2, 1], over_groups(rec[:, i % 2, 1]), ALU.mult).then_inc(norm_odd, 1)

        def ve_values(ve, it, i):
            ve.wait_ge(c_hid, it * PAIRS + i + 1)
            ve.tensor_tensor(c_lo[:, i % 2], c_ps[:], c_hi[:, i % 2].bitcast(F32), ALU.subtract).then_inc(c_lod, 1)

        def ve_group_values(ve, it, first):
            if not first:
                ve.wait_ge(pv_done, it * PAIRS)
            ve.tensor_copy(val[:].rearrange("p b c -> p (b c)"),
                           z.val[:, ds(it * GROUP, GROUP)].rearrange("p b c -> p (b c)")).then_inc(val_in, 1)

        def ve_add(ve, it):
            ve.wait_ge(wo_done, it * PAIRS + PAIRS)
            for n in range(2):
                x = e.X[:, ds(it * GROUP + 2 * n, 2)].rearrange("p t d -> p (t d)")
                ve.tensor_tensor(x, wo_ps[n][:], x, ALU.add).then_inc(added, 1)

        def ve_pass(ve, it, first=False, last=False):
            for i in range(PAIRS):
                S = it * PAIRS + i
                before, ahead = shifted(it, i, -1, first, last), shifted(it, i, AHEAD, first, last)
                for h in range(2):
                    ve.wait_ge(scores_done, 2 * S + h + 1)
                    ve.tensor_reduce(nmax[:, i % 2, h], by_batch(sc_ps[h][:]), X_AXIS, ALU.max, negate=True).then_inc(max_done, 1)
                if ahead:
                    ve_rot(ve, *ahead)
                    ve_cos(ve, *ahead, 0)
                ve_rec(ve, it, i, 0)
                if ahead:
                    ve_cos(ve, *ahead, 1)
                ve_rec(ve, it, i, 1)
                ve_norm_odd(ve, it, i)
                if before:
                    ve_values(ve, *before)
                if i == 0:
                    ve_group_values(ve, it, first)
                if i == 1 and not first:
                    ve_add(ve, it - 1)

        def pool_sum(pool, it, i, h):
            S = it * PAIRS + i
            rows = slice(KVC, P) if h == 0 else slice(0, ROPE)
            pool.wait_ge(rot_done, S + 1)
            pool.wait_ge(cos_done, 2 * S + h + 1)
            if h == 1:
                pool.wait_ge(q_sum, 2 * S + 1)
            elif not known_before(it, i, 1):
                pool.wait_ge(q_sum, 2 * S)
                if not known_before(it, i, AHEAD):
                    pool.wait_ge(norm_even, S - AHEAD + 1)
            pool.tensor_tensor(q[rows, i % 2, h], q[rows, i % 2, h], rot[rows, :], ALU.add).then_inc(q_sum, 1)

        def pool_pass(pool, it, first=False, last=False):
            for i in range(PAIRS):
                S = it * PAIRS + i
                ahead = shifted(it, i, AHEAD, first, last)
                pool.wait_ge(rec_done, 2 * S + 1)
                pool.tensor_tensor(prob[:, i % 2, 0], prob[:, i % 2, 0], over_groups(rec[:, i % 2, 0]), ALU.mult).then_inc(norm_even, 1)
                if ahead:
                    pool_sum(pool, *ahead, 0)
                    pool_sum(pool, *ahead, 1)

        with nc.Block() as block:
            @block.gpsimd
            def _(pool):
                for i in range(AHEAD):
                    for h in range(2):
                        pool_sum(pool, 0, i, h)
                pool_pass(pool, 0, first=True)
                with pool.Fori(1, GROUPS - 1) as it:
                    pool_pass(pool, it)
                pool_pass(pool, GROUPS - 1, last=True)

            @block.scalar
            def _(act):
                act_pass(act, 0, first=True)
                with act.Fori(1, GROUPS - 1) as it:
                    act_pass(act, it)
                act_pass(act, GROUPS - 1, last=True)
                for h in range(2):
                    act_turn(act, GROUPS - 1, PAIRS - 1, h)
                act_values(act, GROUPS - 1, PAIRS - 1)

            @block.vector
            def _(ve):
                for i in range(AHEAD):
                    ve_rot(ve, 0, i)
                    ve_cos(ve, 0, i, 0)
                    ve_cos(ve, 0, i, 1)
                ve_pass(ve, 0, first=True)
                with ve.Fori(1, GROUPS - 1) as it:
                    ve_pass(ve, it)
                ve_pass(ve, GROUPS - 1, last=True)
                ve_values(ve, GROUPS - 1, PAIRS - 1)
                ve_add(ve, GROUPS - 1)

            @block.tensor
            def _(pe):
                for i in range(AHEAD):
                    pe_rot(pe, 0, i)
                    pe_query(pe, 0, i, 0)
                    pe_query(pe, 0, i, 1)
                pe_pass(pe, 0, first=True)
                with pe.Fori(1, GROUPS - 1) as it:
                    pe_pass(pe, it)
                pe_pass(pe, GROUPS - 1, last=True)
                for h in range(2):
                    pe_turn(pe, GROUPS - 1, PAIRS - 1, h)
                pe_values(pe, GROUPS - 1, PAIRS - 1, ahead=False)
                pe_out(pe, GROUPS - 1, PAIRS - 2)
                pe_out(pe, GROUPS - 1, PAIRS - 1)


FFN = 1024
BLOCK = 32
FP8_MAX = 448.0
FP8_EPS = 1e-30
FP8_LEAST = 2.0 ** -6
TO_EIGHTHS = 1.5 * 2.0 ** 20
EXPONENT = 0x7F800000


class Quantizer:

    def __init__(self, nc, ctx, tag, width, room=None):
        def sb(name, shape, dt=F32):
            return ctx.enter_context(nc.sbuf_tensor(f"{tag}_{name}", shape, dt))

        n = width // BLOCK
        self.n = n
        self.top, self.scale, self.inverse = sb("top", [P, n]), sb("scale", [P, n]), sb("inverse", [P, n])
        if room is None:
            room = sb("room", [P, 2 * width])
        self.quot, self.magic = room[:, 0:width], room[:, width:2 * width]
        self.scaled, self.quotients, self.rounded, self.whole, self.restored, self.chain = (
            ctx.enter_context(nc.semaphore(f"{tag}_{s}"))
            for s in ("scaled", "quotients", "rounded", "whole", "restored", "chain"))

    def blocks(self, a):
        return a.rearrange("p (n w) -> p n w", w=BLOCK)

    def spread(self, a):
        return a.unsqueeze(2).broadcast_to([P, self.n, BLOCK])

    LINKS = 4

    def link(self, ve, at, k, instruction):
        instruction.then_inc(self.chain, 1)
        ve.wait_ge(self.chain, at * self.LINKS + k)

    def scales(self, ve, at, src):
        self.link(ve, at, 1, ve.tensor_reduce(self.top[:], self.blocks(src), X_AXIS, ALU.max, apply_absolute_value=True))
        if not (isinstance(at, int) and at == 0):
            ve.wait_ge(self.restored, at)
        self.link(ve, at, 2, ve.tensor_scalar(self.scale[:], self.top[:], 1.0 / FP8_MAX, FP8_EPS, ALU.mult, ALU.max))
        ve.reciprocal(self.inverse[:], self.scale[:]).then_inc(self.scaled, 1)

    def quotient(self, pool, at, src):
        pool.wait_ge(self.scaled, at + 1)
        pool.tensor_tensor(self.blocks(self.quot[:]), self.blocks(src), self.spread(self.inverse[:]),
                           ALU.mult).then_inc(self.quotients, 1)

    def round(self, ve, at):
        ve.wait_ge(self.quotients, at + 1)
        self.link(ve, at, 3, ve.tensor_single_scalar(self.magic[:].bitcast(I32), self.quot[:].bitcast(I32), EXPONENT,
                                                     ALU.bitwise_and))
        self.link(ve, at, 4, ve.tensor_scalar(self.magic[:], self.magic[:], FP8_LEAST, TO_EIGHTHS, ALU.max, ALU.mult))
        ve.tensor_tensor(self.quot[:], self.quot[:], self.magic[:], ALU.add).then_inc(self.rounded, 1)

    def restore(self, pool, at, out):
        pool.wait_ge(self.rounded, at + 1)
        pool.tensor_tensor(self.quot[:], self.quot[:], self.magic[:], ALU.subtract).then_inc(self.whole, 1)
        pool.wait_ge(self.whole, at + 1)
        pool.tensor_tensor(self.blocks(out), self.blocks(self.quot[:]), self.spread(self.scale[:]),
                           ALU.mult).then_inc(self.restored, 1)


class RawFfnWeights:

    CHUNKS = 6
    WIDTH = 1024

    def __init__(self, nc, ctx):
        self.raw = ctx.enter_context(nc.sbuf_tensor("fw_raw", [P, self.CHUNKS, self.WIDTH], F32))
        self.w_in = ctx.enter_context(nc.semaphore("fw_in"))


class FfnWeights:
    def __init__(self, nc, ctx):
        def sb(name, shape):
            return ctx.enter_context(nc.sbuf_tensor(f"f_{name}", shape, F32R))

        self.gu_hi, self.gu_lo = sb("gu_hi", [P, 2, KT, FFN]), sb("gu_lo", [P, 2, KT, FFN])
        self.down_hi, self.down_lo = sb("down_hi", [P, FFN // P, D]), sb("down_lo", [P, FFN // P, D])


def phase_ffn_weights(nc, e, raw, w):
    CHUNKS = RawFfnWeights.CHUNKS
    with ExitStack() as ctx:
        bank = [ctx.enter_context(nc.psum_tensor(f"fw_bank{i}", [P, GW], F32)) for i in range(8)]
        turned, hi_done, lo_done = (ctx.enter_context(nc.semaphore(f"fw_{n}")) for n in ("turned", "hi_done", "lo_done"))

        def target(t, c, m):
            if c < 4:
                half = (c % 2) * GW
                return t[0][:, c // 2, m, half:half + GW].rearrange("p (a b) -> p a b", a=GROUP)
            return t[1][:, 4 * m:4 * m + 4, (c - 4) * P:(c - 3) * P]

        his, los = (w.gu_hi, w.down_hi), (w.gu_lo, w.down_lo)

        def halves(c):
            return [(m, bank[2 * (c % 4) + m]) for m in range(2)]

        def by_tile(a):
            return a[:].rearrange("p (a b) -> p a b", a=GROUP)

        with nc.Block() as block:
            @block.tensor
            def _(pe):
                for c in range(CHUNKS):
                    if c >= 4:
                        pe.wait_ge(lo_done, 2 * (c - 3))
                    for m, ps in halves(c):
                        for a in range(GROUP):
                            at = (a * KT + m) * P if c < 4 else (4 * m + a) * P
                            mm = pe.transpose(ps[:, a * P:(a + 1) * P], raw[:, c, at:at + P], e.ident[:])
                    mm.then_inc(turned, 1)

            @block.scalar
            def _(act):
                for c in range(CHUNKS):
                    act.wait_ge(turned, c + 1)
                    for m, ps in halves(c):
                        act.activation(target(his, c, m), by_tile(ps), ACT.Copy).then_inc(hi_done, 1)

            @block.vector
            def _(ve):
                for c in range(CHUNKS):
                    for m, ps in halves(c):
                        ve.wait_ge(hi_done, 2 * c + m + 1)
                        ve.tensor_tensor(target(los, c, m), by_tile(ps), target(his, c, m).bitcast(F32),
                                         ALU.subtract).then_inc(lo_done, 1)


def phase_ffn(nc, e, w, out):
    PASSES = BATCHES // 2
    with ExitStack() as ctx:
        def sb(name, shape, dt=F32):
            return ctx.enter_context(nc.sbuf_tensor(f"o_{name}", shape, dt))

        def sem(name):
            return ctx.enter_context(nc.semaphore(f"o_{name}"))

        st, mv = sb("st", [P, BATCHES, 6]), sb("mv", [P, BATCHES, 2])
        va, rs, nt, nu = (sb(n, [P, BATCHES]) for n in ("va", "rs", "nt", "nu"))
        xn = sb("xn", [P, 2, D])
        xT_hi, xT_lo = sb("xT_hi", [P, 2, KT, P], F32R), sb("xT_lo", [P, 2, KT, P], F32R)
        act_out = sb("act_out", [P, FFN])
        inner = sb("inner", [P, 2, FFN])
        iT_hi, iT_lo = sb("iT_hi", [P, FFN // P, P], F32R), sb("iT_lo", [P, FFN // P, P], F32R)
        bank = [ctx.enter_context(nc.psum_tensor(f"o_bank{i}", [P, GW], F32)) for i in range(8)]
        g_ps, u_ps, xT_ps, iT_ps, o_ps = bank[0:2], bank[2:4], bank[4], bank[5:7], bank[7]
        qx, qi = Quantizer(nc, ctx, "ox", D), Quantizer(nc, ctx, "oi", FFN)

        stats_chain, ready, x_turned, x_hid, x_lod = (sem(n) for n in ("stats", "ready", "x_turned", "x_hid", "x_lod"))
        up_done, silu_done, inner_done = sem("up_done"), sem("silu_done"), sem("inner_done")
        i_turned, i_hid, i_lod, down_done, added, stored = (sem(n) for n in ("i_turned", "i_hid", "i_lod", "down_done", "added", "stored"))

        def tile_of(x, t):
            return x[:, ds(t, 1)].rearrange("p a d -> p (a d)")

        def first_tile(t):
            return isinstance(t, int) and t == 0

        def ve_input_a(ve, t, par):
            if not (isinstance(t, int) and t < 2):
                ve.wait_ge(x_turned, t - 1)
            ve.tensor_scalar(xn[:, par], tile_of(e.X, t), mv[:, ds(t, 1), 0], rs[:, ds(t, 1)], ALU.subtract, ALU.mult)\
                .then_inc(ready, 1)
            ve.wait_ge(ready, t + 1)
            qx.scales(ve, t, xn[:, par])

        def ve_input_b(ve, t, par):
            qx.round(ve, t)

        def ve_input_c(ve, t, par):
            ve.wait_ge(x_hid, t + 1)
            ve.tensor_tensor(xT_lo[:, par].rearrange("p k c -> p (k c)"), xT_ps[:, 0:D],
                             xT_hi[:, par].rearrange("p k c -> p (k c)").bitcast(F32), ALU.subtract).then_inc(x_lod, 1)

        def pool_input_a(pool, t, par):
            qx.quotient(pool, t, xn[:, par])

        def pool_input_b(pool, t, par):
            qx.restore(pool, t, xn[:, par])

        def pe_input(pe, t, par):
            pe.wait_ge(qx.restored, t + 1)
            if not first_tile(t):
                pe.wait_ge(x_lod, t)
            for k in range(KT):
                mm = pe.transpose(xT_ps[:, k * P:(k + 1) * P], xn[:, par, k * P:(k + 1) * P], e.ident[:])
            mm.then_inc(x_turned, 1)

        def act_input(act, t, par):
            act.wait_ge(x_turned, t + 1)
            if not (isinstance(t, int) and t < 2):
                act.wait_ge(up_done, 2 * t - 2)
            act.activation(xT_hi[:, par].rearrange("p k c -> p (k c)"), xT_ps[:, 0:D], ACT.Copy).then_inc(x_hid, 1)

        def pe_up(pe, t, par):
            pe.wait_ge(x_lod, t + 1)
            if not first_tile(t):
                pe.wait_ge(silu_done, 2 * t)
                pe.wait_ge(inner_done, 2 * t)
            for half in range(2):
                cols = slice(half * GW, (half + 1) * GW)
                for a, ps in ((0, g_ps[half]), (1, u_ps[half])):
                    for k in range(KT):
                        mm = parts(pe, ps[:], xT_hi[:, par, k], xT_lo[:, par, k], w.gu_hi[:, a, k, cols], w.gu_lo[:, a, k, cols],
                                   start=(k == 0), stop=(k == KT - 1))
                mm.then_inc(up_done, 1)

        def act_silu(act, t, par):
            for half in range(2):
                act.wait_ge(up_done, 2 * t + half + 1)
                if not first_tile(t):
                    act.wait_ge(inner_done, 2 * t - 1 + half)
                act.activation(act_out[:, half * GW:(half + 1) * GW], g_ps[half][:], ACT.Silu).then_inc(silu_done, 1)

        def ve_inner(ve, t, par):
            if not (isinstance(t, int) and t < 2):
                ve.wait_ge(i_turned, t - 1)
            for half in range(2):
                cols = slice(half * GW, (half + 1) * GW)
                ve.wait_ge(silu_done, 2 * t + half + 1)
                ve.tensor_tensor(inner[:, par, cols], u_ps[half][:], act_out[:, cols], ALU.mult).then_inc(inner_done, 1)
            ve.wait_ge(inner_done, 2 * t + 2)
            qi.scales(ve, t, inner[:, par])

        def pe_turn(pe, t, par):
            pe.wait_ge(qi.restored, t + 1)
            if not first_tile(t):
                pe.wait_ge(i_lod, 2 * t)
            for half in range(2):
                for a in range(GROUP):
                    i = half * GROUP + a
                    mm = pe.transpose(iT_ps[half][:, a * P:(a + 1) * P], inner[:, par, i * P:(i + 1) * P], e.ident[:])
            mm.then_inc(i_turned, 1)

        def act_turn(act, t):
            act.wait_ge(i_turned, t + 1)
            if not first_tile(t):
                act.wait_ge(down_done, t)
            for half in range(2):
                act.activation(iT_hi[:, 4 * half:4 * half + 4].rearrange("p a c -> p (a c)"), iT_ps[half][:], ACT.Copy).then_inc(i_hid, 1)

        def ve_turn(ve, t):
            for half in range(2):
                ve.wait_ge(i_hid, 2 * t + half + 1)
                ve.tensor_tensor(iT_lo[:, 4 * half:4 * half + 4].rearrange("p a c -> p (a c)"), iT_ps[half][:],
                                 iT_hi[:, 4 * half:4 * half + 4].rearrange("p a c -> p (a c)").bitcast(F32),
                                 ALU.subtract).then_inc(i_lod, 1)

        def pe_down(pe, t):
            if not first_tile(t):
                pe.wait_ge(added, t)
            for i in range(FFN // P):
                if i % GROUP == 0:
                    pe.wait_ge(i_lod, 2 * t + i // GROUP + 1)
                mm = parts(pe, o_ps[:, 0:D], iT_hi[:, i], iT_lo[:, i], w.down_hi[:, i], w.down_lo[:, i],
                           start=(i == 0), stop=(i == FFN // P - 1))
            mm.then_inc(down_done, 1)

        def ve_add(ve, t):
            ve.wait_ge(down_done, t + 1)
            x = tile_of(e.X, t)
            ve.tensor_tensor(x, o_ps[:, 0:D], x, ALU.add).then_inc(added, 1)

        def each(it):
            for par in range(2):
                t = 2 * it + par
                near = isinstance(t, int)
                yield t, par, None if near and t < 2 else t - 2, *(
                    None if near and t + n >= BATCHES else t + n for n in (1, 2, 3))

        def pe_pass(pe, it):
            for t, par, before, after, _, _ in each(it):
                if before is not None:
                    pe_turn(pe, before, par)
                pe_up(pe, t, par)
                if after is not None:
                    pe_input(pe, after, 1 - par)
                if before is not None:
                    pe_down(pe, before)

        def act_pass(act, it):
            for t, par, before, after, _, _ in each(it):
                if before is not None:
                    act_turn(act, before)
                act_silu(act, t, par)
                if after is not None:
                    act_input(act, after, 1 - par)

        def ve_pass(ve, it):
            for t, par, before, after, second, third in each(it):
                if before is not None:
                    ve_turn(ve, before)
                ve_inner(ve, t, par)
                if after is not None:
                    ve_input_c(ve, after, 1 - par)
                if second is not None:
                    ve_input_b(ve, second, par)
                qi.round(ve, t)
                if third is not None:
                    ve_input_a(ve, third, 1 - par)
                if before is not None:
                    ve_add(ve, before)

        def pool_pass(pool, it):
            for t, par, _, _, second, third in each(it):
                qi.quotient(pool, t, inner[:, par])
                if second is not None:
                    pool_input_b(pool, second, par)
                qi.restore(pool, t, inner[:, par])
                if third is not None:
                    pool_input_a(pool, third, 1 - par)

        def passes(engine, one_pass):
            one_pass(engine, 0)
            one_pass(engine, 1)
            with engine.Fori(2, PASSES - 2) as it:
                one_pass(engine, it)
            one_pass(engine, PASSES - 2)
            one_pass(engine, PASSES - 1)

        with nc.Block() as block:
            @block.vector
            def _(ve):
                links = [0]

                def link(instruction):
                    links[0] += 1
                    instruction.then_inc(stats_chain, 1)
                    ve.wait_ge(stats_chain, links[0])

                for t in range(BATCHES):
                    last = ve.bn_stats(st[:, t], e.X[:, t])
                link(last)
                for t in range(BATCHES):
                    last = ve.bn_aggr(mv[:, t], st[:, t])
                link(last)
                link(ve.tensor_scalar(va[:], mv[:, :, 1], LN_EPS, None, ALU.add))
                rsqrt_steps(ve, link, va[:], rs[:], nt[:], nu[:])
                for t in range(2):
                    ve_input_a(ve, t, t)
                    ve_input_b(ve, t, t)
                ve_input_c(ve, 0, 0)
                ve_input_a(ve, 2, 0)
                passes(ve, ve_pass)
                for t in range(BATCHES - 2, BATCHES):
                    ve_turn(ve, t)
                    ve_add(ve, t)

            @block.gpsimd
            def _(pool):
                for t in range(2):
                    pool_input_a(pool, t, t)
                    pool_input_b(pool, t, t)
                pool_input_a(pool, 2, 0)
                passes(pool, pool_pass)

            @block.scalar
            def _(act):
                act_input(act, 0, 0)
                passes(act, act_pass)
                for t in range(BATCHES - 2, BATCHES):
                    act_turn(act, t)

            @block.tensor
            def _(pe):
                pe_input(pe, 0, 0)
                passes(pe, pe_pass)
                for t in range(BATCHES - 2, BATCHES):
                    pe_turn(pe, t, t % 2)
                    pe_down(pe, t)

            @block.sync
            def _(sp):
                with sp.Fori(0, BATCHES) as t:
                    sp.wait_ge(added, t + 1)
                    sp.dma_start(out[ds(t, 1)].rearrange("a p d -> p (a d)"), tile_of(e.X, t)).then_inc(stored, 16)
                sp.wait_ge(stored, 16 * BATCHES)


def attention_state(nc, ctx):
    w = Env()

    def sb(name, shape, dt=F32):
        return ctx.enter_context(nc.sbuf_tensor(name, shape, dt))

    w.hT_hi = sb("hT_hi", [P, KT, BATCHES * P], F32R)
    w.hT_lo = sb("hT_lo", [P, KT, BATCHES * P], F32R)
    w.raw = sb("w_raw", [P, 2, 4, KT, D])
    w.hi = sb("w_hi", [P, 2, 4, KT, D], F32R)
    w.lo = sb("w_lo", [P, 2, 4, KT, D], F32R)
    w.causal32 = sb("causal32", [P, P])
    w.causal = sb("causal", [P, P], F32R)
    w.ln1 = sb("ln1", [P, KT])
    return w


def clear_semaphores(nc):
    used = sorted(nc.released_uncleared_semaphores)
    with nc.Block() as block:
        @block.gpsimd
        def _(pool):
            pool.sem_clear(range(used[0], used[-1] + 1))


def build_program(nc, ins, out):
    with ExitStack() as ctx:
        e = constants_and_state(nc, ctx, ins)
        fw = RawFfnWeights(nc, ctx)
        with ExitStack() as c0:
            mw = MoeWeights(nc, c0)
            e.Y = c0.enter_context(nc.sbuf_tensor("Y", [P, BATCHES, D], F32))
            with ExitStack() as c1:
                w = attention_state(nc, c1)
                phase_a(nc, e, ins, w, mw, fw)
                phase_attention(nc, e, ins, w, mw, fw)
            phase_moe(nc, e, ins, mw)
        with ExitStack() as c2:
            z = LatentState(nc, c2)
            phase_latent_keys(nc, e, ins, z)
            qc_hi = c2.enter_context(nc.sbuf_tensor("qc_hi", [QC, BATCHES * P], F32R))
            qc_lo = c2.enter_context(nc.sbuf_tensor("qc_lo", [QC, BATCHES * P], F32R))
            phase_latent_queries(nc, e, ins, z, qc_hi, qc_lo)
            phase_latent_attention(nc, e, z, qc_hi, qc_lo)
        with ExitStack() as c3:
            wf = FfnWeights(nc, c3)
            clear_semaphores(nc)
            phase_ffn_weights(nc, e, fw.raw, wf)
            phase_ffn(nc, e, wf, out)


def layouts(i):
    import numpy as np

    def by_pair(m):
        return m.reshape(KT, P, PAIRS, 2 * HD).transpose(1, 2, 0, 3)

    fill = np.zeros((TILES * P - EXPERTS * EI - SI, D), np.float32)

    def rows(experts, shared):
        return np.concatenate([experts.reshape(EXPERTS * EI, D), shared, fill]).reshape(TILES, P, D)

    up = [rows(i["L0_ffn_eg_w"], i["L0_ffn_sg_w"]), rows(i["L0_ffn_eu_w"], i["L0_ffn_su_w"])]
    up = [m.reshape(TILES, P, KT, P).transpose(3, 0, 2, 1).reshape(P, TILES, KT * P) for m in up]
    down = rows(i["L0_ffn_ed_w"].transpose(0, 2, 1), i["L0_ffn_sd_w"].T).transpose(1, 0, 2)
    owner = np.minimum(np.arange(TILES * P) // EI, EXPERTS)
    sel = (np.arange(P)[:, None] == owner[None]).astype(np.float32).reshape(P, TILES, P)
    w_moe = np.concatenate([*up, down, sel], axis=2)
    wo = i["L0_ffn_wo"].reshape(PAIRS, 2, P, D).transpose(2, 0, 1, 3)
    inv = (1.0 / np.float32(10000.0) ** (np.arange(HALF, dtype=np.float32) / np.float32(HALF))).astype(np.float32)
    ang = (inv[:, None] * np.arange(P, dtype=np.float32)[None]).astype(np.float32)
    cos = np.tile(np.cos(ang), (2 * P // ROPE, 1))
    sin = np.tile(np.concatenate([-np.sin(ang), np.sin(ang)]), (P // ROPE, 1))
    one = np.ones((KVC, P), np.float32)
    scale = np.float32(1.0) / np.sqrt(np.float32(HD + ROPE))
    key = np.tile(np.arange(P, dtype=np.float32), (P, 1))
    tab = np.stack([scale * np.concatenate([one, cos[KVC:]]), scale * np.concatenate([cos[:ROPE], one]), scale * sin,
                    cos, sin, key], axis=1).astype(np.float32)

    def swap(m):
        return np.concatenate([m[..., HALF:], m[..., :HALF]], axis=-1)

    qr = i["L1_xattn_W_qr"].reshape(QC, HEADS, ROPE)
    kr = i["L1_xattn_W_kr"]
    kvc = i["L1_xattn_W_kvc"].reshape(KT, P, KVC).transpose(1, 0, 2)
    gate, up = (i[f"L1_ffn_{n}_w"].reshape(2, GROUP, P, D).transpose(2, 0, 1, 3).reshape(P, 2, GROUP * D)
                for n in ("gate", "up"))
    down = i["L1_ffn_down_w"].reshape(KT, P, FFN).transpose(1, 0, 2)
    return {
        "w_ffn": np.concatenate([gate, up, down], axis=1),
        "uqT": i["L1_xattn_W_uq"].reshape(QC, HEADS, HD).transpose(2, 1, 0),
        "ukT": i["L1_xattn_W_uk"].reshape(KVC, HEADS, HD).transpose(2, 1, 0),
        "uvT": i["L1_xattn_W_uv"].reshape(KVC, HEADS, HD).transpose(2, 1, 0),
        "w_o2": i["L1_xattn_W_o"].reshape(HEADS, HD, D).transpose(1, 0, 2),
        "wkvc": np.concatenate([kvc, kvc], axis=2),
        "wkr": np.stack([np.concatenate([kr, kr], axis=1), np.concatenate([swap(kr), swap(kr)], axis=1)], axis=1),
        "qr": qr,
        "qrb": np.concatenate([swap(qr[:, 1::2]), swap(qr[:, 0::2])], axis=2),
        "wdq": i["L1_xattn_W_dq"].reshape(KT, P, QC).transpose(1, 0, 2),
        "seg": i["itok_BxS_0_1023"].T,
        "tab": tab,
        "ln2": i["L0_ffn_ln2_w"].reshape(KT, P).T,
        "gate": i["L0_ffn_gate_w"].T.reshape(KT, P, EXPERTS).transpose(1, 0, 2),
        "w_moe": w_moe,
        "x": i["x"],
        "ctx": i["ctx_2048"],
        "ctxT": i["ctx_2048"].reshape(-1, D).T,
        "mask": i["mask_BxS2_bk0"],
        "ln1": i["L0_ffn_ln1_w"].reshape(KT, P).T,
        "w_attn": np.stack([by_pair(i["L0_ffn_wq"]), by_pair(i["L0_ffn_wk"]), by_pair(i["L0_ffn_wv"]), wo], axis=2),
    }


def kernel(**inputs):
    import numpy as _np
    import concourse.bacc as _bacc
    from concourse import mybir as _mybir
    from concourse.bass_utils import run_bass_kernel_spmd as _run

    nc = _bacc.Bacc("TRN2", target_bir_lowering=False, num_devices=1)
    arrays = {"in_" + k: _np.ascontiguousarray(v) for k, v in layouts({k: _np.asarray(v) for k, v in inputs.items()}).items()}
    ins = {k[3:]: nc.dram_tensor(k, v.shape, _mybir.dt.from_np(v.dtype), kind="ExternalInput").ap()
           for k, v in arrays.items()}
    out = nc.dram_tensor("out_x", (BATCHES, P, D), F32, kind="ExternalOutput").ap()
    build_program(nc, ins, out)
    r = _run(nc, [arrays], core_ids=[0])
    return r.results[0]["out_x"]
```

```python
from contextlib import ExitStack

import concourse.bass as bass
from concourse import mybir

F32 = mybir.dt.float32
F32R = mybir.dt.float32r
I32 = mybir.dt.int32
U8 = mybir.dt.uint8
ALU = mybir.AluOpType
ACT = mybir.ActivationFunctionType
X_AXIS = mybir.AxisListType.X
ds = bass.ds

P = 128
BATCHES = 16
D = 256
KT = D // P
GROUP = 4
GROUPS = BATCHES // GROUP
GW = GROUP * P

HEADS = 16
HD = 128
PAIRS = HEADS // 2
LN_EPS = 1e-5
RMS_EPS = 1e-6


class Env:
    pass


def constants_and_state(nc, ctx, ins):
    e = Env()

    def sb(name, shape, dt=F32):
        return ctx.enter_context(nc.sbuf_tensor(name, shape, dt))

    e.X = sb("X", [P, BATCHES, D])
    e.stats = sb("stats", [P, BATCHES, 6])
    e.ident = sb("ident", [P, P])
    e.ident_r = sb("ident_r", [P, P], F32R)
    e.one = sb("one", [P, 1])
    return e


def copy_pool(pool, e, out, src):
    return pool.tensor_tensor(out, src, e.one[:, 0:1].broadcast_to(list(src.shape)), ALU.mult)


def rsqrt_steps(ve, link, var, y, t, u, last=None):
    link(ve.tensor_scalar(y.bitcast(I32), var.bitcast(I32), -0.5, 1597463007.0, ALU.mult, ALU.add))
    for n in range(3):
        link(ve.scalar_tensor_tensor(out=t, in0=y, scalar=-0.5, in1=y, op0=ALU.mult, op1=ALU.mult))
        link(ve.tensor_tensor(u, t, var, ALU.mult))
        (last if last and n == 2 else link)(
            ve.scalar_tensor_tensor(out=y, in0=u, scalar=1.5, in1=y, op0=ALU.add, op1=ALU.mult))


def over_groups(a):
    return a.unsqueeze(2).broadcast_to([P, GROUP, P])


def phase_a(nc, e, ins, w, mw, fw):
    HALF_TILES = BATCHES // 2
    with ExitStack() as ctx:
        def sb(name, shape, dt=F32):
            return ctx.enter_context(nc.sbuf_tensor(f"a_{name}", shape, dt))

        def sem(name):
            return ctx.enter_context(nc.semaphore(f"a_{name}"))

        ctxn = sb("ctxn", [P, BATCHES, D])
        later = fw.raw[:].rearrange("p c w -> p (c w)")
        ctxT = later[:, 0:KT * BATCHES * P].rearrange("p (k t) -> p k t", k=KT)
        mask8 = sb("mask8", [P, BATCHES * P], U8)
        mbias = mw.hi[:].rearrange("p j c -> p (j c)")[:, 0:BATCHES * P]
        valid = sb("valid", [P, BATCHES])
        st, mv = sb("st", [P, BATCHES, 6]), sb("mv", [P, BATCHES, 2])
        va, rs, rr, nt, nu, nmax, sums, rec = (
            sb(n, [P, BATCHES]) for n in ("va", "rs", "rr", "nt", "nu", "nmax", "sums", "rec"))
        xn = sb("xn", [P, 2, GROUP, D])
        lnT = later[:, KT * BATCHES * P:KT * (BATCHES * P + 2 * GW)].rearrange("p (a k c) -> p a k c", a=2, k=KT)
        prob = sb("prob", [P, 2, GROUP, P])
        probT = sb("probT", [P, 2, GW])
        bank = [ctx.enter_context(nc.psum_tensor(f"a_bank{i}", [P, GW], F32)) for i in range(8)]
        xT_ps, sc_ps, pT_ps, av_ps = bank[0:2], bank[2:4], bank[6:8], bank[4:6]
        hT_ps = (bank[0:2], bank[2:4])

        x_in = [sem(f"x_in{g}") for g in range(GROUPS)]
        ctx_in, ctxT_in, small_in, w_in = sem("ctx_in"), sem("ctxT_in"), sem("small_in"), sem("w_in")
        zeroed, ident_done, consts, bias_done, w_hi = (sem(n) for n in ("zeroed", "ident", "consts", "bias", "w_hi"))
        chain, valid_done, ln_ready, ln_out, x_turned, lnT_out = (
            sem(n) for n in ("chain", "valid_done", "ln_ready", "ln_out", "x_turned", "lnT_out"))
        scores_done, max_done, exp_done, pT_done, pT_out, av_done, x_added = (
            sem(n) for n in ("scores", "max", "exp", "pT_done", "pT_out", "av", "x_added"))
        y_ready, rms_ready, h_in, h_turned, h_hi, h_lo = (
            sem(n) for n in ("y_ready", "rms_ready", "h_in", "h_turned", "h_hi", "h_lo"))

        with nc.Block() as block:
            @block.sync
            def _(sp):
                for g in range(GROUPS):
                    tiles = slice(g * GROUP, (g + 1) * GROUP)
                    sp.dma_start(e.X[:, tiles], ins["x"][tiles].rearrange("b p d -> p b d")).then_inc(x_in[g], 16)
                sp.dma_start(ctxn[:], ins["ctx"].rearrange("b p d -> p b d")).then_inc(ctx_in, 16)
                sp.dma_start(w.raw[:], ins["w_attn"][:, 0:2]).then_inc(w_in, 16)

            @block.gpsimd
            def _(pool):
                pool.memset(e.one[:], 1.0)
                pool.memset(e.ident[:], 0.0).then_inc(zeroed, 1)
                pool.wait_ge(zeroed, 1)
                pool.affine_select(out=e.ident[:], in_=e.ident[:], compare_op=ALU.not_equal, fill=1.0, base=0,
                                   pattern=[[-1, P]], channel_multiplier=1).then_inc(ident_done, 1)
                pool.memset(w.causal[:], 0.0).then_inc(zeroed, 1)
                pool.wait_ge(zeroed, 2)
                pool.affine_select(out=w.causal[:], in_=w.causal[:], compare_op=ALU.is_ge, fill=-1.0e9, base=0,
                                   pattern=[[-1, P]], channel_multiplier=1).then_inc(zeroed, 1)
                pool.wait_ge(zeroed, 3)
                pool.wait_ge(ident_done, 1)
                pool.tensor_scalar(e.ident_r[:], e.ident[:], 1.0, None, ALU.mult).then_inc(consts, 1)
                pool.wait_ge(small_in, 32)
                pool.tensor_scalar(mbias, mask8[:], 1.0e30, -1.0e30, ALU.mult, ALU.add).then_inc(bias_done, 1)
                pool.wait_ge(w_in, 16)
                for n in range(2):
                    pool.tensor_scalar(w.hi[:, n], w.raw[:, n], 1.0, None, ALU.mult).then_inc(w_hi, 1)
                for n in range(2):
                    pool.wait_ge(w_hi, n + 1)
                    pool.tensor_tensor(w.lo[:, n], w.raw[:, n], w.hi[:, n].bitcast(F32), ALU.subtract)

            def act_lnT(act, g):
                act.wait_ge(x_turned, g + 1)
                if g >= 2:
                    act.wait_ge(scores_done, g - 1)
                for k in range(KT):
                    act.activation(lnT[:, g % 2, k], xT_ps[k][:], ACT.Copy, scale=float(D) ** -0.5).then_inc(lnT_out, 1)

            def act_exp(act, g):
                act.wait_ge(max_done, g + 1)
                if g >= 2:
                    act.wait_ge(pT_done, g - 1)
                for b in range(GROUP):
                    t = g * GROUP + b
                    act.activation(prob[:, g % 2, b], sc_ps[g % 2][:, b * P:(b + 1) * P], ACT.Exp, bias=nmax[:, t:t + 1],
                                   accum_out=sums[:, t:t + 1]).then_inc(exp_done, 1)

            def act_pT(act, g):
                act.wait_ge(pT_done, g + 1)
                if g >= 2:
                    act.wait_ge(av_done, g - 1)
                act.activation(probT[:, g % 2], pT_ps[g % 2][:], ACT.Copy).then_inc(pT_out, 1)

            def act_h(act, g):
                act.wait_ge(y_ready, g // 2 + 1)
                act.wait_ge(rms_ready, g // 2 + 1)
                if g < 2:
                    act.wait_ge(x_turned, GROUPS - 1 + g)
                else:
                    act.wait_ge(h_turned, g - 1)
                for b in range(GROUP):
                    t = g * GROUP + b
                    last = act.activation(xn[:, g % 2, b], e.Y[:, t], ACT.Copy, scale=rr[:, t:t + 1])
                last.then_inc(h_in, 1)

            @block.scalar
            def _(act):
                act.dma_start(mask8[:], ins["mask"].rearrange("b m -> (b m)").partition_broadcast(P)).then_inc(small_in, 16)
                act.dma_start(w.ln1[:], ins["ln1"]).then_inc(small_in, 16)
                act.dma_start(ctxT, ins["ctxT"].rearrange("(k p) t -> p k t", p=P)).then_inc(ctxT_in, 16)
                for i in range(GROUPS + 2):
                    for step, g in ((act_lnT, i), (act_exp, i - 1), (act_pT, i - 2)):
                        if 0 <= g < GROUPS:
                            step(act, g)
                act.wait_ge(small_in, 32)
                act_h(act, 0)
                for g in range(GROUPS):
                    if g + 1 < GROUPS:
                        act_h(act, g + 1)
                    act.wait_ge(h_turned, g + 1)
                    for k in range(KT):
                        act.activation(w.hT_hi[:, k, g * GW:(g + 1) * GW], hT_ps[g % 2][k][:], ACT.Copy,
                                       scale=w.ln1[:, k:k + 1]).then_inc(h_hi, 1)

            def pe_turn_x(pe, g):
                pe.wait_ge(ln_out, g + 1)
                if g >= 1:
                    pe.wait_ge(lnT_out, KT * g)
                for k in range(KT):
                    for b in range(GROUP):
                        mm = pe.transpose(xT_ps[k][:, b * P:(b + 1) * P], xn[:, g % 2, b, k * P:(k + 1) * P], e.ident[:])
                mm.then_inc(x_turned, 1)

            def pe_scores(pe, g):
                pe.wait_ge(lnT_out, KT * g + KT)
                if g == 0:
                    pe.wait_ge(ctxT_in, 16)
                    pe.wait_ge(bias_done, 1)
                if g >= 2:
                    pe.wait_ge(exp_done, GROUP * (g - 1))
                for b in range(GROUP):
                    t = g * GROUP + b
                    for k in range(KT):
                        pe.matmul(sc_ps[g % 2][:, b * P:(b + 1) * P], lnT[:, g % 2, k, b * P:(b + 1) * P],
                                  ctxT[:, k, t * P:(t + 1) * P], start=(b == 0 and k == 0), stop=False,
                                  skip_group_check=True)
                pe.matmul(sc_ps[g % 2][:], e.ident_r[:], mbias[:, g * GW:(g + 1) * GW], start=False, stop=True,
                          skip_group_check=True).then_inc(scores_done, 1)

            def pe_turn_p(pe, g):
                pe.wait_ge(exp_done, GROUP * g + GROUP)
                if g >= 2:
                    pe.wait_ge(pT_out, g - 1)
                for b in range(GROUP):
                    mm = pe.transpose(pT_ps[g % 2][:, b * P:(b + 1) * P], prob[:, g % 2, b], e.ident[:])
                mm.then_inc(pT_done, 1)

            def pe_av(pe, g):
                pe.wait_ge(pT_out, g + 1)
                if g == 0:
                    pe.wait_ge(ctx_in, 16)
                if g >= 1:
                    pe.wait_ge(x_added, g)
                for b in range(GROUP):
                    mm = pe.matmul(av_ps[b // 2][:, (b % 2) * D:(b % 2 + 1) * D], probT[:, g % 2, b * P:(b + 1) * P],
                                   ctxn[:, g * GROUP + b], start=(b % 2 == 0), stop=True, skip_group_check=True)
                mm.then_inc(av_done, 1)

            @block.tensor
            def _(pe):
                pe.wait_ge(ident_done, 1)
                pe.wait_ge(consts, 1)
                for i in range(GROUPS + 3):
                    for step, g in ((pe_turn_x, i), (pe_scores, i - 1), (pe_turn_p, i - 2), (pe_av, i - 3)):
                        if 0 <= g < GROUPS:
                            step(pe, g)
                for g in range(GROUPS):
                    pe.wait_ge(h_in, g + 1)
                    if g >= 2:
                        pe.wait_ge(h_lo, KT * (g - 1))
                    for k in range(KT):
                        for b in range(GROUP):
                            mm = pe.transpose(hT_ps[g % 2][k][:, b * P:(b + 1) * P], xn[:, g % 2, b, k * P:(k + 1) * P],
                                              e.ident[:])
                    mm.then_inc(h_turned, 1)

            @block.vector
            def _(ve):
                links = [0]

                def link(instruction):
                    links[0] += 1
                    instruction.then_inc(chain, 1)
                    ve.wait_ge(chain, links[0])

                def statistics(half, last):
                    tiles = range(half * HALF_TILES, (half + 1) * HALF_TILES)
                    cols = slice(half * HALF_TILES, (half + 1) * HALF_TILES)
                    for t in tiles:
                        if last is not None and t % GROUP == 0:
                            ve.wait_ge(x_in[t // GROUP], 16)
                        done = ve.bn_stats(st[:, t], e.X[:, t])
                    link(done)
                    for t in tiles:
                        done = ve.bn_aggr(mv[:, t], st[:, t])
                    link(done)
                    link(ve.tensor_scalar(va[:, cols], mv[:, cols, 1], LN_EPS, None, ALU.add))
                    rsqrt_steps(ve, link, va[:, cols], rs[:, cols], nt[:, cols], nu[:, cols], last)

                def maxima(g):
                    ve.wait_ge(scores_done, g + 1)
                    ve.tensor_reduce(nmax[:, g * GROUP:(g + 1) * GROUP], sc_ps[g % 2][:].rearrange("p (b m) -> p b m", b=GROUP),
                                     X_AXIS, ALU.max, negate=True).then_inc(max_done, 1)

                def finish(g):
                    cols = slice(g * GROUP, (g + 1) * GROUP)
                    ve.wait_ge(exp_done, GROUP * g + GROUP)
                    link(ve.reciprocal(rec[:, cols], sums[:, cols]))
                    link(ve.tensor_tensor(rec[:, cols], rec[:, cols], valid[:, cols], ALU.mult))
                    ve.wait_ge(av_done, g + 1)
                    for b in range(GROUP):
                        t = g * GROUP + b
                        done = ve.scalar_tensor_tensor(out=e.X[:, t], in0=av_ps[b // 2][:, (b % 2) * D:(b % 2 + 1) * D],
                                                       scalar=rec[:, t:t + 1], in1=e.X[:, t], op0=ALU.mult, op1=ALU.add)
                    done.then_inc(x_added, 1)

                def normalise(half):
                    cols = slice(half * HALF_TILES, (half + 1) * HALF_TILES)
                    ve.wait_ge(x_added, 2 * half + 2)
                    statistics(half, None)
                    for t in range(half * HALF_TILES, (half + 1) * HALF_TILES):
                        done = ve.tensor_scalar(e.Y[:, t], e.X[:, t], mv[:, t, 0:1], rs[:, t:t + 1], ALU.subtract, ALU.mult)
                    done.then_inc(y_ready, 1)
                    link(ve.tensor_tensor(nt[:, cols], rs[:, cols], rs[:, cols], ALU.mult))
                    link(ve.tensor_tensor(nt[:, cols], nt[:, cols], mv[:, cols, 1], ALU.mult))
                    link(ve.tensor_scalar(va[:, cols], nt[:, cols], RMS_EPS, None, ALU.add))
                    rsqrt_steps(ve, link, va[:, cols], rr[:, cols], nt[:, cols], nu[:, cols],
                                lambda instruction: instruction.then_inc(rms_ready, 1))

                for half in range(2):
                    statistics(half, lambda instruction: instruction.then_inc(ln_ready, 1))
                    ve.wait_ge(ln_ready, half + 1)
                    for g in (2 * half, 2 * half + 1):
                        if g >= 2:
                            ve.wait_ge(x_turned, g - 1)
                        for b in range(GROUP):
                            t = g * GROUP + b
                            done = ve.tensor_scalar(xn[:, g % 2, b], e.X[:, t], mv[:, t, 0:1], rs[:, t:t + 1],
                                                    ALU.subtract, ALU.mult)
                        done.then_inc(ln_out, 1)
                ve.wait_ge(small_in, 32)
                ve.tensor_reduce(valid[:], mask8[:].rearrange("p (b m) -> p b m", b=BATCHES), X_AXIS, ALU.max).then_inc(valid_done, 1)
                ve.wait_ge(valid_done, 1)
                maxima(0)
                maxima(1)
                for g in range(GROUPS):
                    finish(g)
                    if g + 2 < GROUPS:
                        maxima(g + 2)
                    if g == 1:
                        normalise(0)
                normalise(1)
                for g in range(GROUPS):
                    for k in range(KT):
                        ve.wait_ge(h_hi, KT * g + k + 1)
                        hi = w.hT_hi[:, k, g * GW:(g + 1) * GW]
                        ve.scalar_tensor_tensor(out=w.hT_lo[:, k, g * GW:(g + 1) * GW], in0=hT_ps[g % 2][k][:],
                                                scalar=w.ln1[:, k:k + 1], in1=hi.bitcast(F32), op0=ALU.mult,
                                                op1=ALU.subtract).then_inc(h_lo, 1)


def phase_attention(nc, e, ins, w, mw, fw):
    STEPS = 2 * GROUPS
    PASSES = PAIRS // 2
    UNITS = 6
    RING = 4
    with ExitStack() as ctx:
        def sb(name, shape, dt=F32):
            return ctx.enter_context(nc.sbuf_tensor(name, shape, dt))

        def sem(name):
            return ctx.enter_context(nc.semaphore(name))

        qk = sb("qk", [P, 4, GW])
        v = sb("v", [P, 2, GROUP, 2 * HD])
        prob = sb("b_prob", [P, 2, GROUP, P])
        b_probT = sb("b_probT", [P, 2, GW])
        ao_hi = sb("ao_hi", [P, 2, GW], F32R)
        ao_lo = sb("ao_lo", [P, 2, GW], F32R)
        nmax = sb("b_nmax", [P, 2, 2, GROUP])
        sums = sb("b_sums", [P, 2, 2, GROUP])
        rec = sb("b_rec", [P, 2, 2, GROUP])
        ring = [ctx.enter_context(nc.psum_tensor(f"b_ring{i}", [P, GW], F32)) for i in range(RING)]
        sc_ps = [ctx.enter_context(nc.psum_tensor(f"b_sc{i}", [P, GW], F32)) for i in range(2)]
        wo_ps = [ctx.enter_context(nc.psum_tensor(f"b_wo{i}", [P, GW], F32)) for i in range(2)]

        proj_done, qk_out, v_out = sem("proj_done"), sem("qk_out"), sem("v_out")
        scores_done, masked, max_done, exp_done = sem("scores_done"), sem("masked"), sem("max_done"), sem("exp_done")
        rec_done, norm_done = sem("rec_done"), sem("norm_done")
        probT_done, probT_out = sem("probT_done"), sem("probT_out")
        pv_done, ao_hid, ao_lod = sem("pv_done"), sem("ao_hid"), sem("ao_lod")
        wo_done, y_added = sem("wo_done"), sem("y_added")
        raw_in = [sem("raw_in0"), sem("raw_in1")]
        qkv_hi_split, qkv_split = sem("qkv_hi_split"), sem("qkv_split")
        wo_hi_split, wo_split = sem("wo_hi_split"), sem("wo_split")
        moe_raw_in, moe_hi = sem("moe_raw_in"), sem("moe_hi")
        moe_raw = fw.raw[:].rearrange("p c w -> p (c w)")[:, 0:SLOTS * WCOLS].rearrange("p (j c) -> p j c", j=SLOTS)
        moe_split = sem("moe_split")
        qz = Quantizer(nc, ctx, "fw", fw.WIDTH, w.raw[:, 0].rearrange("p a k c -> p (a k c)"))

        def pe_project(pe, it, j, first=False):
            S = it * STEPS + j
            g, n = (j // 2) % GROUPS, j % 2
            if j in (1, STEPS) and not (isinstance(it, int) and _pair(it, j) < 2):
                pe.wait_ge(qkv_split, _pair(it, j) - 1)
            for u in range(UNITS):
                out = ring[u % RING]
                if not first:
                    if u in (0, 1):
                        pe.wait_ge(v_out, 2 * (S - 1) + u + 1)
                    elif u in (2, 3):
                        if isinstance(it, int) and S < 2:
                            pe.wait_ge(qk_out, 4 * (S - 1) + u + 1)
                        else:
                            pe.wait_ge(ao_lod, 2 * (S - 2) + (u - 2) + 1)
                if u in (4, 5):
                    pe.wait_ge(qk_out, 4 * S + (u - 4) + 1)
                if u < 4:
                    c = (u // 2) * HD
                    for k in range(KT):
                        h_hi, h_lo = w.hT_hi[:, k, g * GW:(g + 1) * GW], w.hT_lo[:, k, g * GW:(g + 1) * GW]
                        mm = parts(pe, out[:], w.hi[:, n, u % 2, k, c:c + HD], w.lo[:, n, u % 2, k, c:c + HD],
                                   h_hi, h_lo, start=(k == 0), stop=(k == KT - 1))
                else:
                    for t in range(2):
                        tok = g * GW + ((u - 4) * 2 + t) * P
                        for k in range(KT):
                            mm = parts(pe, out[:, t * 2 * HD:(t + 1) * 2 * HD], w.hT_hi[:, k, tok:tok + P],
                                       w.hT_lo[:, k, tok:tok + P], w.hi[:, n, 2, k, :], w.lo[:, n, 2, k, :],
                                       start=(t == 0 and k == 0), stop=(k == KT - 1))
                mm.then_inc(proj_done, 1)

        def _pair(it, j):
            return 2 * it + 2 * (j // STEPS) + j % 2

        def pe_scores(pe, it, j):
            S = it * STEPS + j
            for h in range(2):
                if not (isinstance(it, int) and S < 1):
                    pe.wait_ge(probT_out, 2 * (S - 1) + h + 1)
                pe.wait_ge(qk_out, 4 * S + 2 * h + 2)
                for b in range(GROUP):
                    c = slice(b * P, (b + 1) * P)
                    mm = pe.matmul(sc_ps[h][:, c], qk[:, 2 * h, c], qk[:, 2 * h + 1, c], start=(b == 0), stop=True,
                                   skip_group_check=True)
                mm.then_inc(scores_done, 1)

        def pe_transpose(pe, it, j):
            S = it * STEPS + j
            for h in range(2):
                pe.wait_ge(norm_done, 2 * S + h + 1)
                for b in range(GROUP):
                    mm = pe.transpose(sc_ps[h][:, b * P:(b + 1) * P], prob[:, h, b], e.ident[:])
                mm.then_inc(probT_done, 1)

        def pe_wo(pe, it, j):
            S = it * STEPS + j
            n = j % 2
            pe.wait_ge(ao_lod, 2 * S + 2)
            if j < 2 and not (isinstance(it, int) and it == 0):
                pe.wait_ge(wo_split, 2 * it + n - 1)
            if n == 0 and not (isinstance(it, int) and S < 2):
                pe.wait_ge(y_added, S)
            for b in range(GROUP):
                for h in range(2):
                    mm = parts(pe, wo_ps[b // 2][:, (b % 2) * D:(b % 2 + 1) * D], ao_hi[:, h, b * P:(b + 1) * P],
                               ao_lo[:, h, b * P:(b + 1) * P], w.hi[:, n, 3, h, :], w.lo[:, n, 3, h, :],
                               start=(n == 0 and h == 0 and b % 2 == 0), stop=(n == 1 and h == 1))
            mm.then_inc(wo_done, 1)

        def pe_pv(pe, it, j, last=False):
            S = it * STEPS + j
            pe.wait_ge(v_out, 2 * S + 2)
            for h in range(2):
                pe.wait_ge(probT_out, 2 * S + h + 1)
                out = ring[2 + h]
                if not last:
                    pe.wait_ge(qk_out, 4 * (S + 1) + 2 + h + 1)
                elif last:
                    pe.wait_ge(ao_lod, 2 * (S - 1) + h + 1)
                for b in range(GROUP):
                    c = slice(b * P, (b + 1) * P)
                    mm = pe.matmul(out[:, c], v[:, j % 2, b, h * HD:(h + 1) * HD], b_probT[:, h, c], start=(b == 0),
                                   stop=True, skip_group_check=True)
                mm.then_inc(pv_done, 1)

        def pe_pass(pe, it, first=False, last=False):
            for j in range(STEPS):
                end = last and j == STEPS - 1
                pe_scores(pe, it, j)
                if not end:
                    pe_project(pe, it, j + 1)
                pe_transpose(pe, it, j)
                if j > 0:
                    pe_wo(pe, it, j - 1)
                elif not first:
                    pe_wo(pe, it - 1, STEPS - 1)
                pe_pv(pe, it, j, last=end)

        SCALE = float(HD) ** -0.5

        def act_project(act, it, j):
            S = it * STEPS + j
            for u in range(4):
                act.wait_ge(proj_done, UNITS * S + u + 1)
                act.activation(qk[:, u], ring[u][:], ACT.Copy, scale=SCALE if u % 2 == 0 else 1.0).then_inc(qk_out, 1)

        def act_pass(act, it, last=False):
            for j in range(STEPS):
                S = it * STEPS + j
                for h in range(2):
                    act.wait_ge(max_done, 2 * S + h + 1)
                    for b in range(GROUP):
                        act.activation(prob[:, h, b], prob[:, h, b], ACT.Exp,
                                       bias=nmax[:, j % 2, h, b:b + 1],
                                       accum_out=sums[:, j % 2, h, b:b + 1]).then_inc(exp_done, 1)
                if not (last and j == STEPS - 1):
                    act_project(act, it, j + 1)
                for h in range(2):
                    act.wait_ge(probT_done, 2 * S + h + 1)
                    act.activation(b_probT[:, h], sc_ps[h][:], ACT.Copy).then_inc(probT_out, 1)
                for h in range(2):
                    act.wait_ge(pv_done, 2 * S + h + 1)
                    act.activation(ao_hi[:, h], ring[2 + h][:], ACT.Copy).then_inc(ao_hid, 1)

        def dve_project(ve, it, j):
            S = it * STEPS + j
            for u in (4, 5):
                ve.wait_ge(proj_done, UNITS * S + u + 1)
                t = 2 * (u - 4)
                ve.tensor_copy(v[:, j % 2, t:t + 2].rearrange("p t c -> p (t c)"), ring[u % RING][:]).then_inc(v_out, 1)

        def dve_ao(ve, it, j):
            S = it * STEPS + j
            for h in range(2):
                ve.wait_ge(ao_hid, 2 * S + h + 1)
                ve.tensor_tensor(ao_lo[:, h], ring[2 + h][:], ao_hi[:, h].bitcast(F32), ALU.subtract).then_inc(ao_lod, 1)

        def dve_add(ve, it, j):
            S = it * STEPS + j
            g = j // 2
            ve.wait_ge(wo_done, S + 1)
            for n in range(2):
                y = e.Y[:, g * GROUP + 2 * n:g * GROUP + 2 * n + 2].rearrange("p t d -> p (t d)")
                if not (isinstance(it, int) and it == 0):
                    ve.wait_ge(y_added, S - 1 + n)
                ve.tensor_tensor(y, wo_ps[n][:], y, ALU.add).then_inc(y_added, 1)

        def dve_pass(ve, it, first=False, last=False):
            for j in range(STEPS):
                S = it * STEPS + j
                before = (it, j - 1) if j > 0 else (it - 1, STEPS - 1)
                for h in range(2):
                    ve.wait_ge(scores_done, 2 * S + h + 1)
                    if not (first and j == 0):
                        ve.wait_ge(probT_done, 2 * (S - 1) + h + 1)
                    ve.tensor_tensor(prob[:, h], sc_ps[h][:].rearrange("p (b m) -> p b m", b=GROUP),
                                     w.causal[:].unsqueeze(1).broadcast_to([P, GROUP, P]), ALU.add).then_inc(masked, 1)
                for h in range(2):
                    ve.wait_ge(masked, 2 * S + h + 1)
                    ve.tensor_reduce(nmax[:, j % 2, h], prob[:, h], X_AXIS, ALU.max, negate=True).then_inc(max_done, 1)
                if not (first and j == 0):
                    dve_ao(ve, *before)
                more = not (last and j == STEPS - 1)
                for h in range(2):
                    ve.wait_ge(exp_done, GROUP * (2 * S + h) + GROUP)
                    ve.reciprocal(rec[:, j % 2, h], sums[:, j % 2, h]).then_inc(rec_done, 1)
                chunk = j - 1 if last and 0 <= j - 1 < fw.CHUNKS else None
                if chunk is not None:
                    if chunk == 0:
                        ve.wait_ge(fw.w_in, 16)
                    qz.scales(ve, chunk, fw.raw[:, chunk])
                if more:
                    dve_project(ve, it, j + 1)
                if chunk is not None:
                    qz.round(ve, chunk)
                if j % 2 == 0 and not (first and j == 0):
                    dve_add(ve, *before)
                if last and j % 2 == 0 and j > 0:
                    ve.wait_ge(y_added, S)
                    early_statistics(ve, e.stats, e.Y, j // 2 - 1, GROUPS - 1)

        def pool_split(pool, n, which, hi_sem, lo_sem, hi_at, lo_at):
            hi = w.hi[:, n, which].rearrange("p a k c -> p (a k c)")
            lo = w.lo[:, n, which].rearrange("p a k c -> p (a k c)")
            raw = w.raw[:, n, which].rearrange("p a k c -> p (a k c)")
            copy_pool(pool, e, hi, raw).then_inc(hi_sem, 1)
            pool.wait_ge(hi_sem, hi_at)
            pool.tensor_tensor(lo, raw, hi.bitcast(F32), ALU.subtract).then_inc(lo_sem, 1)

        def pool_pass(pool, it, first=False, last=False):
            for j in range(STEPS):
                S = it * STEPS + j
                for h in range(2):
                    pool.wait_ge(rec_done, 2 * S + h + 1)
                    pool.tensor_tensor(prob[:, h], prob[:, h], over_groups(rec[:, j % 2, h]), ALU.mult).then_inc(norm_done, 1)
                if first and j < SLOTS:
                    pool.wait_ge(moe_raw_in, 16 * SLOTS)
                    pool.tensor_scalar(mw.hi[:, j], moe_raw[:, j], 1.0, None, ALU.mult).then_inc(moe_hi, 1)
                    pool.wait_ge(moe_hi, j + 1)
                    pool.tensor_tensor(mw.lo[:, j], moe_raw[:, j, 0:SEL], mw.hi[:, j, 0:SEL].bitcast(F32),
                                       ALU.subtract).then_inc(moe_split, 1)
                if last and 0 <= j - 1 < fw.CHUNKS:
                    if j == 1:
                        pool.wait_ge(fw.w_in, 16)
                    qz.quotient(pool, j - 1, fw.raw[:, j - 1])
                    qz.restore(pool, j - 1, fw.raw[:, j - 1])
                if not last and j >= STEPS - 3 and j < STEPS - 1:
                    n = j - (STEPS - 3)
                    pool.wait_ge(proj_done, UNITS * (S + 2))
                    pool.wait_ge(raw_in[n], 16 * (it + 1))
                    pool_split(pool, n, slice(0, 3), qkv_hi_split, qkv_split, 2 * it + n + 1, 2 * it + n + 1)
                if not last and j == STEPS - 1:
                    pool.wait_ge(wo_done, S)
                    pool_split(pool, 0, slice(3, 4), wo_hi_split, wo_split, 2 * it + 1, 2 * it + 1)
                if not first and j == 0:
                    pool.wait_ge(wo_done, S)
                    pool_split(pool, 1, slice(3, 4), wo_hi_split, wo_split, 2 * it, 2 * it)

        def sp_pass(sp, it):
            for n in range(2):
                if not (isinstance(it, int) and it == 0):
                    sp.wait_ge(wo_split, 2 * (it - 1) + n + 1)
                sp.dma_start(w.raw[:, n:n + 1], ins["w_attn"][:, ds(2 * it + 2 + n, 1)]).then_inc(raw_in[n], 16)

        with nc.Block() as block:
            @block.sync
            def _(sp):
                sp_pass(sp, 0)
                for j in range(SLOTS):
                    sp.dma_start(moe_raw[:, j], ins["w_moe"][:, j]).then_inc(moe_raw_in, 16)
                sp.wait_ge(moe_split, SLOTS)
                sp.dma_start(fw.raw[:], ins["w_ffn"]).then_inc(fw.w_in, 16)
                with sp.Fori(1, PASSES - 1) as it:
                    sp_pass(sp, it)

            @block.gpsimd
            def _(pool):
                pool_pass(pool, 0, first=True)
                with pool.Fori(1, PASSES - 1) as it:
                    pool_pass(pool, it)
                pool_pass(pool, PASSES - 1, last=True)

            @block.scalar
            def _(act):
                act_project(act, 0, 0)
                act_pass(act, 0)
                with act.Fori(1, PASSES - 1) as it:
                    act_pass(act, it)
                act_pass(act, PASSES - 1, last=True)

            @block.vector
            def _(ve):
                dve_project(ve, 0, 0)
                dve_pass(ve, 0, first=True)
                with ve.Fori(1, PASSES - 1) as it:
                    dve_pass(ve, it)
                dve_pass(ve, PASSES - 1, last=True)
                dve_ao(ve, PASSES - 1, STEPS - 1)
                dve_add(ve, PASSES - 1, STEPS - 1)

            @block.tensor
            def _(pe):
                pe_project(pe, 0, 0, first=True)
                pe_pass(pe, 0, first=True)
                with pe.Fori(1, PASSES - 1) as it:
                    pe_pass(pe, it)
                pe_pass(pe, PASSES - 1, last=True)
                pe_wo(pe, PASSES - 1, STEPS - 1)



class Norm:

    def __init__(self, nc, ctx, tag, stats, banks):
        def sb(name, shape, dt=F32):
            return ctx.enter_context(nc.sbuf_tensor(f"{tag}_{name}", shape, dt))

        self.st, self.mv = stats, sb("mv", [P, BATCHES, 2])
        self.va, self.rs, self.shift = sb("va", [P, BATCHES]), sb("rs", [P, BATCHES]), sb("shift", [P, BATCHES])
        self.nt, self.nu = sb("nt", [P, BATCHES]), sb("nu", [P, BATCHES])
        self.xn = sb("xn", [P, 2, GROUP, D])
        self.banks = banks
        self.depth = len(banks) // KT
        self.chain, self.stats_done, self.ready, self.turned, self.hi_done, self.lo_done = (
            ctx.enter_context(nc.semaphore(f"{tag}_{n}")) for n in ("chain", "stats_done", "ready", "turned", "hi", "lo"))

    def bank(self, g, k):
        return self.banks[KT * (g % self.depth) + k]


EARLY = BATCHES - GROUP


def early_statistics(ve, stats, src, n, of):
    for t in range(n * EARLY // of, (n + 1) * EARLY // of):
        ve.bn_stats(stats[:, t], src[:, t])


def norm_statistics(ve, n, src, eps, centred):
    links = [0]

    def link(instruction):
        links[0] += 1
        instruction.then_inc(n.chain, 1)
        ve.wait_ge(n.chain, links[0])

    for half in range(2):
        tiles = range(half * BATCHES // 2, (half + 1) * BATCHES // 2)
        c = slice(half * BATCHES // 2, (half + 1) * BATCHES // 2)
        va, rs, nt, nu, shift = (a[:, c] for a in (n.va, n.rs, n.nt, n.nu, n.shift))
        if half == 1:
            for t in range(EARLY, BATCHES):
                last = ve.bn_stats(n.st[:, t], src[:, t])
            link(last)
        for t in tiles:
            last = ve.bn_aggr(n.mv[:, t], n.st[:, t])
        link(last)
        if centred:
            link(ve.tensor_scalar(va, n.mv[:, c, 1], eps, None, ALU.add))
            rsqrt_steps(ve, link, va, rs, nt, nu)
            ve.scalar_tensor_tensor(out=shift, in0=n.mv[:, c, 0], scalar=-1.0, in1=rs, op0=ALU.mult,
                                    op1=ALU.mult).then_inc(n.stats_done, 1)
        else:
            link(ve.tensor_tensor(nt, n.mv[:, c, 0], n.mv[:, c, 0], ALU.mult))
            link(ve.scalar_tensor_tensor(out=va, in0=nt, scalar=eps, in1=n.mv[:, c, 1], op0=ALU.add, op1=ALU.add))
            rsqrt_steps(ve, link, va, rs, nt, nu, lambda instruction: instruction.then_inc(n.stats_done, 1))


def norm_low(ve, n, g, hi, lo, weight=None):
    for k in range(KT):
        ve.wait_ge(n.hi_done, KT * g + k + 1)
        if weight is None:
            ve.tensor_tensor(lo[:, k], n.bank(g, k)[:], hi[:, k].bitcast(F32), ALU.subtract).then_inc(n.lo_done, 1)
        else:
            ve.scalar_tensor_tensor(out=lo[:, k], in0=n.bank(g, k)[:], scalar=weight[:, k:k + 1], in1=hi[:, k].bitcast(F32),
                                    op0=ALU.mult, op1=ALU.subtract).then_inc(n.lo_done, 1)


def norm_tensor(pe, n, ident, g):
    pe.wait_ge(n.ready, g + 1)
    if g >= n.depth:
        pe.wait_ge(n.lo_done, KT * (g + 1 - n.depth))
    for k in range(KT):
        for b in range(GROUP):
            mm = pe.transpose(n.bank(g, k)[:, b * P:(b + 1) * P], n.xn[:, g % 2, b, k * P:(k + 1) * P], ident)
    mm.then_inc(n.turned, 1)


def norm_scalar(act, n, g, src, centred):
    act.wait_ge(n.stats_done, g // 2 + 1)
    if g >= 2:
        act.wait_ge(n.turned, g - 1)
    for b in range(GROUP):
        t = g * GROUP + b
        if centred:
            last = act.activation(n.xn[:, g % 2, b], src[:, t], ACT.Identity, scale=n.rs[:, t:t + 1],
                                  bias=n.shift[:, t:t + 1])
        else:
            last = act.activation(n.xn[:, g % 2, b], src[:, t], ACT.Copy, scale=n.rs[:, t:t + 1])
    last.then_inc(n.ready, 1)


def norm_high(act, n, g, hi, weight=None):
    act.wait_ge(n.turned, g + 1)
    for k in range(KT):
        scale = 1.0 if weight is None else weight[:, k:k + 1]
        act.activation(hi[:, k], n.bank(g, k)[:], ACT.Copy, scale=scale).then_inc(n.hi_done, 1)


def group_columns(h, g):
    return h[:, :, g * GW:(g + 1) * GW]


def parts(pe, out, l_hi, l_lo, r_hi, r_lo, start, stop=False):
    pe.matmul(out, l_hi, r_hi, start=start, stop=False, skip_group_check=True)
    pe.matmul(out, l_hi, r_lo, start=False, stop=False, skip_group_check=True)
    return pe.matmul(out, l_lo, r_hi, start=False, stop=stop, skip_group_check=True)


EXPERTS = 16
TOP = 6
EI = 176
SI = 352
TILES = -(-(EXPERTS * EI + SI) // P)
SLOTS = 5
CW_LOW = 32
CW_ROWS = CW_LOW + EXPERTS + 1
UP, DOWN, SEL, WCOLS = KT * P, 2 * KT * P, 2 * KT * P + D, 2 * KT * P + D + P


class MoeWeights:

    def __init__(self, nc, ctx):
        def sb(name, shape, dt=F32):
            return ctx.enter_context(nc.sbuf_tensor(f"m_{name}", shape, dt))

        self.hi = sb("hi", [P, SLOTS, WCOLS], F32R)
        self.lo = sb("lo", [P, SLOTS, SEL], F32R)


def phase_moe(nc, e, ins, mw):
    STEPS = GROUPS * SLOTS
    PASSES = TILES // SLOTS
    LAG = 2
    RING = 4
    assert TILES % SLOTS == 0 and STEPS % RING == 0
    with ExitStack() as ctx:
        def sb(name, shape, dt=F32):
            return ctx.enter_context(nc.sbuf_tensor(name, shape, dt))

        def sem(name):
            return ctx.enter_context(nc.semaphore(name))

        hT_hi = sb("m_hT_hi", [P, KT, BATCHES * P], F32R)
        hT_lo = sb("m_hT_lo", [P, KT, BATCHES * P], F32R)
        raw = sb("m_raw", [P, SLOTS, WCOLS])
        hi, lo = mw.hi, mw.lo
        ln2 = sb("ln2", [P, KT])
        gate = sb("gate", [P, KT, EXPERTS])
        gate_parts = sb("gate_parts", [P, KT, 2, EXPERTS], F32R)
        cw = sb("cw", [P, BATCHES, CW_ROWS])
        cwT = sb("cwT", [CW_ROWS, BATCHES * P], F32R)
        silu = sb("silu", [P, 2, GW])
        gated = sb("gated", [P, 2, GW])
        inner = sb("inner", [P, 2, GW])
        in_hi = sb("in_hi", [P, RING, GW], F32R)
        in_lo = sb("in_lo", [P, RING, GW], F32R)
        bank = [ctx.enter_context(nc.psum_tensor(f"m_bank{i}", [P, GW], F32)) for i in range(8)]
        g_ps, u_ps, c_ps, o_ps = bank[0:2], bank[2:4], bank[4:6], bank[6:8]
        cwT_ps = (bank[4], bank[5], bank[7], bank[6])
        nrm = Norm(nc, ctx, "m", e.stats, bank[0:4])
        PAD = EXPERTS // 2
        lg, pr, gt, eq, sel = (sb(n, [P, BATCHES, EXPERTS]) for n in ("lg", "pr", "gt", "eq", "g_sel"))
        pre = [sb(f"pre{i}", [P, BATCHES, PAD + EXPERTS]) for i in range(2)]
        top8 = sb("top8", [P, BATCHES, 8])
        gmx, cnt, need, tot, inv = (sb(n, [P, BATCHES]) for n in ("gmx", "cnt", "need", "tot", "inv"))

        small_in, x_plus, gate_split = sem("small_in"), sem("x_plus"), sem("gate_split")
        logits_done, g_shift, g_exp, g_chain, cw_ready = (sem(n) for n in ("logits_done", "g_shift", "g_exp", "g_chain", "cw_ready"))
        cwT_done, cwT_hid, cwT_lod = sem("cwT_done"), sem("cwT_hid"), sem("cwT_lod")
        up_hi_split, up_split, down_hi_split, down_split = (sem(n) for n in ("up_hi_split", "up_split", "down_hi_split", "down_split"))
        raw_in = [sem(f"m_raw_in{j}") for j in range(SLOTS)]
        g_done, u_done, c_done, silu_done, gated_done, inner_done = (
            sem(n) for n in ("g_done", "u_done", "c_done", "silu_done", "gated_done", "inner_done"))
        in_hid, in_lod, down_done, added = (sem(n) for n in ("in_hid", "in_lod", "down_done", "added"))

        def spread(a):
            return a.unsqueeze(2).broadcast_to([P, BATCHES, EXPERTS])

        def gate_vector(ve):
            links = [0]

            def link(instruction):
                links[0] += 1
                instruction.then_inc(g_chain, 1)
                ve.wait_ge(g_chain, links[0])

            lps = o_ps[0][:].rearrange("p (t a e) -> p t a e", a=2, e=EXPERTS)
            link(ve.memset(cw[:], 0.0))
            for base in (0, CW_LOW):
                ve.memset(cw[:, :, base + EXPERTS:base + EXPERTS + 1], 1.0)
            ve.memset(pre[0][:], 0.0)
            link(ve.memset(pre[1][:], 0.0))
            ve.wait_ge(logits_done, 1)
            link(ve.tensor_copy(lg[:], lps[:, :, 0]))
            link(ve.tensor_tensor(lg[:], lps[:, :, 1], lg[:], ALU.add))
            link(ve.tensor_reduce(gmx[:], lg[:], X_AXIS, ALU.max))
            ve.tensor_tensor(lg[:], lg[:], spread(gmx[:]), ALU.subtract).then_inc(g_shift, 1)
            ve.wait_ge(g_exp, 1)
            for t in range(BATCHES):
                last = ve.max(top8[:, t], pr[:, t])
            link(last)
            sixth = spread(top8[:, :, TOP - 1])
            ve.tensor_tensor(eq[:], pr[:], sixth, ALU.is_equal)
            link(ve.tensor_tensor(gt[:], pr[:], sixth, ALU.is_gt))
            ve.tensor_copy(pre[0][:, :, PAD:], eq[:])
            link(ve.tensor_reduce(cnt[:], gt[:], X_AXIS, ALU.add))
            link(ve.tensor_scalar(need[:], cnt[:], -1.0, float(TOP), ALU.mult, ALU.add))
            for i, shift in enumerate((1, 2, 4, 8)):
                a, b = pre[i % 2], pre[(i + 1) % 2]
                link(ve.tensor_tensor(b[:, :, PAD:], a[:, :, PAD:], a[:, :, PAD - shift:PAD - shift + EXPERTS], ALU.add))
            link(ve.tensor_tensor(sel[:], pre[0][:, :, PAD:], spread(need[:]), ALU.is_le))
            link(ve.tensor_tensor(sel[:], sel[:], eq[:], ALU.mult))
            link(ve.tensor_tensor(sel[:], sel[:], gt[:], ALU.add))
            link(ve.tensor_tensor(sel[:], sel[:], pr[:], ALU.mult))
            link(ve.tensor_reduce(tot[:], sel[:], X_AXIS, ALU.add))
            link(ve.reciprocal(inv[:], tot[:]))
            for base in (0, CW_LOW):
                last = ve.tensor_tensor(cw[:, :, base:base + EXPERTS], sel[:], spread(inv[:]), ALU.mult)
            last.then_inc(cw_ready, 1)
            for g in range(GROUPS):
                ve.wait_ge(cwT_hid, g + 1)
                cols = slice(g * GW, (g + 1) * GW)
                low = cwT[CW_LOW:CW_ROWS, cols]
                ve.tensor_tensor(low, cwT_ps[g][CW_LOW:CW_ROWS, :], low.bitcast(F32), ALU.subtract).then_inc(cwT_lod, 1)

        def pe_logits(pe, g):
            if g == 0:
                pe.wait_ge(gate_split, 2)
            pe.wait_ge(nrm.lo_done, KT * (g + 1))
            for t in range(g * GROUP, (g + 1) * GROUP):
                out = o_ps[0][:, t * 2 * EXPERTS:(t + 1) * 2 * EXPERTS]
                for k in range(KT):
                    for h in (hT_hi, hT_lo):
                        mm = pe.matmul(out, h[:, k, t * P:(t + 1) * P], gate_parts[:, k].rearrange("p a e -> p (a e)"),
                                       start=(t == 0 and k == 0 and h is hT_hi), stop=(k == KT - 1 and h is hT_lo),
                                       skip_group_check=True)
            if g == GROUPS - 1:
                mm.then_inc(logits_done, 1)

        def pe_gate_up(pe, it, i):
            S, g, j, par = it * STEPS + i, i // SLOTS, i % SLOTS, i % 2
            early = isinstance(it, int) and S < 2
            if g == 0 and not (isinstance(it, int) and it == 0):
                pe.wait_ge(up_split, (it - 1) * SLOTS + j + 1)
            cols = slice(g * GW, (g + 1) * GW)
            for base, out, done, free in ((0, g_ps[par], g_done, silu_done), (UP, u_ps[par], u_done, gated_done)):
                if not early:
                    pe.wait_ge(free, S - 1)
                for k in range(KT):
                    wc = slice(base + k * P, base + (k + 1) * P)
                    mm = parts(pe, out[:], hi[:, j, wc], lo[:, j, wc], hT_hi[:, k, cols], hT_lo[:, k, cols],
                               start=(k == 0), stop=(k == KT - 1))
                mm.then_inc(done, 1)

        def pe_weights(pe, it, i):
            S, g, j, par = it * STEPS + i, i // SLOTS, i % SLOTS, i % 2
            cols = slice(g * GW, (g + 1) * GW)
            if not (isinstance(it, int) and S < 2):
                pe.wait_ge(inner_done, S - 1)
            pe.matmul(c_ps[par][:], hi[0:CW_ROWS, j, SEL:WCOLS], cwT[:, cols], start=True, stop=True).then_inc(c_done, 1)

        def pe_down(pe, it, i):
            S, g, j = it * STEPS + i, i // SLOTS, i % SLOTS
            pe.wait_ge(in_lod, S + 1)
            if g == 0 and not (isinstance(it, int) and it == 0):
                pe.wait_ge(down_split, (it - 1) * SLOTS + j + 1)
            if j == 0 and not (isinstance(it, int) and it == 0 and g == 0):
                pe.wait_ge(added, 2 * (it * GROUPS + g))
            for b in range(GROUP):
                c = slice(b * P, (b + 1) * P)
                mm = parts(pe, o_ps[b // 2][:, (b % 2) * D:(b % 2 + 1) * D], in_hi[:, i % RING, c], in_lo[:, i % RING, c],
                           hi[:, j, DOWN:SEL], lo[:, j, DOWN:SEL], start=(j == 0 and b % 2 == 0), stop=(j == SLOTS - 1))
            mm.then_inc(down_done, 1)

        def lagging(it, i, first):
            return (it, i - LAG) if i >= LAG else None if first else (it - 1, i - LAG + STEPS)

        def pe_pass(pe, it, first=False):
            for i in range(STEPS):
                if not (first and i < 2):
                    pe_gate_up(pe, it, i)
                pe_weights(pe, it, i)
                if (before := lagging(it, i, first)) is not None:
                    pe_down(pe, *before)

        def act_silu(act, it, i):
            S = it * STEPS + i
            act.wait_ge(g_done, S + 1)
            act.activation(silu[:, i % 2], g_ps[i % 2][:], ACT.Silu).then_inc(silu_done, 1)

        def act_hi(act, it, i):
            S = it * STEPS + i
            act.wait_ge(inner_done, S + 1)
            act.activation(in_hi[:, i % RING], inner[:, i % 2], ACT.Copy).then_inc(in_hid, 1)

        def act_pass(act, it, first=False):
            for i in range(STEPS):
                act_silu(act, it, i)
                if i > 0:
                    act_hi(act, it, i - 1)
                elif not first:
                    act_hi(act, it - 1, STEPS - 1)

        def ve_add(ve, it, i):
            S, g = it * STEPS + i, i // SLOTS
            ve.wait_ge(down_done, S + 1)
            for n in range(2):
                x = e.X[:, g * GROUP + 2 * n:g * GROUP + 2 * n + 2].rearrange("p t d -> p (t d)")
                if not (isinstance(it, int) and it == 0):
                    ve.wait_ge(added, 2 * (it * GROUPS + g) + n)
                ve.tensor_tensor(x, o_ps[n][:], x, ALU.add).then_inc(added, 1)

        def ve_pass(ve, it, first=False, last=False):
            for i in range(STEPS):
                S, par = it * STEPS + i, i % 2
                ve.wait_ge(silu_done, S + 1)
                ve.wait_ge(u_done, S + 1)
                ve.tensor_tensor(gated[:, par], u_ps[par][:], silu[:, par], ALU.mult).then_inc(gated_done, 1)
                ve.wait_ge(c_done, S + 1)
                ve.wait_ge(gated_done, S + 1)
                if not (isinstance(it, int) and S < 2):
                    ve.wait_ge(in_lod, S - 1)
                ve.tensor_tensor(inner[:, par], c_ps[par][:], gated[:, par], ALU.mult).then_inc(inner_done, 1)
                before = lagging(it, i, first)
                if before is not None and before[1] % SLOTS == SLOTS - 1:
                    ve_add(ve, *before)
                    if last and i > LAG:
                        g = before[1] // SLOTS
                        ve.wait_ge(added, 2 * (it * GROUPS + g + 1))
                        early_statistics(ve, e.stats, e.X, g, GROUPS - 1)

        def pool_low(pool, it, i):
            S = it * STEPS + i
            pool.wait_ge(in_hid, S + 1)
            pool.tensor_tensor(in_lo[:, i % RING], inner[:, i % 2], in_hi[:, i % RING].bitcast(F32),
                               ALU.subtract).then_inc(in_lod, 1)

        def pool_refill_up(pool, it, j):
            pool.wait_ge(c_done, it * STEPS + STEPS - SLOTS + j + 1)
            pool.wait_ge(raw_in[j], 16 * (it + 1))
            copy_pool(pool, e, hi[:, j, SEL:WCOLS], raw[:, j, SEL:WCOLS])
            copy_pool(pool, e, hi[:, j, 0:DOWN], raw[:, j, 0:DOWN]).then_inc(up_hi_split, 1)
            pool.wait_ge(up_hi_split, it * SLOTS + j + 1)
            pool.tensor_tensor(lo[:, j, 0:DOWN], raw[:, j, 0:DOWN], hi[:, j, 0:DOWN].bitcast(F32),
                               ALU.subtract).then_inc(up_split, 1)

        def pool_refill_down(pool, it, j):
            pool.wait_ge(down_done, it * STEPS + STEPS - SLOTS + j + 1)
            copy_pool(pool, e, hi[:, j, DOWN:SEL], raw[:, j, DOWN:SEL]).then_inc(down_hi_split, 1)
            pool.wait_ge(down_hi_split, it * SLOTS + j + 1)
            pool.tensor_tensor(lo[:, j, DOWN:SEL], raw[:, j, DOWN:SEL], hi[:, j, DOWN:SEL].bitcast(F32),
                               ALU.subtract).then_inc(down_split, 1)

        def pool_pass(pool, it, first=False, last=False):
            for i in range(STEPS):
                pool_low(pool, it, i)
                if not last and i >= STEPS - SLOTS:
                    pool_refill_up(pool, it, i - (STEPS - SLOTS))
                back = i - (STEPS - SLOTS) - LAG
                if not last and back >= 0:
                    pool_refill_down(pool, it, back)
                if not first and i < LAG:
                    pool_refill_down(pool, it - 1, SLOTS - LAG + i)

        with nc.Block() as block:
            @block.sync
            def _(sp):
                sp.dma_start(ln2[:], ins["ln2"]).then_inc(small_in, 16)
                sp.dma_start(gate[:], ins["gate"]).then_inc(small_in, 16)
                for j in range(SLOTS):
                    sp.dma_start(raw[:, j], ins["w_moe"][:, SLOTS + j]).then_inc(raw_in[j], 16)
                with sp.Fori(2, PASSES) as it:
                    for j in range(SLOTS):
                        sp.wait_ge(down_split, (it - 2) * SLOTS + j + 1)
                        sp.wait_ge(up_split, (it - 2) * SLOTS + j + 1)
                        sp.dma_start(raw[:, j:j + 1], ins["w_moe"][:, ds(it * SLOTS + j, 1)]).then_inc(raw_in[j], 16)

            @block.gpsimd
            def _(pool):
                pool.wait_ge(small_in, 32)
                pool.tensor_scalar(gate_parts[:, :, 0], gate[:], 1.0, None, ALU.mult).then_inc(gate_split, 1)
                pool.wait_ge(gate_split, 1)
                pool.tensor_tensor(gate_parts[:, :, 1], gate[:], gate_parts[:, :, 0].bitcast(F32),
                                   ALU.subtract).then_inc(gate_split, 1)
                pool.tensor_tensor(e.X[:].rearrange("p t d -> p (t d)"), e.X[:].rearrange("p t d -> p (t d)"),
                                   e.Y[:].rearrange("p t d -> p (t d)"), ALU.add).then_inc(x_plus, 1)
                pool_pass(pool, 0, first=True)
                with pool.Fori(1, PASSES - 1) as it:
                    pool_pass(pool, it)
                pool_pass(pool, PASSES - 1, last=True)

            @block.scalar
            def _(act):
                norm_scalar(act, nrm, 0, e.Y, False)
                act.wait_ge(small_in, 32)
                for g in range(GROUPS):
                    if g + 1 < GROUPS:
                        norm_scalar(act, nrm, g + 1, e.Y, False)
                    norm_high(act, nrm, g, group_columns(hT_hi, g), ln2)
                act.wait_ge(g_shift, 1)
                act.activation(pr[:], lg[:], ACT.Exp).then_inc(g_exp, 1)
                for g in range(GROUPS):
                    act.wait_ge(cwT_done, g + 1)
                    act.activation(cwT[:, g * GW:(g + 1) * GW], cwT_ps[g][0:CW_ROWS, :], ACT.Copy).then_inc(cwT_hid, 1)
                act_pass(act, 0, first=True)
                with act.Fori(1, PASSES) as it:
                    act_pass(act, it)
                act_hi(act, PASSES - 1, STEPS - 1)

            @block.vector
            def _(ve):
                norm_statistics(ve, nrm, e.Y, RMS_EPS, False)
                ve.wait_ge(small_in, 32)
                for g in range(GROUPS):
                    norm_low(ve, nrm, g, group_columns(hT_hi, g), group_columns(hT_lo, g), ln2)
                gate_vector(ve)
                ve.wait_ge(x_plus, 1)
                ve_pass(ve, 0, first=True)
                with ve.Fori(1, PASSES - 1) as it:
                    ve_pass(ve, it)
                ve_pass(ve, PASSES - 1, last=True)
                ve_add(ve, PASSES - 1, STEPS - 1)

            @block.tensor
            def _(pe):
                for g in range(GROUPS + 1):
                    if g < GROUPS:
                        norm_tensor(pe, nrm, e.ident[:], g)
                    if g >= 1:
                        pe_logits(pe, g - 1)
                for i in range(2):
                    pe_gate_up(pe, 0, i)
                pe.wait_ge(cw_ready, 1)
                for g in range(GROUPS):
                    for b in range(GROUP):
                        mm = pe.transpose(cwT_ps[g][0:CW_ROWS, b * P:(b + 1) * P], cw[:, g * GROUP + b], e.ident[:])
                    mm.then_inc(cwT_done, 1)
                pe.wait_ge(cwT_lod, GROUPS)
                pe_pass(pe, 0, first=True)
                with pe.Fori(1, PASSES) as it:
                    pe_pass(pe, it)
                for i in range(STEPS - LAG, STEPS):
                    pe_down(pe, PASSES - 1, i)


KVC, QC, ROPE = 64, 96, 64
HALF = ROPE // 2
LOOKBACK = 8
T_EVEN, T_ODD, T_SIN_Q, T_COS, T_SIN, T_KEY = range(6)


class LatentState:

    def __init__(self, nc, ctx):
        def sb(name, shape, dt=F32):
            return ctx.enter_context(nc.sbuf_tensor(f"l_{name}", shape, dt))

        self.key = sb("key", [P, 2, BATCHES * P])
        self.val = sb("val", [P, BATCHES, 3 * KVC])
        self.mask = sb("mask", [P, BATCHES, P], F32R)
        self.wa_hi = sb("wa_hi", [QC, HEADS, P], F32R)
        self.wa_lo = sb("wa_lo", [QC, HEADS, P], F32R)
        self.wb_hi = sb("wb_hi", [QC, PAIRS, P], F32R)
        self.wb_lo = sb("wb_lo", [QC, PAIRS, P], F32R)
        self.wv_hi = sb("wv_hi", [P, PAIRS, D], F32R)
        self.wv_lo = sb("wv_lo", [P, PAIRS, D], F32R)
        self.tab = sb("tab", [P, 6, P])


def phase_latent_prepare(nc, e, ins, z, qc_hi, qc_lo):
    with ExitStack() as ctx:
        def sb(name, shape, dt=F32):
            return ctx.enter_context(nc.sbuf_tensor(f"k_{name}", shape, dt))

        def sem(name):
            return ctx.enter_context(nc.semaphore(f"k_{name}"))

        ctxT = sb("ctxT", [P, KT, BATCHES * P])
        wkvc = sb("wkvc", [P, KT, 2 * KVC])
        wkr = sb("wkr", [KVC, 2, P])
        uqT = sb("uqT", [P, HEADS, QC])
        ukT = sb("ukT", [P, HEADS, KVC])
        uvT = ukT
        wo = sb("wo", [P, HEADS, D])
        qr = sb("qr", [QC, HEADS, ROPE])
        qrb = sb("qrb", [QC, PAIRS, P])
        wdq = sb("wdq", [P, KT, QC])
        wdq_hi, wdq_lo = sb("wdq_hi", [P, KT, QC], F32R), sb("wdq_lo", [P, KT, QC], F32R)
        hT_hi, hT_lo = sb("hT_hi", [P, KT, GW], F32R), sb("hT_lo", [P, KT, GW], F32R)
        seg = sb("seg", [P, BATCHES], I32)
        segf = sb("segf", [P, BATCHES])
        dist = wo[:].rearrange("p h d -> p (h d)")[:, 0:BATCHES * P].rearrange("p (b k) -> p b k", b=BATCHES)
        kvT, rot, rot2 = (uqT[:].rearrange("p h c -> p (h c)")[:, n * GW:(n + 1) * GW] for n in range(3))
        bank = [ctx.enter_context(nc.psum_tensor(f"k_bank{i}", [P, GW], F32)) for i in range(8)]
        qc_ps, absorbed_ps, kvT_ps, kv_ps, kr_ps, wv_ps = bank[2:4], bank[4:6], bank[4], bank[5], bank[6:8], bank[4:8]
        nrm = Norm(nc, ctx, "k", e.stats, bank[0:2])

        absorb_in, wdq_in, ctx_in, rope_in, out_in, tab_in, seg_in = (
            sem(n) for n in ("absorb_in", "wdq_in", "ctx_in", "rope_in", "out_in", "tab_in", "seg_in"))
        absorbed, a_hi, a_lo, wv_done, wv_hi, wv_lo = (sem(n) for n in ("absorbed", "a_hi", "a_lo", "wv_done", "wv_hi", "wv_lo"))
        wdq_split, pool_chain, val_zero, mask_chain, masked = (
            sem(n) for n in ("wdq_split", "pool", "val_zero", "mask_chain", "masked"))
        kvT_done, kvT_sb, kr_done, kv_done = sem("kvT_done"), sem("kvT_sb"), sem("kr_done"), sem("kv_done")
        key_out, val_out, r1, r2, r3, rk_out = (sem(n) for n in ("key_out", "val_out", "r1", "r2", "r3", "rk_out"))
        qc_done, qc_hid, qc_lod = (sem(n) for n in ("qc_done", "qc_hid", "qc_lod"))

        def columns(g):
            return slice(g * GW, (g + 1) * GW)

        def absorbed_parts(t, half, odd):
            cols = slice(KVC, P) if odd else slice(0, KVC)
            src = absorbed_ps[half][0:QC, :].rearrange("q (h c) -> q h c", c=KVC)[:, odd::2]
            return t[:, 8 * half + odd:8 * half + 8:2, cols], src

        def output_parts(t, i):
            return t[:, 2 * i:2 * i + 2].rearrange("p a c -> p (a c)")

        def pe_absorb(pe):
            pe.wait_ge(absorb_in, 32)
            for h in range(HEADS):
                mm = pe.matmul(absorbed_ps[h // 8][0:QC, (h % 8) * KVC:(h % 8 + 1) * KVC], uqT[:, h], ukT[:, h],
                               start=True, stop=True)
            mm.then_inc(absorbed, 1)

        def pe_queries(pe, g):
            pe.wait_ge(nrm.lo_done, KT * (g + 1))
            pe.wait_ge(wdq_split, 2)
            if g >= 2:
                pe.wait_ge(qc_lod, g - 1)
            for k in range(KT):
                mm = parts(pe, qc_ps[g % 2][0:QC, :], wdq_hi[:, k], wdq_lo[:, k], hT_hi[:, k], hT_lo[:, k],
                           start=(k == 0), stop=(k == KT - 1))
            mm.then_inc(qc_done, 1)

        def pe_keys(pe, g):
            pe.wait_ge(ctx_in, 48)
            if g == 0:
                pe.wait_ge(a_lo, 4)
            else:
                pe.wait_ge(key_out, 2 * g)
            for k in range(KT):
                mm = pe.matmul(kvT_ps[:], wkvc[:, k], ctxT[:, k, columns(g)], start=(k == 0), stop=(k == KT - 1))
            mm.then_inc(kvT_done, 1)
            if g > 0:
                pe.wait_ge(val_out, g)
            for b in range(GROUP):
                t = g * GROUP + b
                for k in range(KT):
                    mm = pe.matmul(kv_ps[:, b * KVC:(b + 1) * KVC], ctxT[:, k, t * P:(t + 1) * P],
                                   wkvc[:, k, 0:KVC], start=(b == 0 and k == 0), stop=(k == KT - 1),
                                   skip_group_check=True)
            mm.then_inc(kv_done, 1)
            pe.wait_ge(kvT_sb, g + 1)
            if g > 0:
                pe.wait_ge(r2, g)
            pe.matmul(kr_ps[0][:], wkr[:, 0], kvT[0:KVC, :], start=True, stop=True)
            pe.matmul(kr_ps[1][:], wkr[:, 1], kvT[0:KVC, :], start=True, stop=True).then_inc(kr_done, 1)

        def pe_outputs(pe):
            pe.wait_ge(out_in, 32)
            pe.wait_ge(key_out, 2 * GROUPS)
            pe.wait_ge(val_out, GROUPS)
            pe.wait_ge(r2, GROUPS)
            for p in range(PAIRS):
                for odd in range(2):
                    mm = pe.matmul(wv_ps[p // 2][odd * KVC:(odd + 1) * KVC, (p % 2) * D:(p % 2 + 1) * D],
                                   uvT[:, 2 * p + odd], wo[:, 2 * p + odd], start=True, stop=True)
            mm.then_inc(wv_done, 1)

        def act_keys(act, g):
            act.wait_ge(kvT_done, g + 1)
            if g > 0:
                act.wait_ge(kr_done, g)
            act.activation(kvT, kvT_ps[:], ACT.Copy).then_inc(kvT_sb, 1)
            act.activation(z.key[0:KVC, 0, columns(g)], kvT_ps[0:KVC, :], ACT.Copy).then_inc(key_out, 1)
            act.activation(z.key[KVC:P, 1, columns(g)], kvT_ps[KVC:P, :], ACT.Copy).then_inc(key_out, 1)
            act.wait_ge(kv_done, g + 1)
            act.wait_ge(val_zero, 1)
            act.activation(z.val[:, g * GROUP:(g + 1) * GROUP, KVC:2 * KVC],
                           kv_ps[:, 0:GROUP * KVC].rearrange("p (b c) -> p b c", b=GROUP), ACT.Copy).then_inc(val_out, 1)

        def table(n):
            return z.tab[:, n].unsqueeze(1).broadcast_to([P, GROUP, P])

        def by_batch(a):
            return a.rearrange("p (b c) -> p b c", b=GROUP)

        def ve_keys(ve, g):
            ve.wait_ge(kr_done, g + 1)
            if g >= 1:
                ve.wait_ge(rk_out, 2 * g)
            ve.tensor_tensor(by_batch(rot2), by_batch(kr_ps[1][:]), table(T_SIN), ALU.mult).then_inc(r1, 1)
            ve.tensor_tensor(by_batch(rot), by_batch(kr_ps[0][:]), table(T_COS), ALU.mult).then_inc(r2, 1)
            ve.wait_ge(r1, g + 1)
            ve.wait_ge(r2, g + 1)
            ve.tensor_tensor(rot, rot, rot2, ALU.add).then_inc(r3, 1)
            ve.wait_ge(r3, g + 1)
            ve.tensor_copy(z.key[KVC:P, 0, columns(g)], rot[KVC:P, :]).then_inc(rk_out, 1)
            ve.tensor_copy(z.key[0:KVC, 1, columns(g)], rot[0:KVC, :]).then_inc(rk_out, 1)

        def ve_mask(ve):
            ve.wait_ge(seg_in, 16)
            ve.wait_ge(tab_in, 16)
            ve.tensor_copy(segf[:], seg[:]).then_inc(mask_chain, 1)
            ve.wait_ge(mask_chain, 1)
            keys = z.tab[:, T_KEY].unsqueeze(1).broadcast_to([P, BATCHES, P])
            ve.scalar_tensor_tensor(out=dist, in0=keys, scalar=LOOKBACK / 2,
                                    in1=segf[:].unsqueeze(2).broadcast_to([P, BATCHES, P]),
                                    op0=ALU.add, op1=ALU.subtract).then_inc(mask_chain, 1)
            ve.wait_ge(mask_chain, 2)
            ve.tensor_single_scalar(dist.bitcast(I32), dist.bitcast(I32), 0x7FFFFFFF, ALU.bitwise_and).then_inc(mask_chain, 1)
            ve.wait_ge(mask_chain, 3)
            ve.tensor_scalar(z.mask[:], dist, LOOKBACK / 2, -1.0e30, ALU.is_gt, ALU.mult).then_inc(masked, 1)

        with nc.Block() as block:
            @block.sync
            def _(sp):
                for dst, name, arrived in ((uqT, "uqT", absorb_in), (ukT, "ukT", absorb_in), (wdq, "wdq", wdq_in),
                                           (wkvc, "wkvc", ctx_in), (wkr, "wkr", ctx_in)):
                    sp.dma_start(dst[:], ins[name]).then_inc(arrived, 16)
                sp.dma_start(ctxT[:], ins["ctxT"].rearrange("(k p) t -> p k t", p=P)).then_inc(ctx_in, 16)
                for dst, name, arrived in ((qr, "qr", rope_in), (qrb, "qrb", rope_in)):
                    sp.dma_start(dst[:], ins[name]).then_inc(arrived, 16)
                sp.wait_ge(absorbed, 1)
                sp.dma_start(uvT[:], ins["uvT"]).then_inc(out_in, 16)
                sp.wait_ge(masked, 1)
                sp.dma_start(wo[:], ins["w_o2"]).then_inc(out_in, 16)

            @block.gpsimd
            def _(pool):
                links = [0]

                def link(instruction):
                    links[0] += 1
                    instruction.then_inc(pool_chain, 1)
                    pool.wait_ge(pool_chain, links[0])

                pool.wait_ge(wdq_in, 16)
                pool.tensor_scalar(wdq_hi[:], wdq[:], 1.0, None, ALU.mult).then_inc(wdq_split, 1)
                pool.wait_ge(wdq_split, 1)
                pool.tensor_tensor(wdq_lo[:], wdq[:], wdq_hi[:].bitcast(F32), ALU.subtract).then_inc(wdq_split, 1)
                pool.memset(z.val[:], 0.0).then_inc(val_zero, 1)
                pool.wait_ge(rope_in, 32)
                link(pool.tensor_scalar(z.wb_hi[:], qrb[:], 1.0, None, ALU.mult))
                pool.tensor_tensor(z.wb_lo[:], qrb[:], z.wb_hi[:].bitcast(F32), ALU.subtract)
                for odd in range(2):
                    cols = slice(0, ROPE) if odd else slice(KVC, P)
                    link(pool.tensor_scalar(z.wa_hi[:, odd::2, cols], qr[:, odd::2], 1.0, None, ALU.mult))
                    pool.tensor_tensor(z.wa_lo[:, odd::2, cols], qr[:, odd::2], z.wa_hi[:, odd::2, cols].bitcast(F32), ALU.subtract)

            @block.tensor
            def _(pe):
                pe_absorb(pe)
                norm_tensor(pe, nrm, e.ident[:], 0)
                for g in range(GROUPS):
                    pe_queries(pe, g)
                    if g + 1 < GROUPS:
                        norm_tensor(pe, nrm, e.ident[:], g + 1)
                    pe_keys(pe, g)
                pe_outputs(pe)

            @block.scalar
            def _(act):
                act.dma_start(seg[:], ins["seg"]).then_inc(seg_in, 16)
                act.dma_start(z.tab[:], ins["tab"]).then_inc(tab_in, 16)
                act.wait_ge(absorbed, 1)
                for half in range(2):
                    for odd in range(2):
                        out, src = absorbed_parts(z.wa_hi, half, odd)
                        act.activation(out, src, ACT.Copy).then_inc(a_hi, 1)
                norm_scalar(act, nrm, 0, e.X, True)
                norm_high(act, nrm, 0, hT_hi)
                norm_scalar(act, nrm, 1, e.X, True)
                for g in range(GROUPS):
                    act.wait_ge(qc_done, g + 1)
                    act.activation(qc_hi[:, columns(g)], qc_ps[g % 2][0:QC, :], ACT.Copy).then_inc(qc_hid, 1)
                    if g + 1 < GROUPS:
                        norm_high(act, nrm, g + 1, hT_hi)
                    if g + 2 < GROUPS:
                        norm_scalar(act, nrm, g + 2, e.X, True)
                    act_keys(act, g)
                act.wait_ge(wv_done, 1)
                for i in range(4):
                    act.activation(output_parts(z.wv_hi, i), wv_ps[i][:], ACT.Copy).then_inc(wv_hi, 1)

            @block.vector
            def _(ve):
                norm_statistics(ve, nrm, e.X, LN_EPS, True)
                for half in range(2):
                    for odd in range(2):
                        ve.wait_ge(a_hi, 2 * half + 2)
                        out, src = absorbed_parts(z.wa_lo, half, odd)
                        high, _ = absorbed_parts(z.wa_hi, half, odd)
                        ve.tensor_tensor(out, src, high.bitcast(F32), ALU.subtract).then_inc(a_lo, 1)
                norm_low(ve, nrm, 0, hT_hi, hT_lo)
                ve_mask(ve)
                for g in range(GROUPS):
                    ve.wait_ge(qc_hid, g + 1)
                    ve.tensor_tensor(qc_lo[:, columns(g)], qc_ps[g % 2][0:QC, :], qc_hi[:, columns(g)].bitcast(F32),
                                     ALU.subtract).then_inc(qc_lod, 1)
                    if g + 1 < GROUPS:
                        norm_low(ve, nrm, g + 1, hT_hi, hT_lo)
                    ve_keys(ve, g)
                for i in range(4):
                    ve.wait_ge(wv_hi, i + 1)
                    ve.tensor_tensor(output_parts(z.wv_lo, i), wv_ps[i][:], output_parts(z.wv_hi, i).bitcast(F32),
                                     ALU.subtract).then_inc(wv_lo, 1)


def phase_latent_attention(nc, e, z, qc_hi, qc_lo):
    AHEAD = 2
    with ExitStack() as ctx:
        def sb(name, shape, dt=F32):
            return ctx.enter_context(nc.sbuf_tensor(f"t_{name}", shape, dt))

        def sem(name):
            return ctx.enter_context(nc.semaphore(f"t_{name}"))

        val = sb("val", [P, GROUP, 3 * KVC])
        rot = sb("rot", [P, GW])
        q = sb("q", [P, 2, 2, GW])
        prob = sb("prob", [P, 2, 2, GROUP, P])
        pT = sb("pT", [P, 2, GW])
        c_hi = sb("c_hi", [P, 2, GW], F32R)
        c_lo = sb("c_lo", [P, 2, GW], F32R)
        nmax, sums, rec = (sb(n, [P, 2, 2, GROUP]) for n in ("nmax", "sums", "rec"))
        bank = [ctx.enter_context(nc.psum_tensor(f"t_bank{i}", [P, GW], F32)) for i in range(8)]
        b_ps, a_ps, pT_ps, sc_ps, wo_ps = bank[0], bank[1:3], bank[3], bank[4:6], bank[6:8]
        c_ps = b_ps

        rot_proj, rot_done, q_proj, cos_done, q_sum = (sem(n) for n in ("rot_proj", "rot_done", "q_proj", "cos_done", "q_sum"))
        scores_done, max_done, exp_done, rec_done, norm_even, norm_odd = (
            sem(n) for n in ("scores_done", "max_done", "exp_done", "rec_done", "norm_even", "norm_odd"))
        pT_done, pT_out, pv_done, c_hid, c_lod, wo_done, added, val_in = (
            sem(n) for n in ("pT_done", "pT_out", "pv_done", "c_hid", "c_lod", "wo_done", "added", "val_in"))

        def shifted(it, i, by, first, last):
            n = i + by
            if n < 0:
                return None if first else (it - 1, n + PAIRS)
            if n >= PAIRS:
                return None if last else (it + 1, n - PAIRS)
            return it, n

        def known_before(it, i, n):
            return isinstance(it, int) and it * PAIRS + i < n

        def columns(it):
            return slice(it * GW, (it + 1) * GW) if isinstance(it, int) else ds(it * GW, GW)

        def pe_rot(pe, it, i):
            S = it * PAIRS + i
            if not known_before(it, i, AHEAD + 2):
                pe.wait_ge(c_lod, S - AHEAD - 1)
            elif S > 0:
                pe.wait_ge(rot_done, S)
            parts(pe, b_ps[:], z.wb_hi[:, i], z.wb_lo[:, i], qc_hi[:, columns(it)], qc_lo[:, columns(it)],
                  start=True, stop=True).then_inc(rot_proj, 1)

        def pe_query(pe, it, i, h):
            S = it * PAIRS + i
            if not known_before(it, i, 1):
                pe.wait_ge(cos_done, 2 * S - 1 + h)
            parts(pe, a_ps[h][:], z.wa_hi[:, 2 * i + h], z.wa_lo[:, 2 * i + h], qc_hi[:, columns(it)],
                  qc_lo[:, columns(it)], start=True, stop=True).then_inc(q_proj, 1)

        def pe_scores(pe, it, i):
            S = it * PAIRS + i
            for h in range(2):
                pe.wait_ge(q_sum, 2 * S + h + 1)
                if not known_before(it, i, 1):
                    pe.wait_ge(exp_done, GROUP * (2 * S - 1 + h))
                for b in range(GROUP):
                    c = slice(b * P, (b + 1) * P)
                    keys = (it * GROUP + b) * P
                    at = slice(keys, keys + P) if isinstance(it, int) else ds(keys, P)
                    pe.matmul(sc_ps[h][:, c], q[:, i % 2, h, c], z.key[:, h, at], start=(b == 0), stop=False,
                              skip_group_check=True)
                pe.matmul(sc_ps[h][:].rearrange("p (b k) -> p b k", b=GROUP), e.ident_r[:],
                          z.mask[:, ds(it * GROUP, GROUP)], start=False, stop=True, skip_group_check=True)\
                    .then_inc(scores_done, 1)

        def pe_turn(pe, it, i, h):
            S = it * PAIRS + i
            pe.wait_ge((norm_even, norm_odd)[h], S + 1)
            if h == 1:
                pe.wait_ge(pT_out, 2 * S + 1)
            elif not known_before(it, i, 1):
                pe.wait_ge(pT_out, 2 * S)
            for b in range(GROUP):
                mm = pe.transpose(pT_ps[:, b * P:(b + 1) * P], prob[:, i % 2, h, b], e.ident[:])
            mm.then_inc(pT_done, 1)

        def pe_values(pe, it, i, ahead):
            S = it * PAIRS + i
            if i == 0:
                pe.wait_ge(val_in, it + 1)
            if ahead:
                pe.wait_ge(rot_done, S + AHEAD + 2)
            else:
                pe.wait_ge(c_lod, S)
            for h in range(2):
                pe.wait_ge(pT_out, 2 * S + h + 1)
                block_of = slice(KVC, 3 * KVC) if h == 0 else slice(0, 2 * KVC)
                for b in range(GROUP):
                    c = slice(b * P, (b + 1) * P)
                    mm = pe.matmul(c_ps[:, c], val[:, b, block_of], pT[:, h, c], start=(h == 0 and b == 0), stop=(h == 1),
                                   skip_group_check=True)
            mm.then_inc(pv_done, 1)

        def pe_out(pe, it, i):
            S = it * PAIRS + i
            pe.wait_ge(c_lod, S + 1)
            if i == 0 and not known_before(it, i, 1):
                pe.wait_ge(added, 2 * it)
            for b in range(GROUP):
                c = slice(b * P, (b + 1) * P)
                mm = parts(pe, wo_ps[b // 2][:, (b % 2) * D:(b % 2 + 1) * D], c_hi[:, i % 2, c], c_lo[:, i % 2, c],
                           z.wv_hi[:, i], z.wv_lo[:, i], start=(i == 0 and b % 2 == 0), stop=(i == PAIRS - 1))
            mm.then_inc(wo_done, 1)

        def pe_pass(pe, it, first=False, last=False):
            for i in range(PAIRS):
                before, before2 = shifted(it, i, -1, first, last), shifted(it, i, -2, first, last)
                ahead = shifted(it, i, AHEAD, first, last)
                pe_scores(pe, it, i)
                if before:
                    pe_turn(pe, *before, 0)
                if ahead:
                    pe_rot(pe, *ahead)
                    pe_query(pe, *ahead, 0)
                if before:
                    pe_turn(pe, *before, 1)
                if ahead:
                    pe_query(pe, *ahead, 1)
                if before:
                    pe_values(pe, *before, ahead=ahead is not None)
                if before2:
                    pe_out(pe, *before2)

        def act_exp(act, it, i, h):
            S = it * PAIRS + i
            act.wait_ge(max_done, 2 * S + h + 1)
            for b in range(GROUP):
                act.activation(prob[:, i % 2, h, b], sc_ps[h][:, b * P:(b + 1) * P], ACT.Exp, bias=nmax[:, i % 2, h, b:b + 1],
                               accum_out=sums[:, i % 2, h, b:b + 1]).then_inc(exp_done, 1)

        def act_turn(act, it, i, h):
            act.wait_ge(pT_done, 2 * (it * PAIRS + i) + h + 1)
            act.activation(pT[:, h], pT_ps[:], ACT.Copy).then_inc(pT_out, 1)

        def act_values(act, it, i):
            act.wait_ge(pv_done, it * PAIRS + i + 1)
            act.activation(c_hi[:, i % 2], c_ps[:], ACT.Copy).then_inc(c_hid, 1)

        def act_pass(act, it, first=False, last=False):
            for i in range(PAIRS):
                before = shifted(it, i, -1, first, last)
                act_exp(act, it, i, 0)
                if before:
                    act_turn(act, *before, 0)
                    act_turn(act, *before, 1)
                act_exp(act, it, i, 1)
                if before:
                    act_values(act, *before)

        def ve_rot(ve, it, i):
            S = it * PAIRS + i
            ve.wait_ge(rot_proj, S + 1)
            if not known_before(it, i, 1):
                ve.wait_ge(q_sum, 2 * S)
            ve.tensor_tensor(by_batch(rot[:]), by_batch(b_ps[:]), table(T_SIN_Q), ALU.mult).then_inc(rot_done, 1)

        def ve_cos(ve, it, i, h):
            S = it * PAIRS + i
            ve.wait_ge(q_proj, 2 * S + h + 1)
            if not known_before(it, i, AHEAD):
                ve.wait_ge(scores_done, 2 * (S - AHEAD) + h + 1)
            ve.tensor_tensor(by_batch(q[:, i % 2, h]), by_batch(a_ps[h][:]), table((T_EVEN, T_ODD)[h]), ALU.mult).then_inc(cos_done, 1)

        def table(n):
            return z.tab[:, n].unsqueeze(1).broadcast_to([P, GROUP, P])

        def by_batch(a):
            return a.rearrange("p (b c) -> p b c", b=GROUP)

        def ve_rec(ve, it, i, h):
            S = it * PAIRS + i
            ve.wait_ge(exp_done, GROUP * (2 * S + h + 1))
            ve.reciprocal(rec[:, i % 2, h], sums[:, i % 2, h]).then_inc(rec_done, 1)

        def ve_norm_odd(ve, it, i):
            ve.wait_ge(rec_done, 2 * (it * PAIRS + i) + 2)
            ve.tensor_tensor(prob[:, i % 2, 1], prob[:, i % 2, 1], over_groups(rec[:, i % 2, 1]), ALU.mult).then_inc(norm_odd, 1)

        def ve_values(ve, it, i):
            ve.wait_ge(c_hid, it * PAIRS + i + 1)
            ve.tensor_tensor(c_lo[:, i % 2], c_ps[:], c_hi[:, i % 2].bitcast(F32), ALU.subtract).then_inc(c_lod, 1)

        def ve_group_values(ve, it, first):
            if not first:
                ve.wait_ge(pv_done, it * PAIRS)
            ve.tensor_copy(val[:].rearrange("p b c -> p (b c)"),
                           z.val[:, ds(it * GROUP, GROUP)].rearrange("p b c -> p (b c)")).then_inc(val_in, 1)

        def ve_add(ve, it):
            ve.wait_ge(wo_done, it * PAIRS + PAIRS)
            for n in range(2):
                x = e.X[:, ds(it * GROUP + 2 * n, 2)].rearrange("p t d -> p (t d)")
                ve.tensor_tensor(x, wo_ps[n][:], x, ALU.add).then_inc(added, 1)

        def ve_pass(ve, it, first=False, last=False):
            for i in range(PAIRS):
                S = it * PAIRS + i
                before, ahead = shifted(it, i, -1, first, last), shifted(it, i, AHEAD, first, last)
                for h in range(2):
                    ve.wait_ge(scores_done, 2 * S + h + 1)
                    ve.tensor_reduce(nmax[:, i % 2, h], by_batch(sc_ps[h][:]), X_AXIS, ALU.max, negate=True).then_inc(max_done, 1)
                if ahead:
                    ve_rot(ve, *ahead)
                    ve_cos(ve, *ahead, 0)
                ve_rec(ve, it, i, 0)
                if ahead:
                    ve_cos(ve, *ahead, 1)
                ve_rec(ve, it, i, 1)
                ve_norm_odd(ve, it, i)
                if before:
                    ve_values(ve, *before)
                if i == 0:
                    ve_group_values(ve, it, first)
                if i == 1 and not first:
                    ve_add(ve, it - 1)
                if i >= 2 and last:
                    if i == 2:
                        ve.wait_ge(added, 2 * (GROUPS - 1))
                    early_statistics(ve, e.stats, e.X, i - 2, PAIRS - 2)

        def pool_sum(pool, it, i, h):
            S = it * PAIRS + i
            rows = slice(KVC, P) if h == 0 else slice(0, ROPE)
            pool.wait_ge(rot_done, S + 1)
            pool.wait_ge(cos_done, 2 * S + h + 1)
            if h == 1:
                pool.wait_ge(q_sum, 2 * S + 1)
            elif not known_before(it, i, 1):
                pool.wait_ge(q_sum, 2 * S)
                if not known_before(it, i, AHEAD):
                    pool.wait_ge(norm_even, S - AHEAD + 1)
            pool.tensor_tensor(q[rows, i % 2, h], q[rows, i % 2, h], rot[rows, :], ALU.add).then_inc(q_sum, 1)

        def pool_pass(pool, it, first=False, last=False):
            for i in range(PAIRS):
                S = it * PAIRS + i
                ahead = shifted(it, i, AHEAD, first, last)
                pool.wait_ge(rec_done, 2 * S + 1)
                pool.tensor_tensor(prob[:, i % 2, 0], prob[:, i % 2, 0], over_groups(rec[:, i % 2, 0]), ALU.mult).then_inc(norm_even, 1)
                if ahead:
                    pool_sum(pool, *ahead, 0)
                    pool_sum(pool, *ahead, 1)

        with nc.Block() as block:
            @block.gpsimd
            def _(pool):
                for i in range(AHEAD):
                    for h in range(2):
                        pool_sum(pool, 0, i, h)
                pool_pass(pool, 0, first=True)
                with pool.Fori(1, GROUPS - 1) as it:
                    pool_pass(pool, it)
                pool_pass(pool, GROUPS - 1, last=True)

            @block.scalar
            def _(act):
                act_pass(act, 0, first=True)
                with act.Fori(1, GROUPS - 1) as it:
                    act_pass(act, it)
                act_pass(act, GROUPS - 1, last=True)
                for h in range(2):
                    act_turn(act, GROUPS - 1, PAIRS - 1, h)
                act_values(act, GROUPS - 1, PAIRS - 1)

            @block.vector
            def _(ve):
                for i in range(AHEAD):
                    ve_rot(ve, 0, i)
                    ve_cos(ve, 0, i, 0)
                    ve_cos(ve, 0, i, 1)
                ve_pass(ve, 0, first=True)
                with ve.Fori(1, GROUPS - 1) as it:
                    ve_pass(ve, it)
                ve_pass(ve, GROUPS - 1, last=True)
                ve_values(ve, GROUPS - 1, PAIRS - 1)
                ve_add(ve, GROUPS - 1)

            @block.tensor
            def _(pe):
                for i in range(AHEAD):
                    pe_rot(pe, 0, i)
                    pe_query(pe, 0, i, 0)
                    pe_query(pe, 0, i, 1)
                pe_pass(pe, 0, first=True)
                with pe.Fori(1, GROUPS - 1) as it:
                    pe_pass(pe, it)
                pe_pass(pe, GROUPS - 1, last=True)
                for h in range(2):
                    pe_turn(pe, GROUPS - 1, PAIRS - 1, h)
                pe_values(pe, GROUPS - 1, PAIRS - 1, ahead=False)
                pe_out(pe, GROUPS - 1, PAIRS - 2)
                pe_out(pe, GROUPS - 1, PAIRS - 1)


FFN = 1024
BLOCK = 32
FP8_MAX = 448.0
FP8_EPS = 1e-30
FP8_LEAST = 2.0 ** -6
TO_EIGHTHS = 1.5 * 2.0 ** 20
EXPONENT = 0x7F800000


class Quantizer:

    def __init__(self, nc, ctx, tag, width, room=None):
        def sb(name, shape, dt=F32):
            return ctx.enter_context(nc.sbuf_tensor(f"{tag}_{name}", shape, dt))

        n = width // BLOCK
        self.n = n
        self.top, self.scale, self.inverse = sb("top", [P, n]), sb("scale", [P, n]), sb("inverse", [P, n])
        if room is None:
            room = sb("room", [P, 2 * width])
        self.quot, self.magic = room[:, 0:width], room[:, width:2 * width]
        self.scaled, self.quotients, self.rounded, self.whole, self.restored, self.chain = (
            ctx.enter_context(nc.semaphore(f"{tag}_{s}"))
            for s in ("scaled", "quotients", "rounded", "whole", "restored", "chain"))

    def blocks(self, a):
        return a.rearrange("p (n w) -> p n w", w=BLOCK)

    def spread(self, a):
        return a.unsqueeze(2).broadcast_to([P, self.n, BLOCK])

    LINKS = 4

    def link(self, ve, at, k, instruction):
        instruction.then_inc(self.chain, 1)
        ve.wait_ge(self.chain, at * self.LINKS + k)

    def scales(self, ve, at, src):
        self.link(ve, at, 1, ve.tensor_reduce(self.top[:], self.blocks(src), X_AXIS, ALU.max, apply_absolute_value=True))
        if not (isinstance(at, int) and at == 0):
            ve.wait_ge(self.restored, at)
        self.link(ve, at, 2, ve.tensor_scalar(self.scale[:], self.top[:], 1.0 / FP8_MAX, FP8_EPS, ALU.mult, ALU.max))
        ve.reciprocal(self.inverse[:], self.scale[:]).then_inc(self.scaled, 1)

    def quotient(self, pool, at, src):
        pool.wait_ge(self.scaled, at + 1)
        pool.tensor_tensor(self.blocks(self.quot[:]), self.blocks(src), self.spread(self.inverse[:]),
                           ALU.mult).then_inc(self.quotients, 1)

    def round(self, ve, at):
        ve.wait_ge(self.quotients, at + 1)
        self.link(ve, at, 3, ve.tensor_single_scalar(self.magic[:].bitcast(I32), self.quot[:].bitcast(I32), EXPONENT,
                                                     ALU.bitwise_and))
        self.link(ve, at, 4, ve.tensor_scalar(self.magic[:], self.magic[:], FP8_LEAST, TO_EIGHTHS, ALU.max, ALU.mult))
        ve.tensor_tensor(self.quot[:], self.quot[:], self.magic[:], ALU.add).then_inc(self.rounded, 1)

    def restore(self, pool, at, out):
        pool.wait_ge(self.rounded, at + 1)
        pool.tensor_tensor(self.quot[:], self.quot[:], self.magic[:], ALU.subtract).then_inc(self.whole, 1)
        pool.wait_ge(self.whole, at + 1)
        pool.tensor_tensor(self.blocks(out), self.blocks(self.quot[:]), self.spread(self.scale[:]),
                           ALU.mult).then_inc(self.restored, 1)


class RawFfnWeights:

    CHUNKS = 6
    WIDTH = 1024

    def __init__(self, nc, ctx):
        self.raw = ctx.enter_context(nc.sbuf_tensor("fw_raw", [P, self.CHUNKS, self.WIDTH], F32))
        self.w_in = ctx.enter_context(nc.semaphore("fw_in"))


class FfnWeights:
    def __init__(self, nc, ctx):
        def sb(name, shape):
            return ctx.enter_context(nc.sbuf_tensor(f"f_{name}", shape, F32R))

        self.gu_hi, self.gu_lo = sb("gu_hi", [P, 2, KT, FFN]), sb("gu_lo", [P, 2, KT, FFN])
        self.down_hi, self.down_lo = sb("down_hi", [P, FFN // P, D]), sb("down_lo", [P, FFN // P, D])


def phase_ffn_weights(nc, e, raw, w):
    CHUNKS = RawFfnWeights.CHUNKS
    with ExitStack() as ctx:
        bank = [ctx.enter_context(nc.psum_tensor(f"fw_bank{i}", [P, GW], F32)) for i in range(8)]
        turned, hi_done, lo_done = (ctx.enter_context(nc.semaphore(f"fw_{n}")) for n in ("turned", "hi_done", "lo_done"))

        def target(t, c, m):
            if c < 4:
                half = (c % 2) * GW
                return t[0][:, c // 2, m, half:half + GW].rearrange("p (a b) -> p a b", a=GROUP)
            return t[1][:, 4 * m:4 * m + 4, (c - 4) * P:(c - 3) * P]

        his, los = (w.gu_hi, w.down_hi), (w.gu_lo, w.down_lo)

        def halves(c):
            return [(m, bank[2 * (c % 4) + m]) for m in range(2)]

        def by_tile(a):
            return a[:].rearrange("p (a b) -> p a b", a=GROUP)

        with nc.Block() as block:
            @block.tensor
            def _(pe):
                for c in range(CHUNKS):
                    if c >= 4:
                        pe.wait_ge(lo_done, 2 * (c - 3))
                    for m, ps in halves(c):
                        for a in range(GROUP):
                            at = (a * KT + m) * P if c < 4 else (4 * m + a) * P
                            mm = pe.transpose(ps[:, a * P:(a + 1) * P], raw[:, c, at:at + P], e.ident[:])
                    mm.then_inc(turned, 1)

            @block.scalar
            def _(act):
                for c in range(CHUNKS):
                    act.wait_ge(turned, c + 1)
                    for m, ps in halves(c):
                        act.activation(target(his, c, m), by_tile(ps), ACT.Copy).then_inc(hi_done, 1)

            @block.vector
            def _(ve):
                for c in range(CHUNKS):
                    for m, ps in halves(c):
                        ve.wait_ge(hi_done, 2 * c + m + 1)
                        ve.tensor_tensor(target(los, c, m), by_tile(ps), target(his, c, m).bitcast(F32),
                                         ALU.subtract).then_inc(lo_done, 1)


def phase_ffn(nc, e, w, out):
    PASSES = BATCHES // 2
    with ExitStack() as ctx:
        def sb(name, shape, dt=F32):
            return ctx.enter_context(nc.sbuf_tensor(f"o_{name}", shape, dt))

        def sem(name):
            return ctx.enter_context(nc.semaphore(f"o_{name}"))

        mv = sb("mv", [P, BATCHES, 2])
        va, rs, nt, nu = (sb(n, [P, BATCHES]) for n in ("va", "rs", "nt", "nu"))
        xn = sb("xn", [P, 2, D])
        xT_hi, xT_lo = sb("xT_hi", [P, 2, KT, P], F32R), sb("xT_lo", [P, 2, KT, P], F32R)
        act_out = sb("act_out", [P, FFN])
        inner = sb("inner", [P, 2, FFN])
        iT_hi, iT_lo = sb("iT_hi", [P, FFN // P, P], F32R), sb("iT_lo", [P, FFN // P, P], F32R)
        bank = [ctx.enter_context(nc.psum_tensor(f"o_bank{i}", [P, GW], F32)) for i in range(8)]
        g_ps, u_ps, xT_ps, iT_ps, o_ps = bank[0:2], bank[2:4], bank[4], bank[5:7], bank[7]
        qx, qi = Quantizer(nc, ctx, "ox", D), Quantizer(nc, ctx, "oi", FFN)

        stats_chain, ready, x_turned, x_hid, x_lod = (sem(n) for n in ("stats", "ready", "x_turned", "x_hid", "x_lod"))
        up_done, silu_done, inner_done = sem("up_done"), sem("silu_done"), sem("inner_done")
        i_turned, i_hid, i_lod, down_done, added, stored = (sem(n) for n in ("i_turned", "i_hid", "i_lod", "down_done", "added", "stored"))

        def tile_of(x, t):
            return x[:, ds(t, 1)].rearrange("p a d -> p (a d)")

        def first_tile(t):
            return isinstance(t, int) and t == 0

        def ve_input_a(ve, t, par):
            if not (isinstance(t, int) and t < 2):
                ve.wait_ge(x_turned, t - 1)
            ve.tensor_scalar(xn[:, par], tile_of(e.X, t), mv[:, ds(t, 1), 0], rs[:, ds(t, 1)], ALU.subtract, ALU.mult)\
                .then_inc(ready, 1)
            ve.wait_ge(ready, t + 1)
            qx.scales(ve, t, xn[:, par])

        def ve_input_b(ve, t, par):
            qx.round(ve, t)

        def ve_input_c(ve, t, par):
            ve.wait_ge(x_hid, t + 1)
            ve.tensor_tensor(xT_lo[:, par].rearrange("p k c -> p (k c)"), xT_ps[:, 0:D],
                             xT_hi[:, par].rearrange("p k c -> p (k c)").bitcast(F32), ALU.subtract).then_inc(x_lod, 1)

        def pool_input_a(pool, t, par):
            qx.quotient(pool, t, xn[:, par])

        def pool_input_b(pool, t, par):
            qx.restore(pool, t, xn[:, par])

        def pe_input(pe, t, par):
            pe.wait_ge(qx.restored, t + 1)
            if not first_tile(t):
                pe.wait_ge(x_lod, t)
            for k in range(KT):
                mm = pe.transpose(xT_ps[:, k * P:(k + 1) * P], xn[:, par, k * P:(k + 1) * P], e.ident[:])
            mm.then_inc(x_turned, 1)

        def act_input(act, t, par):
            act.wait_ge(x_turned, t + 1)
            if not (isinstance(t, int) and t < 2):
                act.wait_ge(up_done, 2 * t - 2)
            act.activation(xT_hi[:, par].rearrange("p k c -> p (k c)"), xT_ps[:, 0:D], ACT.Copy).then_inc(x_hid, 1)

        def pe_up(pe, t, par):
            pe.wait_ge(x_lod, t + 1)
            if not first_tile(t):
                pe.wait_ge(silu_done, 2 * t)
                pe.wait_ge(inner_done, 2 * t)
            for half in range(2):
                cols = slice(half * GW, (half + 1) * GW)
                for a, ps in ((0, g_ps[half]), (1, u_ps[half])):
                    for k in range(KT):
                        mm = parts(pe, ps[:], xT_hi[:, par, k], xT_lo[:, par, k], w.gu_hi[:, a, k, cols], w.gu_lo[:, a, k, cols],
                                   start=(k == 0), stop=(k == KT - 1))
                mm.then_inc(up_done, 1)

        def act_silu(act, t, par):
            for half in range(2):
                act.wait_ge(up_done, 2 * t + half + 1)
                if not first_tile(t):
                    act.wait_ge(inner_done, 2 * t - 1 + half)
                act.activation(act_out[:, half * GW:(half + 1) * GW], g_ps[half][:], ACT.Silu).then_inc(silu_done, 1)

        def ve_inner(ve, t, par):
            if not (isinstance(t, int) and t < 2):
                ve.wait_ge(i_turned, t - 1)
            for half in range(2):
                cols = slice(half * GW, (half + 1) * GW)
                ve.wait_ge(silu_done, 2 * t + half + 1)
                ve.tensor_tensor(inner[:, par, cols], u_ps[half][:], act_out[:, cols], ALU.mult).then_inc(inner_done, 1)

        def ve_scales(ve, t, par):
            ve.wait_ge(inner_done, 2 * t + 2)
            qi.scales(ve, t, inner[:, par])

        def pe_turn(pe, t, par):
            pe.wait_ge(qi.restored, t + 1)
            if not first_tile(t):
                pe.wait_ge(i_lod, 2 * t)
            for half in range(2):
                for a in range(GROUP):
                    i = half * GROUP + a
                    mm = pe.transpose(iT_ps[half][:, a * P:(a + 1) * P], inner[:, par, i * P:(i + 1) * P], e.ident[:])
            mm.then_inc(i_turned, 1)

        def act_turn(act, t):
            act.wait_ge(i_turned, t + 1)
            if not first_tile(t):
                act.wait_ge(down_done, t)
            for half in range(2):
                act.activation(iT_hi[:, 4 * half:4 * half + 4].rearrange("p a c -> p (a c)"), iT_ps[half][:], ACT.Copy).then_inc(i_hid, 1)

        def ve_turn(ve, t):
            for half in range(2):
                ve.wait_ge(i_hid, 2 * t + half + 1)
                ve.tensor_tensor(iT_lo[:, 4 * half:4 * half + 4].rearrange("p a c -> p (a c)"), iT_ps[half][:],
                                 iT_hi[:, 4 * half:4 * half + 4].rearrange("p a c -> p (a c)").bitcast(F32),
                                 ALU.subtract).then_inc(i_lod, 1)

        def pe_down(pe, t):
            if not first_tile(t):
                pe.wait_ge(added, t)
            for i in range(FFN // P):
                if i % GROUP == 0:
                    pe.wait_ge(i_lod, 2 * t + i // GROUP + 1)
                mm = parts(pe, o_ps[:, 0:D], iT_hi[:, i], iT_lo[:, i], w.down_hi[:, i], w.down_lo[:, i],
                           start=(i == 0), stop=(i == FFN // P - 1))
            mm.then_inc(down_done, 1)

        def ve_add(ve, t):
            ve.wait_ge(down_done, t + 1)
            x = tile_of(e.X, t)
            ve.tensor_tensor(x, o_ps[:, 0:D], x, ALU.add).then_inc(added, 1)

        def each(it):
            for par in range(2):
                t = 2 * it + par

                def tile(n, t=t):
                    return None if isinstance(t, int) and not 0 <= t + n < BATCHES else t + n

                yield par, tile

        def pe_pass(pe, it):
            for par, tile in each(it):
                pe_up(pe, tile(0), par)
                if tile(1) is not None:
                    pe_input(pe, tile(1), 1 - par)
                if tile(-2) is not None:
                    pe_down(pe, tile(-2))
                if tile(-1) is not None:
                    pe_turn(pe, tile(-1), 1 - par)

        def act_pass(act, it):
            for par, tile in each(it):
                act_silu(act, tile(0), par)
                if tile(1) is not None:
                    act_input(act, tile(1), 1 - par)
                if tile(-1) is not None:
                    act_turn(act, tile(-1))

        def ve_pass(ve, it):
            for par, tile in each(it):
                ve_inner(ve, tile(0), par)
                if tile(1) is not None:
                    ve_input_c(ve, tile(1), 1 - par)
                ve_scales(ve, tile(0), par)
                if tile(2) is not None:
                    ve_input_b(ve, tile(2), par)
                if tile(-1) is not None:
                    ve_turn(ve, tile(-1))
                qi.round(ve, tile(0))
                if tile(3) is not None:
                    ve_input_a(ve, tile(3), 1 - par)
                if tile(-2) is not None:
                    ve_add(ve, tile(-2))

        def pool_pass(pool, it):
            for par, tile in each(it):
                qi.quotient(pool, tile(0), inner[:, par])
                if tile(2) is not None:
                    pool_input_b(pool, tile(2), par)
                qi.restore(pool, tile(0), inner[:, par])
                if tile(3) is not None:
                    pool_input_a(pool, tile(3), 1 - par)

        def passes(engine, one_pass):
            one_pass(engine, 0)
            one_pass(engine, 1)
            with engine.Fori(2, PASSES - 2) as it:
                one_pass(engine, it)
            one_pass(engine, PASSES - 2)
            one_pass(engine, PASSES - 1)

        with nc.Block() as block:
            @block.vector
            def _(ve):
                links = [0]

                def link(instruction):
                    links[0] += 1
                    instruction.then_inc(stats_chain, 1)
                    ve.wait_ge(stats_chain, links[0])

                for t in range(EARLY, BATCHES):
                    last = ve.bn_stats(e.stats[:, t], e.X[:, t])
                link(last)
                for t in range(BATCHES):
                    last = ve.bn_aggr(mv[:, t], e.stats[:, t])
                link(last)
                link(ve.tensor_scalar(va[:], mv[:, :, 1], LN_EPS, None, ALU.add))
                rsqrt_steps(ve, link, va[:], rs[:], nt[:], nu[:])
                for t in range(2):
                    ve_input_a(ve, t, t)
                    ve_input_b(ve, t, t)
                ve_input_c(ve, 0, 0)
                ve_input_a(ve, 2, 0)
                passes(ve, ve_pass)
                ve_turn(ve, BATCHES - 1)
                ve_add(ve, BATCHES - 2)
                ve_add(ve, BATCHES - 1)

            @block.gpsimd
            def _(pool):
                for t in range(2):
                    pool_input_a(pool, t, t)
                    pool_input_b(pool, t, t)
                pool_input_a(pool, 2, 0)
                passes(pool, pool_pass)

            @block.scalar
            def _(act):
                act_input(act, 0, 0)
                passes(act, act_pass)
                act_turn(act, BATCHES - 1)

            @block.tensor
            def _(pe):
                pe_input(pe, 0, 0)
                passes(pe, pe_pass)
                pe_down(pe, BATCHES - 2)
                pe_turn(pe, BATCHES - 1, 1)
                pe_down(pe, BATCHES - 1)

            @block.sync
            def _(sp):
                with sp.Fori(0, BATCHES) as t:
                    sp.wait_ge(added, t + 1)
                    sp.dma_start(out[ds(t, 1)].rearrange("a p d -> p (a d)"), tile_of(e.X, t)).then_inc(stored, 16)
                sp.wait_ge(stored, 16 * BATCHES)


def attention_state(nc, ctx):
    w = Env()

    def sb(name, shape, dt=F32):
        return ctx.enter_context(nc.sbuf_tensor(name, shape, dt))

    w.hT_hi = sb("hT_hi", [P, KT, BATCHES * P], F32R)
    w.hT_lo = sb("hT_lo", [P, KT, BATCHES * P], F32R)
    w.raw = sb("w_raw", [P, 2, 4, KT, D])
    w.hi = sb("w_hi", [P, 2, 4, KT, D], F32R)
    w.lo = sb("w_lo", [P, 2, 4, KT, D], F32R)
    w.causal = sb("causal", [P, P])
    w.ln1 = sb("ln1", [P, KT])
    return w


def clear_semaphores(nc):
    used = sorted(nc.released_uncleared_semaphores)
    with nc.Block() as block:
        @block.gpsimd
        def _(pool):
            pool.sem_clear(range(used[0], used[-1] + 1))


def build_program(nc, ins, out):
    with ExitStack() as ctx:
        e = constants_and_state(nc, ctx, ins)
        fw = RawFfnWeights(nc, ctx)
        with ExitStack() as c0:
            mw = MoeWeights(nc, c0)
            e.Y = c0.enter_context(nc.sbuf_tensor("Y", [P, BATCHES, D], F32))
            with ExitStack() as c1:
                w = attention_state(nc, c1)
                phase_a(nc, e, ins, w, mw, fw)
                phase_attention(nc, e, ins, w, mw, fw)
            phase_moe(nc, e, ins, mw)
        with ExitStack() as c2:
            z = LatentState(nc, c2)
            qc_hi = c2.enter_context(nc.sbuf_tensor("qc_hi", [QC, BATCHES * P], F32R))
            qc_lo = c2.enter_context(nc.sbuf_tensor("qc_lo", [QC, BATCHES * P], F32R))
            phase_latent_prepare(nc, e, ins, z, qc_hi, qc_lo)
            phase_latent_attention(nc, e, z, qc_hi, qc_lo)
        with ExitStack() as c3:
            wf = FfnWeights(nc, c3)
            clear_semaphores(nc)
            phase_ffn_weights(nc, e, fw.raw, wf)
            phase_ffn(nc, e, wf, out)


def layouts(i):
    import numpy as np

    def by_pair(m):
        return m.reshape(KT, P, PAIRS, 2 * HD).transpose(1, 2, 0, 3)

    fill = np.zeros((TILES * P - EXPERTS * EI - SI, D), np.float32)

    def rows(experts, shared):
        return np.concatenate([experts.reshape(EXPERTS * EI, D), shared, fill]).reshape(TILES, P, D)

    up = [rows(i["L0_ffn_eg_w"], i["L0_ffn_sg_w"]), rows(i["L0_ffn_eu_w"], i["L0_ffn_su_w"])]
    up = [m.reshape(TILES, P, KT, P).transpose(3, 0, 2, 1).reshape(P, TILES, KT * P) for m in up]
    down = rows(i["L0_ffn_ed_w"].transpose(0, 2, 1), i["L0_ffn_sd_w"].T).transpose(1, 0, 2)
    owner = np.minimum(np.arange(TILES * P) // EI, EXPERTS)
    rows_of = np.arange(P)[:, None]
    sel = ((rows_of == owner[None]) | (rows_of - CW_LOW == owner[None])).astype(np.float32).reshape(P, TILES, P)
    w_moe = np.concatenate([*up, down, sel], axis=2)
    wo = i["L0_ffn_wo"].reshape(PAIRS, 2, P, D).transpose(2, 0, 1, 3)
    inv = (1.0 / np.float32(10000.0) ** (np.arange(HALF, dtype=np.float32) / np.float32(HALF))).astype(np.float32)
    ang = (inv[:, None] * np.arange(P, dtype=np.float32)[None]).astype(np.float32)
    cos = np.tile(np.cos(ang), (2 * P // ROPE, 1))
    sin = np.tile(np.concatenate([-np.sin(ang), np.sin(ang)]), (P // ROPE, 1))
    one = np.ones((KVC, P), np.float32)
    scale = np.float32(1.0) / np.sqrt(np.float32(HD + ROPE))
    key = np.tile(np.arange(P, dtype=np.float32), (P, 1))
    tab = np.stack([scale * np.concatenate([one, cos[KVC:]]), scale * np.concatenate([cos[:ROPE], one]), scale * sin,
                    cos, sin, key], axis=1).astype(np.float32)

    def swap(m):
        return np.concatenate([m[..., HALF:], m[..., :HALF]], axis=-1)

    qr = i["L1_xattn_W_qr"].reshape(QC, HEADS, ROPE)
    kr = i["L1_xattn_W_kr"]
    kvc = i["L1_xattn_W_kvc"].reshape(KT, P, KVC).transpose(1, 0, 2)
    gate, up = (i[f"L1_ffn_{n}_w"].reshape(2, GROUP, P, D).transpose(2, 0, 1, 3).reshape(P, 2, GROUP * D)
                for n in ("gate", "up"))
    down = i["L1_ffn_down_w"].reshape(KT, P, FFN).transpose(1, 0, 2)
    return {
        "w_ffn": np.concatenate([gate, up, down], axis=1),
        "uqT": i["L1_xattn_W_uq"].reshape(QC, HEADS, HD).transpose(2, 1, 0),
        "ukT": i["L1_xattn_W_uk"].reshape(KVC, HEADS, HD).transpose(2, 1, 0),
        "uvT": i["L1_xattn_W_uv"].reshape(KVC, HEADS, HD).transpose(2, 1, 0),
        "w_o2": i["L1_xattn_W_o"].reshape(HEADS, HD, D).transpose(1, 0, 2),
        "wkvc": np.concatenate([kvc, kvc], axis=2),
        "wkr": np.stack([np.concatenate([kr, kr], axis=1), np.concatenate([swap(kr), swap(kr)], axis=1)], axis=1),
        "qr": qr,
        "qrb": np.concatenate([swap(qr[:, 1::2]), swap(qr[:, 0::2])], axis=2),
        "wdq": i["L1_xattn_W_dq"].reshape(KT, P, QC).transpose(1, 0, 2),
        "seg": i["itok_BxS_0_1023"].T,
        "tab": tab,
        "ln2": i["L0_ffn_ln2_w"].reshape(KT, P).T,
        "gate": i["L0_ffn_gate_w"].T.reshape(KT, P, EXPERTS).transpose(1, 0, 2),
        "w_moe": w_moe,
        "x": i["x"],
        "ctx": i["ctx_2048"],
        "ctxT": i["ctx_2048"].reshape(-1, D).T,
        "mask": i["mask_BxS2_bk0"],
        "ln1": i["L0_ffn_ln1_w"].reshape(KT, P).T,
        "w_attn": np.stack([by_pair(i["L0_ffn_wq"]), by_pair(i["L0_ffn_wk"]), by_pair(i["L0_ffn_wv"]), wo], axis=2),
    }


def kernel(**inputs):
    import numpy as _np
    import concourse.bacc as _bacc
    from concourse import mybir as _mybir
    from concourse.bass_utils import run_bass_kernel_spmd as _run

    nc = _bacc.Bacc("TRN2", target_bir_lowering=False, num_devices=1)
    arrays = {"in_" + k: _np.ascontiguousarray(v) for k, v in layouts({k: _np.asarray(v) for k, v in inputs.items()}).items()}
    ins = {k[3:]: nc.dram_tensor(k, v.shape, _mybir.dt.from_np(v.dtype), kind="ExternalInput").ap()
           for k, v in arrays.items()}
    out = nc.dram_tensor("out_x", (BATCHES, P, D), F32, kind="ExternalOutput").ap()
    build_program(nc, ins, out)
    r = _run(nc, [arrays], core_ids=[0])
    return r.results[0]["out_x"]
```
